# Optimizing a Trainium2 kernel written in Bass

```python
import numpy as np
import jax
import jax.numpy as jnp

def _softmax(x, axis=-1):
    return jax.nn.softmax(x, axis=axis)

def _gelu(x):
    return jax.nn.gelu(x, approximate=True)

def _silu(x):
    return jax.nn.silu(x)

def _sigmoid(x):
    return jax.nn.sigmoid(x)

def _layernorm(x, axis=-1, eps=1e-05):
    m = jnp.mean(x, axis=axis, keepdims=True)
    v = jnp.var(x, axis=axis, keepdims=True)
    return (x - m) / jnp.sqrt(v + eps)

def _scatter_add(tgt, idx, src, axis=0):
    return tgt.at[idx].add(src)

def _segment_sum(src, seg, n):
    return jax.ops.segment_sum(src, seg, n)
kernel_name = 'mk_hybrid_d1_jaxref_r4_552f83'

def setup_inputs(seed: int=0):
    np.random.seed(seed)
    _w = jnp.asarray

    def _L0_attn_a_setup():
        import jax, jax.numpy as jnp
        import numpy as np
        B, T, D = (1, 256, 256)
        HQ, HKV, HK, HV = (16, 4, 64, 64)
        KW = 4
        N_CHEB = 2
        CHEB_DAMP = 0.25
        EPS = 1e-06

        def _gka_core(x, Wq, Wk, Wv, Wconv, Wa, Walpha, Wb, A_log, dt_bias, norm_w, Wo):
            Bx, Tx, _ = x.shape
            qkv = jnp.concatenate([x @ Wq, x @ Wk, x @ Wv], axis=-1)
            pad = jnp.pad(qkv, ((0, 0), (KW - 1, 0), (0, 0)))
            conv = sum((pad[:, i:i + Tx, :] * Wconv[:, i] for i in range(KW)))
            qkv = jax.nn.silu(conv)
            q, k, v = jnp.split(qkv, [HQ * HK, HQ * HK + HKV * HK], axis=-1)
            q = q.reshape(Bx, Tx, HQ, HK)
            k = k.reshape(Bx, Tx, HKV, HK)
            v = v.reshape(Bx, Tx, HKV, HV)
            g = -jnp.exp(A_log) * jax.nn.softplus(x @ Wa + dt_bias)
            alpha = jax.nn.sigmoid(x @ Walpha)
            beta = jax.nn.sigmoid(x @ Wb)
            v = v * beta[..., None]
            k = k / (jnp.linalg.norm(k, axis=-1, keepdims=True) + EPS)
            q = q * HK ** (-0.5)
            rep = HQ // HKV
            k = jnp.repeat(k, rep, axis=2)
            v = jnp.repeat(v, rep, axis=2)

            def step(carry, inp):
                Hkk, Hkv = carry
                qt, kt, vt, gt = inp
                d = jnp.exp(gt)[..., None, None]
                Hkk = d * Hkk + kt[..., :, None] * kt[..., None, :]
                Hkv = d * Hkv + kt[..., :, None] * vt[..., None, :]
                xq = qt
                for _ in range(N_CHEB):
                    xq = qt - CHEB_DAMP * jnp.einsum('bhk,bhkl->bhl', xq, Hkk)
                ot = jnp.einsum('bhk,bhkv->bhv', xq, Hkv)
                return ((Hkk, Hkv), ot)
            tm = lambda a: jnp.moveaxis(a, 1, 0)
            init = (jnp.zeros((Bx, HQ, HK, HK), jnp.float32), jnp.zeros((Bx, HQ, HK, HV), jnp.float32))
            _, o = jax.lax.scan(step, init, (tm(q), tm(k), tm(v), tm(g)))
            o = jnp.moveaxis(o, 0, 1)
            o = o * alpha[..., None]
            o = o * jax.lax.rsqrt(jnp.mean(o * o, axis=-1, keepdims=True) + EPS) * norm_w
            return o.reshape(Bx, Tx, HQ * HV) @ Wo
        key = jax.random.key(seed)
        ks = jax.random.split(key, 12)
        C = HQ * HK + HKV * HK + HKV * HV
        s = lambda d: 1.0 / np.sqrt(d)
        inp = {'x': jax.random.normal(ks[0], (B, T, D), jnp.float32), 'Wq': jax.random.normal(ks[1], (D, HQ * HK), jnp.float32) * s(D), 'Wk': jax.random.normal(ks[2], (D, HKV * HK), jnp.float32) * s(D), 'Wv': jax.random.normal(ks[3], (D, HKV * HV), jnp.float32) * s(D), 'Wconv': jax.random.normal(ks[4], (C, KW), jnp.float32) * 0.2, 'Wa': jax.random.normal(ks[5], (D, HQ), jnp.float32) * s(D), 'Walpha': jax.random.normal(ks[6], (D, HQ), jnp.float32) * s(D), 'Wb': jax.random.normal(ks[7], (D, HKV), jnp.float32) * s(D), 'A_log': jnp.log(jax.random.uniform(ks[8], (HQ,), jnp.float32, 1.0, 16.0)), 'dt_bias': jax.random.normal(ks[9], (HQ,), jnp.float32) * 0.5, 'norm_w': jnp.ones((HV,), jnp.float32), 'Wo': jax.random.normal(ks[10], (HQ * HV, D), jnp.float32) * s(HQ * HV)}
        return inp
    _L0_attn_a_in = _L0_attn_a_setup()

    def _L0_attn_b_setup():
        import jax, jax.numpy as jnp
        import numpy as np
        from jax import lax
        DIM = 256
        INNER = 512
        STATE = 64
        B, T = (4, 512)
        DECAY = 0.95
        INPUT_FACTOR = 0.05
        LN_EPS = 1e-05

        def _layernorm(x, g, b):
            mu = jnp.mean(x, axis=-1, keepdims=True)
            var = jnp.mean(jnp.square(x - mu), axis=-1, keepdims=True)
            return (x - mu) * lax.rsqrt(var + LN_EPS) * g + b
        key = jax.random.key(seed)
        ks = jax.random.split(key, 8)
        s = 0.02
        return {'x': jax.random.normal(ks[0], (B, T, DIM), jnp.float32), 'W_in': jax.random.normal(ks[1], (2 * INNER, DIM), jnp.float32) * s, 'conv_w': jax.random.normal(ks[2], (INNER, 1, 4), jnp.float32) * s, 'conv_b': jax.random.normal(ks[3], (INNER,), jnp.float32) * s, 'W_B': jax.random.normal(ks[4], (STATE, INNER), jnp.float32) * s, 'W_C': jax.random.normal(ks[5], (INNER, STATE), jnp.float32) * s, 'D_param': jax.random.normal(ks[6], (INNER,), jnp.float32) * s, 'W_out': jax.random.normal(ks[7], (DIM, INNER), jnp.float32) * s, 'ln_gamma': jnp.ones((DIM,), jnp.float32), 'ln_beta': jnp.zeros((DIM,), jnp.float32)}
    _L0_attn_b_in = _L0_attn_b_setup()

    def _L0_ffn_setup():
        import jax, jax.numpy as jnp
        import numpy as np
        DIM = 256

        def _reference_tuple_inner(x, W_r, W_k, W_v, mu_r, mu_k):
            B, T, C = x.shape
            x_prev = jnp.concatenate([jnp.zeros((B, 1, C), x.dtype), x[:, :-1, :]], axis=1)
            xr = mu_r * x + (1.0 - mu_r) * x_prev
            xk = mu_k * x + (1.0 - mu_k) * x_prev
            r = jax.nn.sigmoid(jnp.einsum('btc,dc->btd', xr, W_r))
            k = jnp.einsum('btc,dc->btd', xk, W_k)
            k_act = jnp.square(jax.nn.relu(k))
            out = r * jnp.einsum('btc,dc->btd', k_act, W_v)
            new_state = x[:, -1, :]
            return (out, new_state)
        key = jax.random.key(seed)
        ks = jax.random.split(key, 6)
        B, T, C = (8, 512, DIM)
        x = jax.random.normal(ks[0], (B, T, C), dtype=jnp.float32)
        s = 1.0 / np.sqrt(C)
        W_r = jax.random.uniform(ks[1], (C, C), jnp.float32, -s, s)
        W_k = jax.random.uniform(ks[2], (C, C), jnp.float32, -s, s)
        W_v = jax.random.uniform(ks[3], (C, C), jnp.float32, -s, s)
        mu_r = jax.random.uniform(ks[4], (C,), jnp.float32)
        mu_k = jax.random.uniform(ks[5], (C,), jnp.float32)
        return {'x': x, 'W_r': W_r, 'W_k': W_k, 'W_v': W_v, 'mu_r': mu_r, 'mu_k': mu_k}
    _L0_ffn_in = _L0_ffn_setup()
    _d = {'L0_attn_a_x': _L0_attn_a_in['x'], 'L0_attn_a_Wq': _L0_attn_a_in['Wq'], 'L0_attn_a_Wk': _L0_attn_a_in['Wk'], 'L0_attn_a_Wv': _L0_attn_a_in['Wv'], 'L0_attn_a_Wconv': _L0_attn_a_in['Wconv'], 'L0_attn_a_Wa': _L0_attn_a_in['Wa'], 'L0_attn_a_Walpha': _L0_attn_a_in['Walpha'], 'L0_attn_a_Wb': _L0_attn_a_in['Wb'], 'L0_attn_a_A_log': _L0_attn_a_in['A_log'], 'L0_attn_a_dt_bias': _L0_attn_a_in['dt_bias'], 'L0_attn_a_norm_w': _L0_attn_a_in['norm_w'], 'L0_attn_a_Wo': _L0_attn_a_in['Wo'], 'L0_attn_b_W_in': _L0_attn_b_in['W_in'], 'L0_attn_b_conv_w': _L0_attn_b_in['conv_w'], 'L0_attn_b_conv_b': _L0_attn_b_in['conv_b'], 'L0_attn_b_W_B': _L0_attn_b_in['W_B'], 'L0_attn_b_W_C': _L0_attn_b_in['W_C'], 'L0_attn_b_D_param': _L0_attn_b_in['D_param'], 'L0_attn_b_W_out': _L0_attn_b_in['W_out'], 'L0_attn_b_ln_gamma': _L0_attn_b_in['ln_gamma'], 'L0_attn_b_ln_beta': _L0_attn_b_in['ln_beta'], 'L0_ffn_W_r': _L0_ffn_in['W_r'], 'L0_ffn_W_k': _L0_ffn_in['W_k'], 'L0_ffn_W_v': _L0_ffn_in['W_v'], 'L0_ffn_mu_r': _L0_ffn_in['mu_r'], 'L0_ffn_mu_k': _L0_ffn_in['mu_k']}
    _x0 = _d['L0_attn_a_x']
    _d['L0_attn_a_x'] = jax.random.normal(jax.random.fold_in(jax.random.key(seed), 1), (16, 1024, 256), dtype=_x0.dtype)
    del _x0
    return _d

def reference(L0_attn_a_x, L0_attn_a_Wq, L0_attn_a_Wk, L0_attn_a_Wv, L0_attn_a_Wconv, L0_attn_a_Wa, L0_attn_a_Walpha, L0_attn_a_Wb, L0_attn_a_A_log, L0_attn_a_dt_bias, L0_attn_a_norm_w, L0_attn_a_Wo, L0_attn_b_W_in, L0_attn_b_conv_w, L0_attn_b_conv_b, L0_attn_b_W_B, L0_attn_b_W_C, L0_attn_b_D_param, L0_attn_b_W_out, L0_attn_b_ln_gamma, L0_attn_b_ln_beta, L0_ffn_W_r, L0_ffn_W_k, L0_ffn_W_v, L0_ffn_mu_r, L0_ffn_mu_k):

    def _L0_attn_a_ref(x, Wq, Wk, Wv, Wconv, Wa, Walpha, Wb, A_log, dt_bias, norm_w, Wo):
        import jax, jax.numpy as jnp
        import numpy as np
        B, T, D = (1, 256, 256)
        HQ, HKV, HK, HV = (16, 4, 64, 64)
        KW = 4
        N_CHEB = 2
        CHEB_DAMP = 0.25
        EPS = 1e-06

        def _gka_core(x, Wq, Wk, Wv, Wconv, Wa, Walpha, Wb, A_log, dt_bias, norm_w, Wo):
            Bx, Tx, _ = x.shape
            qkv = jnp.concatenate([x @ Wq, x @ Wk, x @ Wv], axis=-1)
            pad = jnp.pad(qkv, ((0, 0), (KW - 1, 0), (0, 0)))
            conv = sum((pad[:, i:i + Tx, :] * Wconv[:, i] for i in range(KW)))
            qkv = jax.nn.silu(conv)
            q, k, v = jnp.split(qkv, [HQ * HK, HQ * HK + HKV * HK], axis=-1)
            q = q.reshape(Bx, Tx, HQ, HK)
            k = k.reshape(Bx, Tx, HKV, HK)
            v = v.reshape(Bx, Tx, HKV, HV)
            g = -jnp.exp(A_log) * jax.nn.softplus(x @ Wa + dt_bias)
            alpha = jax.nn.sigmoid(x @ Walpha)
            beta = jax.nn.sigmoid(x @ Wb)
            v = v * beta[..., None]
            k = k / (jnp.linalg.norm(k, axis=-1, keepdims=True) + EPS)
            q = q * HK ** (-0.5)
            rep = HQ // HKV
            k = jnp.repeat(k, rep, axis=2)
            v = jnp.repeat(v, rep, axis=2)

            def step(carry, inp):
                Hkk, Hkv = carry
                qt, kt, vt, gt = inp
                d = jnp.exp(gt)[..., None, None]
                Hkk = d * Hkk + kt[..., :, None] * kt[..., None, :]
                Hkv = d * Hkv + kt[..., :, None] * vt[..., None, :]
                xq = qt
                for _ in range(N_CHEB):
                    xq = qt - CHEB_DAMP * jnp.einsum('bhk,bhkl->bhl', xq, Hkk)
                ot = jnp.einsum('bhk,bhkv->bhv', xq, Hkv)
                return ((Hkk, Hkv), ot)
            tm = lambda a: jnp.moveaxis(a, 1, 0)
            init = (jnp.zeros((Bx, HQ, HK, HK), jnp.float32), jnp.zeros((Bx, HQ, HK, HV), jnp.float32))
            _, o = jax.lax.scan(step, init, (tm(q), tm(k), tm(v), tm(g)))
            o = jnp.moveaxis(o, 0, 1)
            o = o * alpha[..., None]
            o = o * jax.lax.rsqrt(jnp.mean(o * o, axis=-1, keepdims=True) + EPS) * norm_w
            return o.reshape(Bx, Tx, HQ * HV) @ Wo
        return _gka_core(x, Wq, Wk, Wv, Wconv, Wa, Walpha, Wb, A_log, dt_bias, norm_w, Wo)

    def _L0_attn_b_ref(x, W_in, conv_w, conv_b, W_B, W_C, D_param, W_out, ln_gamma, ln_beta):
        import jax, jax.numpy as jnp
        import numpy as np
        from jax import lax
        DIM = 256
        INNER = 512
        STATE = 64
        B, T = (4, 512)
        DECAY = 0.95
        INPUT_FACTOR = 0.05
        LN_EPS = 1e-05

        def _layernorm(x, g, b):
            mu = jnp.mean(x, axis=-1, keepdims=True)
            var = jnp.mean(jnp.square(x - mu), axis=-1, keepdims=True)
            return (x - mu) * lax.rsqrt(var + LN_EPS) * g + b
        Bn, Tn, Dn = x.shape
        x_proj = jnp.einsum('btd,ed->bte', x, W_in)
        x_input, x_gate = jnp.split(x_proj, 2, axis=-1)
        xc = lax.conv_general_dilated(x_input.transpose(0, 2, 1), conv_w, window_strides=(1,), padding=[(3, 0)], feature_group_count=INNER) + conv_b[None, :, None]
        u = jax.nn.silu(xc).transpose(0, 2, 1)
        Bu = jnp.einsum('btc,sc->bts', u, W_B)

        def step(h, bu_t):
            h = DECAY * h + INPUT_FACTOR * bu_t
            return (h, h)
        h0 = jnp.zeros((Bn, STATE), x.dtype)
        _, hs = lax.scan(step, h0, Bu.transpose(1, 0, 2))
        hs = hs.transpose(1, 0, 2)
        y = jnp.einsum('bts,cs->btc', hs, W_C) + D_param * u
        y = y * jax.nn.silu(x_gate)
        y = jnp.einsum('btc,dc->btd', y, W_out)
        return _layernorm(y + x, ln_gamma, ln_beta)

    def _L0_ffn_ref(x, W_r, W_k, W_v, mu_r, mu_k):
        import jax, jax.numpy as jnp
        import numpy as np
        DIM = 256

        def _reference_tuple_inner(x, W_r, W_k, W_v, mu_r, mu_k):
            B, T, C = x.shape
            x_prev = jnp.concatenate([jnp.zeros((B, 1, C), x.dtype), x[:, :-1, :]], axis=1)
            xr = mu_r * x + (1.0 - mu_r) * x_prev
            xk = mu_k * x + (1.0 - mu_k) * x_prev
            r = jax.nn.sigmoid(jnp.einsum('btc,dc->btd', xr, W_r))
            k = jnp.einsum('btc,dc->btd', xk, W_k)
            k_act = jnp.square(jax.nn.relu(k))
            out = r * jnp.einsum('btc,dc->btd', k_act, W_v)
            new_state = x[:, -1, :]
            return (out, new_state)
        return _reference_tuple_inner(x, W_r, W_k, W_v, mu_r, mu_k)[0]
    x = L0_attn_a_x
    x = x + _L0_attn_a_ref(_layernorm(x, axis=-1), L0_attn_a_Wq, L0_attn_a_Wk, L0_attn_a_Wv, L0_attn_a_Wconv, L0_attn_a_Wa, L0_attn_a_Walpha, L0_attn_a_Wb, L0_attn_a_A_log, L0_attn_a_dt_bias, L0_attn_a_norm_w, L0_attn_a_Wo)
    x = x + _L0_ffn_ref(_layernorm(x, axis=-1), L0_ffn_W_r, L0_ffn_W_k, L0_ffn_W_v, L0_ffn_mu_r, L0_ffn_mu_k)
    x = x + _L0_attn_b_ref(_layernorm(x, axis=-1), L0_attn_b_W_in, L0_attn_b_conv_w, L0_attn_b_conv_b, L0_attn_b_W_B, L0_attn_b_W_C, L0_attn_b_D_param, L0_attn_b_W_out, L0_attn_b_ln_gamma, L0_attn_b_ln_beta)
    x = x + _L0_ffn_ref(_layernorm(x, axis=-1), L0_ffn_W_r, L0_ffn_W_k, L0_ffn_W_v, L0_ffn_mu_r, L0_ffn_mu_k)
    return x

_drawn_inputs = setup_inputs


def setup_inputs(seed=0):
    import zlib

    import numpy as np

    out = dict(_drawn_inputs(seed))
    spreads = {'L0_attn_a_norm_w': (1.0, 0.2),
     'L0_attn_b_ln_gamma': (1.0, 0.2),
     'L0_attn_b_ln_beta': (0.0, 0.1)}
    factors = {'L0_attn_b_W_in': 8.0,
     'L0_attn_b_conv_w': 8.0,
     'L0_attn_b_conv_b': 8.0,
     'L0_attn_b_W_B': 8.0,
     'L0_attn_b_W_C': 8.0,
     'L0_attn_b_D_param': 8.0,
     'L0_attn_b_W_out': 8.0,
     'L0_ffn_mu_r': 4.946}
    for name, (base, spread) in spreads.items():
        noise = np.random.default_rng([zlib.crc32(name.encode()), seed]).standard_normal(out[name].shape)
        drawn = base * np.exp(spread * noise) if base else spread * noise
        out[name] = jnp.asarray(drawn.astype(out[name].dtype))
    for name, factor in factors.items():
        out[name] = (out[name] * factor).astype(out[name].dtype)
    return out
```

```python
from contextlib import ExitStack

import concourse.bass as bass
from concourse import mybir

F32 = mybir.dt.float32
BF16 = mybir.dt.bfloat16
ALU = mybir.AluOpType
ACT = mybir.ActivationFunctionType
AX_X = mybir.AxisListType.X

P = 128
BATCH, T, D = 16, 1024, 256
HQ, HKV, DH = 16, 4, 64
BT = 256
CT = 64
NJ = BT // P
NC = BT // CT
NBLK = BATCH * T // BT
BPS = T // BT
DK = D // P
NPAIR = HKV // 2
REP = HQ // HKV
NT = NPAIR * REP
QKV = 2 * NPAIR + NT
NU = QKV // 2
KW = 4
INNER, STATE = 512, 64
NE = INNER // P
DAMP = 0.25
DECAY, INPUT_FACTOR = 0.95, 0.05
EPS_LN, EPS = 1e-5, 1e-6


class Stage:

    def __init__(self, sem, per, step=1):
        self.sem, self.per, self.step = sem, per, step

    def at(self, n, k):
        value = (n * self.per + k) * self.step
        return self.sem, max(value, 0) if isinstance(value, int) else value


BANK_USES = [
    ["xt1", "bz", ("qkv", 1), ("qkv", 3), ("qkv", 5), ("kt", 1), ("vt", 1), ("gbc", 0), ("gbc", 2)],
    ["gate", ("qkv", 0), ("qkv", 2), ("qkv", 4), ("kt", 0), ("vt", 0), "gcol", ("gbc", 1), ("gbc", 3)],
    [("bc", 0), ("bc", 2), "wo", ("r", 2), ("v", 2), ("in", 0), ("in", 2), "bu", ("y", 1), ("xt", 4), ("k", 4)],
    ["ms", ("bc", 1), ("bc", 3), ("xt", 2), ("k", 2), ("xt", 3), ("in", 1), ("in", 3), ("y", 0), "out", ("r", 4), ("v", 4)],
    [x for t in range(NC) for x in (("S1", t), ("Hs0", t))],
    [x for t in range(NC) for x in (("Hs1", t), ("A2", t))],
    [x for t in range(NC) for x in (("A1", t), ("S2", t))],
    [x for t in range(NC) for x in (("S3", t), ("O", t))],
]
USE = {use: (b, i) for b, uses in enumerate(BANK_USES) for i, use in enumerate(uses)}


def hybrid_block_kernel(nc: bass.Bass, a: dict, out: bass.AP):
    ctx = ExitStack()
    with ctx:
        def sb(name, shape, dt=F32):
            return ctx.enter_context(nc.sbuf_tensor(name, shape, dt))

        def stage(name, per, step=1):
            return Stage(ctx.enter_context(nc.semaphore(name)), per, step)

        bank = [ctx.enter_context(nc.psum_tensor(f"bank{b}", [P, 512], F32)) for b in range(8)]

        w_qkv = sb("w_qkv", [P, DK, QKV * P])
        w_gate = sb("w_gate", [P, DK, 48])
        w_beta = sb("w_beta", [P, DK, HKV])
        w_o = sb("w_o", [P, NT, D])
        w_conv = sb("w_conv", [P, QKV, KW])
        f_r = sb("f_r", [P, DK, D])
        f_k = sb("f_k", [P, DK, D])
        f_v = sb("f_v", [P, DK, D])
        mu = sb("mu", [P, 2, DK])
        w_in = sb("w_in", [P, DK, 2 * INNER])
        w_b = sb("w_b", [P, NE, STATE])
        w_c = sb("w_c", [STATE, INNER])
        w_out = sb("w_out", [P, NE, D])
        conv3_w = sb("conv3_w", [P, NE, KW])
        conv3_b = sb("conv3_b", [P, NE])
        d_skip = sb("d_skip", [P, NE])
        gam = sb("gam", [P, D])
        bet3 = sb("bet3", [P, D])
        norm_w = sb("norm_w", [P, 1])
        dt_bias = sb("dt_bias", [HQ, 1])
        neg_a = sb("neg_a", [HQ, 1])
        ident = sb("ident", [P, P])
        causal = sb("causal", [P, CT])
        chunk_start = sb("chunk_start", [HQ, BT])
        head_rows = sb("head_rows", [96, NT, P], BF16)
        head_cols = sb("head_cols", [96, HQ], BF16)
        head_mean = sb("head_mean", [P, NT, HQ])
        decay = sb("decay", [STATE, 1])
        no_halo = sb("no_halo", [P, QKV, KW - 1])
        half_neg = sb("half_neg", [P, 8])
        half_pos = sb("half_pos", [P, 8])
        xin = sb("xin", [P, 2, NJ, D])
        xres = sb("xres", [P, 2, NJ, D])
        xn1 = sb("xn1", [P, NJ, D])
        xn = sb("xn", [P, NJ, D])
        ln_stats = sb("ln_stats", [P, 5, NJ, 6])
        ln_mv = sb("ln_mv", [P, 5, NJ, 2])
        ln_ve = sb("ln_ve", [P, 5, NJ])
        ln_rs = sb("ln_rs", [P, 5, NJ])
        xT1 = sb("xT1", [P, DK, BT])
        raw = sb("raw", [P, QKV, KW - 1 + BT])
        y = sb("y", [P, 2, 2, BT])
        kT = sb("kT", [P, NPAIR, NC, P])
        vT = sb("vT", [P, NPAIR, NC, P])
        qT = sb("qT", [P, NT, BT])
        kD = sb("kD", [P, NPAIR, NC, P])
        vD = sb("vD", [P, NPAIR, NC, P])
        kv = sb("kv", [P, NPAIR, NC, 2, DH])
        k_ss = sb("k_ss", [P, NPAIR * NC])
        k_nr = sb("k_nr", [P, NPAIR * NC])
        k_nrm = sb("k_nrm", [P, NPAIR * NC])
        k_rn = sb("k_rn", [P, NPAIR * NC])
        k_ln = sb("k_ln", [P, NPAIR * NC])
        beta = sb("beta", [P, NPAIR * NC])
        beta_e = sb("beta_e", [P, NPAIR * NC])
        beta_z = sb("beta_z", [P, NPAIR * NC])
        az = sb("az", [HQ, BT])
        az_abs = sb("az_abs", [HQ, BT])
        al = sb("al", [HQ, 2, BT])
        gsum = sb("gsum", [HQ, BT])
        part = sb("part", [96, BT])
        g3 = sb("g3", [96, BT], BF16)
        sc3 = sb("sc3", [96, BT], BF16)
        gcol = sb("gcol", [P, NT, NC])
        wlast = sb("wlast", [P, NT, NC])
        expG = sb("expG", [P, NT, BT])
        M = sb("M", [P, NT, BT])
        sq = expG
        Pb = sb("Pb", [P, 3, NT, CT])
        x1 = sb("x1", [P, NT, CT])
        x2 = sb("x2", [P, NT, CT])
        qE = sb("qE", [P, NT, CT])
        x1E = sb("x1E", [P, NT, CT])
        x2E = sb("x2E", [P, NT, CT])
        R = sb("R", [P, NPAIR, REP, 2 * DH])
        Hst = sb("Hst", [P, NT, 2 * DH])
        Hd = sb("Hd", [P, 2, NT, 2, P])
        oT = sb("oT", [P, NT, BT])
        xfT = sb("xfT", [P, DK, 1 + BT])
        last_col = sb("last_col", [P, 2, DK])
        diff = sb("diff", [P, DK, BT])
        mixed = sb("mixed", [P, 2, DK, BT])
        r_t = sb("r_t", [P, NJ * D])
        kr = sb("kr", [P, DK, BT])
        f_out = diff[:].rearrange("p k t -> p (k t)").rearrange("p (j d) -> p j d", j=NJ)
        raw3 = sb("raw3", [P, NE, KW - 1 + BT])
        uT = sb("uT", [P, NE, BT])
        sg = sb("sg", [P, NE, BT])
        bu = sb("bu", [STATE, BT])
        h3 = bu
        h_last = sb("h_last", [STATE, 1])
        yT = sb("yT", [P, NE, BT])
        y3 = mixed
        z3 = f_out

        full = [stage(f"bank{b}_full", len(u)) for b, u in enumerate(BANK_USES)]
        drained_ = [stage(f"bank{b}_drained", len(u)) for b, u in enumerate(BANK_USES)]
        w_loaded = stage("w_loaded", 0)
        w_ready = stage("w_ready", 0)
        s_exp_a = stage("exp_a_ready", 0)
        x_loaded = [stage(f"x_loaded{i}", 8) for i in range(2)]
        x_stored = [stage(f"x_stored{i}", 8) for i in range(2)]
        LNS = {1: 0, 2: 1, 3: 2, 4: 3, 5: 4}
        ln_dve = {i: stage(f"ln{i}_steps", 3 * NJ + 1) for i in LNS}
        ln_root = {i: stage(f"ln{i}_rstd", 1) for i in LNS}
        halo = stage("halo_ready", 1)
        conv = stage("conv_taps", 6 * NU)
        silu = stage("silu_done", NU)
        gate_act = stage("gate_exps", 5)
        beta_done = stage("beta_done", 2)
        alpha_done = stage("alpha_done", 2)
        g_steps = stage("g_steps", 8)
        k_sq = stage("k_squares", 2)
        k_red = stage("k_norm_steps", 4)
        k_root = stage("k_norm_root", 1)
        k_log = stage("k_norm_log", 1)
        k_normed = stage("k_normed", 2)
        kv_done = stage("kv_stacked", 2)
        gcol_done = stage("gcol_done", 1)
        exp_g = stage("exp_g_done", 4)
        masked = stage("decay_masked", 4)
        exp_m = stage("exp_m_done", 4)
        w_last = stage("w_last_done", 1)
        q_scaled = stage("q_scaled", NC)
        x1_scaled = stage("x1_scaled", NC)
        x2_scaled = stage("x2_scaled", NC)
        r_scaled = stage("kv_weighted", NC)
        h_decayed = stage("h_decayed", NC)
        h_placed = stage("h_placed", NC)
        o_sq = stage("o_squares", 4)
        o_var = stage("o_scale_steps", 6)
        o_root = stage("o_scale_root", 1)
        f_shift = {i: stage(f"ffn{i}_shift", 3) for i in (2, 4)}
        f_mix = {i: stage(f"ffn{i}_mixed", 4) for i in (2, 4)}
        f_sq = {i: stage(f"ffn{i}_squared", 1) for i in (2, 4)}
        f_res = {i: stage(f"ffn{i}_residual", 1) for i in (2, 4)}
        halo3 = stage("halo3_ready", 1)
        conv3 = stage("conv3_taps", 12)
        silu3 = stage("silu3_done", 2)
        scan3 = stage("scan3_steps", 2)
        gated3 = stage("gated3_done", 2)
        l3_res = stage("l3_residual", 3)

        def fill(use, n):
            b, i = USE[use]
            return drained_[b].at(n, i)

        def filled(use, n):
            b, i = USE[use]
            return full[b].at(n, i + 1)

        def drained(use, n):
            b, i = USE[use]
            return drained_[b].at(n, i + 1)

        def full_sem(use):
            return full[USE[use][0]].sem

        def free_sem(use):
            return drained_[USE[use][0]].sem

        def psum(use):
            return bank[USE[use][0]]

        x_dram = a["x"].rearrange("b (q j p) d -> (b q) p j d", q=BPS, p=P)
        out_dram = out.rearrange("b (q j p) d -> (b q) p j d", q=BPS, p=P)
        halves = [(0, slice(0, DH)), (1, slice(DH, P))]

        loads = [
            (w_qkv[:], "w_qkv"), (w_gate[:], "w_gate"), (w_beta[:], "w_beta"), (w_o[:], "w_o"), (w_conv[:], "w_conv"),
            (f_r[:], "f_r"), (f_k[:], "f_k"), (f_v[:], "f_v"), (mu[:], "mu"), (w_in[:], "w_in"), (w_b[:], "w_b"), (w_c[:], "w_c"),
            (w_out[:], "w_out"), (conv3_w[:], "conv3_w"), (conv3_b[:], "conv3_b"), (d_skip[:], "d_skip"), (gam[:], "gam"),
            (bet3[:], "bet3"), (norm_w[:], "norm_w"), (dt_bias[:], "dt_bias"), (neg_a[:], "a_log"), (ident[:], "ident"),
            (causal[:], "causal"), (chunk_start[:], "chunk_start"), (M[0:96, :, 0:P], "head_rows"), (M[0:96, 0, P:P + HQ], "head_cols"),
            (head_mean[:], "head_mean"),
        ]
        N_READY = 6

        def blocks(engine, step):
            for q in range(BPS):
                step(q, q)
            with engine.Fori(1, BATCH) as b:
                for q in range(BPS):
                    step(b * BPS + q, q)
            step(NBLK, 0)

        def parts(n):
            return (False, True) if isinstance(n, int) and n == NBLK else (True, not (isinstance(n, int) and n == 0))

        block = ctx.enter_context(nc.Block())

        @block.sync
        def _(sp):
            for tile, name in loads:
                sp.dma_start(tile, a[name]).then_inc(w_loaded.sem, 16)

            def load(n, slot):
                sp.wait_ge(*drained("wo", n - 2))
                sp.dma_start(xin[:, slot], x_dram[n]).then_inc(x_loaded[slot].sem, 16)

            def store(m, slot):
                sp.wait_ge(*f_res[4].at(m, 1))
                sp.dma_start(out_dram[m], xres[:, slot]).then_inc(x_stored[slot].sem, 16)

            load(0, 0)
            load(1, 1)
            for n in range(2, BPS):
                load(n, n % 2)
                store(n - 2, n % 2)
            with sp.Fori(1, BATCH) as b:
                for q in range(BPS):
                    load(b * BPS + q, q % 2)
                    store(b * BPS + q - 2, q % 2)
            for m in range(NBLK - 2, NBLK):
                store(m, m % 2)
            for slot in range(2):
                sp.wait_ge(*x_stored[slot].at(NBLK, 0))

        @block.tensor
        def _(pe):
            def transposes(use, n, src, ln):
                pe.wait_ge(*ln_dve[ln].at(n, 3 * NJ + 1))
                pe.wait_ge(*fill(use, n))
                for k in range(DK):
                    for j in range(NJ):
                        mm = pe.transpose(psum(use)[:, k * BT + j * P:k * BT + (j + 1) * P],
                                          src[:, j, k * P:(k + 1) * P], ident[:])
                mm.then_inc(full_sem(use), 1)

            def gates(n):
                pe.wait_ge(*drained("xt1", n))
                pe.wait_ge(*fill("gate", n))
                for k in range(DK):
                    mm = pe.matmul(psum("gate")[0:48, 0:BT], w_gate[:, k, :], xT1[:, k, :], start=k == 0, stop=k == DK - 1)
                mm.then_inc(full_sem("gate"), 1)
                pe.wait_ge(*fill("bz", n))
                for c in range(NC):
                    for h, hs in halves:
                        for k in range(DK):
                            mm = pe.matmul(psum("bz")[hs, c * NPAIR:(c + 1) * NPAIR], xT1[:, k, c * CT:(c + 1) * CT],
                                           w_beta[:, k, h * NPAIR:(h + 1) * NPAIR], start=k == 0, stop=k == DK - 1)
                mm.then_inc(full_sem("bz"), 1)

            def qkv(u, n):
                use = ("qkv", u)
                pe.wait_ge(*fill(use, n))
                for e in range(2):
                    for k in range(DK):
                        c = (2 * u + e) * P
                        mm = pe.matmul(psum(use)[:, e * BT:(e + 1) * BT], w_qkv[:, k, c:c + P], xT1[:, k, :],
                                       start=k == 0, stop=k == DK - 1)
                mm.then_inc(full_sem(use), 1)

            def kv_transposes(name, src, p, done, n):
                use = (name, p)
                pe.wait_ge(*silu.at(n, done))
                pe.wait_ge(*fill(use, n))
                for c in range(NC):
                    mm = pe.transpose(psum(use)[:, c * P:(c + 1) * P], src[:, p, c, :], ident[:])
                mm.then_inc(full_sem(use), 1)

            def decay_columns(n):
                pe.wait_ge(*g_steps.at(n, 8))
                pe.wait_ge(*fill("gcol", n))
                for c in range(NC):
                    for h, hs in halves:
                        mm = pe.matmul(psum("gcol")[hs, c * NT:(c + 1) * NT], g3[:, c * CT:(c + 1) * CT],
                                       head_cols[:, h * NT:(h + 1) * NT], start=True, stop=True)
                mm.then_inc(full_sem("gcol"), 1)

            def spread(name, src, g, n):
                use = (name, g)
                pe.wait_ge(*fill(use, n))
                for e in range(2):
                    mm = pe.matmul(psum(use)[:, e * BT:(e + 1) * BT], head_rows[:, 2 * g + e, :], src[:],
                                   start=True, stop=True)
                mm.then_inc(full_sem(use), 1)

            def score(name, src, t, n):
                use = (name, t)
                pe.wait_ge(*fill(use, n))
                for p in range(NPAIR):
                    mm = pe.matmul(psum(use)[:, p * REP * CT:(p + 1) * REP * CT], kT[:, p, t, :],
                                   src[:, p * REP:(p + 1) * REP, :], start=True, stop=True)
                mm.then_inc(full_sem(use), 1)

            def apply(name, values, Pi, scaled, m, t, n):
                use = (name, t)
                pe.wait_ge(*fill(use, n))
                for p in range(NPAIR):
                    pe.matmul(psum(use)[:, p * REP * CT:(p + 1) * REP * CT], values[:, p, t, :],
                              Pb[:, Pi, p * REP:(p + 1) * REP, :], start=p == 0, stop=False, skip_group_check=True)
                for i in range(NT):
                    mm = pe.matmul(psum(use)[:, i * CT:(i + 1) * CT], Hd[:, t % 2, i, m, :], scaled[:, i, :],
                                   start=False, stop=i == NT - 1, skip_group_check=True)
                mm.then_inc(full_sem(use), 1)

            def state(p, t, n):
                use = (f"Hs{p}", t)
                pe.wait_ge(*fill(use, n))
                pe.matmul(psum(use)[:], kD[:, p, t, :], R[:, p].rearrange("s i e -> s (i e)"),
                          start=True, stop=True).then_inc(full_sem(use), 1)

            def s1(t, n):
                if t == 0:
                    pe.wait_ge(*silu.at(n, NU))
                score("S1", qT[:, :, t * CT:(t + 1) * CT], t, n)

            def a1(t, n):
                pe.wait_ge(*k_normed.at(n, 2))
                pe.wait_ge(*drained(("S1", t), n))
                pe.wait_ge(*q_scaled.at(n, t + 1))
                pe.wait_ge(*h_placed.at(n, t))
                apply("A1", kD, 0, qE, 0, t, n)

            def s2(t, n):
                pe.wait_ge(*drained(("A1", t), n))
                score("S2", x1[:], t, n)

            def a2(t, n):
                pe.wait_ge(*drained(("S2", t), n))
                pe.wait_ge(*x1_scaled.at(n, t + 1))
                apply("A2", kD, 1, x1E, 0, t, n)

            def s3(t, n):
                pe.wait_ge(*drained(("A2", t), n))
                score("S3", x2[:], t, n)

            def o(t, n):
                pe.wait_ge(*drained(("S3", t), n))
                pe.wait_ge(*x2_scaled.at(n, t + 1))
                apply("O", vD, 2, x2E, 1, t, n)

            def new_state(t, n):
                pe.wait_ge(*r_scaled.at(n, t + 1))
                state(0, t, n)
                state(1, t, n)

            def head_means(n):
                pe.wait_ge(*o_sq.at(n, 4))
                pe.wait_ge(*fill("ms", n))
                for i in range(NT):
                    mm = pe.matmul(psum("ms")[0:HQ, 0:BT], head_mean[:, i, :], sq[:, i, :], start=i == 0, stop=i == NT - 1)
                mm.then_inc(full_sem("ms"), 1)

            def attention_out(n):
                pe.wait_ge(*drained(("bc", 3), n))
                pe.wait_ge(*drained(("bc", 2), n))
                pe.wait_ge(*fill("wo", n))
                for j in range(NJ):
                    for i in range(NT):
                        mm = pe.matmul(psum("wo")[:, j * D:(j + 1) * D], oT[:, i, j * P:(j + 1) * P], w_o[:, i, :],
                                       start=i == 0, stop=i == NT - 1)
                mm.then_inc(full_sem("wo"), 1)

            def ffn_receptance(L, m):
                use = ("r", L)
                pe.wait_ge(*f_mix[L].at(m, 2))
                pe.wait_ge(*fill(use, m))
                for j in range(NJ):
                    for k in range(DK):
                        mm = pe.matmul(psum(use)[:, j * D:(j + 1) * D], mixed[:, 0, k, j * P:(j + 1) * P], f_r[:, k, :],
                                       start=k == 0, stop=k == DK - 1)
                mm.then_inc(full_sem(use), 1)

            def ffn_keys(L, m):
                use = ("k", L)
                pe.wait_ge(*f_mix[L].at(m, 4))
                pe.wait_ge(*fill(use, m))
                for e in range(DK):
                    for k in range(DK):
                        mm = pe.matmul(psum(use)[:, e * BT:(e + 1) * BT], f_k[:, k, e * P:(e + 1) * P],
                                       mixed[:, 1, k, :], start=k == 0, stop=k == DK - 1)
                mm.then_inc(full_sem(use), 1)

            def ffn_values(L, m):
                use = ("v", L)
                pe.wait_ge(*f_sq[L].at(m, 1))
                pe.wait_ge(*fill(use, m))
                for j in range(NJ):
                    for e in range(DK):
                        mm = pe.matmul(psum(use)[:, j * D:(j + 1) * D], kr[:, e, j * P:(j + 1) * P], f_v[:, e, :],
                                       start=e == 0, stop=e == DK - 1)
                mm.then_inc(full_sem(use), 1)

            def ssm_in(u, m):
                use = ("in", u)
                pe.wait_ge(*drained(("xt", 3), m))
                pe.wait_ge(*fill(use, m))
                for e in range(2):
                    for k in range(DK):
                        c = (2 * u + e) * P
                        mm = pe.matmul(psum(use)[:, e * BT:(e + 1) * BT], w_in[:, k, c:c + P], xfT[:, k, 1:1 + BT],
                                       start=k == 0, stop=k == DK - 1)
                mm.then_inc(full_sem(use), 1)

            def ssm_b(m):
                pe.wait_ge(*silu3.at(m, 2))
                pe.wait_ge(*fill("bu", m))
                for e in range(NE):
                    mm = pe.matmul(psum("bu")[0:STATE, 0:BT], w_b[:, e, :], uT[:, e, :], start=e == 0, stop=e == NE - 1)
                mm.then_inc(full_sem("bu"), 1)

            def ssm_c(v, m):
                use = ("y", v)
                pe.wait_ge(*scan3.at(m, 1))
                pe.wait_ge(*fill(use, m))
                for e in range(2):
                    c = (2 * v + e) * P
                    mm = pe.matmul(psum(use)[:, e * BT:(e + 1) * BT], w_c[:, c:c + P], h3[:], start=True, stop=True)
                mm.then_inc(full_sem(use), 1)

            def ssm_out(m):
                pe.wait_ge(*gated3.at(m, 2))
                pe.wait_ge(*fill("out", m))
                for j in range(NJ):
                    for e in range(NE):
                        mm = pe.matmul(psum("out")[:, j * D:(j + 1) * D], yT[:, e, j * P:(j + 1) * P], w_out[:, e, :],
                                       start=e == 0, stop=e == NE - 1)
                mm.then_inc(full_sem("out"), 1)

            def step(n, q):
                attention, later = parts(n)
                m = n - 1
                if later:
                    head_means(m)
                if attention:
                    transposes("xt1", n, xn1, 1)
                    gates(n)
                    for u in range(4):
                        qkv(u, n)
                if later:
                    pe.wait_ge(*o_var.at(m, 6))
                    for g in range(4):
                        spread("bc", sc3, g, m)
                if attention:
                    qkv(4, n)
                    qkv(5, n)
                    kv_transposes("kt", kT, 0, 1, n)
                    kv_transposes("kt", kT, 1, 1, n)
                if later:
                    attention_out(m)
                if attention:
                    kv_transposes("vt", vT, 0, 2, n)
                    kv_transposes("vt", vT, 1, 2, n)
                    decay_columns(n)
                    for g in range(4):
                        spread("gbc", g3, g, n)
                if later:
                    transposes(("xt", 2), m, xn, 2)
                    ffn_receptance(2, m)
                    ffn_keys(2, m)
                    if not attention:
                        ffn_values(2, m)
                        transposes(("xt", 3), m, xn, 3)
                        for u in range(4):
                            ssm_in(u, m)
                        ssm_b(m)
                        ssm_c(0, m)
                        ssm_c(1, m)
                        ssm_out(m)
                        transposes(("xt", 4), m, xn, 4)
                        ffn_receptance(4, m)
                        ffn_keys(4, m)
                        ffn_values(4, m)
                if not attention:
                    return
                for t in range(NC + 1):
                    if t < NC:
                        s1(t, n)
                    if later and t == 0:
                        ffn_values(2, m)
                    if later and t == 1:
                        ssm_in(2, m)
                    if t >= 1:
                        a2(t - 1, n)
                    if later and t == 2:
                        ssm_b(m)
                    if later and t == 3:
                        ssm_out(m)
                    if later and t == 4:
                        transposes(("xt", 4), m, xn, 4)
                    if t < NC:
                        a1(t, n)
                    if later and t == 0:
                        transposes(("xt", 3), m, xn, 3)
                    if later and t == 1:
                        ssm_in(3, m)
                    if t >= 1:
                        s3(t - 1, n)
                    if later and t == 2:
                        ssm_c(0, m)
                        ssm_c(1, m)
                    if later and t == 4:
                        ffn_receptance(4, m)
                        ffn_keys(4, m)
                    if t < NC:
                        new_state(t, n)
                    if t >= 1:
                        o(t - 1, n)
                    if later and t == 0:
                        ssm_in(0, m)
                    if t < NC:
                        s2(t, n)
                    if later and t == 0:
                        ssm_in(1, m)
                if later:
                    ffn_values(4, m)

            pe.wait_ge(*w_ready.at(0, N_READY))
            pe.wait_ge(*(w_loaded.sem, 16 * len(loads)))
            blocks(pe, step)

        @block.scalar
        def _(act):
            act.wait_ge(w_loaded.sem, 16 * len(loads))
            act.activation(neg_a[:], neg_a[:], ACT.Exp).then_inc(s_exp_a.sem, 1)

            def copy_out(use, n, dst, func=ACT.Copy, scale=1.0):
                act.wait_ge(*filled(use, n))
                act.activation(dst, psum(use)[:, 0:512], func, scale=scale).then_inc(free_sem(use), 1)

            def gate_exps(n, q):
                act.wait_ge(*drained("gate", n))
                act.activation(az_abs[:], az[:], ACT.Abs).then_inc(gate_act.sem, 1)
                act.activation(al[:, q % 2], al[:, q % 2], ACT.Exp).then_inc(gate_act.sem, 1)
                act.wait_ge(*gate_act.at(n, 1))
                act.activation(az_abs[:], az_abs[:], ACT.Exp, scale=-1.0).then_inc(gate_act.sem, 1)
                act.wait_ge(*drained("bz", n))
                act.activation(beta_e[:], beta_z[:], ACT.Exp, scale=-1.0).then_inc(gate_act.sem, 1)

            def keep_halo(s, buf, q, n, taps_done):
                act.wait_ge(*taps_done)
                tiles = buf.shape[1]
                src = no_halo[:, 0:tiles, :] if q == 0 else buf[:, :, BT:BT + KW - 1]
                act.activation(buf[:, :, 0:KW - 1], src, ACT.Copy).then_inc(s.sem, 1)

            def raw_out(u, n):
                use = ("qkv", u)
                act.wait_ge(*filled(use, n))
                act.wait_ge(*halo.at(n, 1))
                act.activation(raw[:, 2 * u:2 * u + 2, KW - 1:], psum(use)[:].rearrange("p (e t) -> p e t", e=2), ACT.Copy)
                act.wait_ge(*silu.at(n, max(u - 1, 0)))
                for e in range(2):
                    ins = act.activation(y[:, u % 2, e, :], psum(use)[:, e * BT:(e + 1) * BT], ACT.Copy,
                                         scale=w_conv[:, 2 * u + e, KW - 1:KW])
                ins.then_inc(free_sem(use), 1)

            def silu_out(u, n):
                act.wait_ge(*conv.at(n, 6 * u + 6))
                if u < 2:
                    dst = (kT, vT)[u]
                    for _, hs in halves:
                        for p in range(NPAIR):
                            ins = act.activation(dst[hs, p, :, hs], y[hs, u % 2, p, :].rearrange("q (c t) -> q c t", c=NC),
                                                 ACT.Silu)
                else:
                    ins = act.activation(qT[:, 2 * (u - 2):2 * (u - 1), :], y[:, u % 2], ACT.Silu)
                ins.then_inc(silu.sem, 1)

            def logs(n):
                act.wait_ge(*gate_act.at(n, 3))
                act.activation(az_abs[:], az_abs[:], ACT.Ln, bias=1.0).then_inc(gate_act.sem, 1)
                act.wait_ge(*k_red.at(n, 4))
                act.activation(k_ln[:], k_nrm[:], ACT.Ln).then_inc(k_log.sem, 1)

            def stack(i, src, n):
                for _, hs in halves:
                    ins = act.activation(kv[hs, :, :, i, :], src[hs, :, :, hs], ACT.Copy)
                ins.then_inc(kv_done.sem, 1)

            def exp_spread(g, n):
                use = ("gbc", g)
                act.wait_ge(*filled(use, n))
                act.activation(expG[:, 2 * g:2 * g + 2, :], psum(use)[:].rearrange("p (e t) -> p e t", e=2), ACT.Exp)\
                   .then_inc(exp_g.sem, 1)

            def exp_mask(g, n):
                act.wait_ge(*masked.at(n, g + 1))
                act.activation(M[:, 2 * g:2 * g + 2, :], M[:, 2 * g:2 * g + 2, :], ACT.Exp).then_inc(exp_m.sem, 1)

            def place_state(t, n):
                act.wait_ge(*drained(("Hs0", t), n))
                act.wait_ge(*drained(("Hs1", t), n))
                if t >= 1:
                    act.wait_ge(*filled(("O", t - 1), n))
                for _, hs in halves:
                    ins = act.activation(Hd[hs, (t + 1) % 2, :, :, hs].rearrange("q i m d -> q (i m) d"),
                                         Hst[hs].rearrange("q i (m d) -> q (i m) d", m=2), ACT.Copy)
                ins.then_inc(h_placed.sem, 1)

            def o_out(t, n):
                use = ("O", t)
                act.wait_ge(*filled(use, n))
                act.activation(oT[:, :, t * CT:(t + 1) * CT], psum(use)[:].rearrange("p (i t) -> p i t", i=NT), ACT.Copy)\
                   .then_inc(free_sem(use), 1)

            def o_sqrt(n):
                act.wait_ge(*drained("ms", n))
                act.activation(part[0:HQ, :], part[0:HQ, :], ACT.Sqrt).then_inc(o_root.sem, 1)

            def xf_out(L, m):
                use = ("xt", L)
                act.wait_ge(*filled(use, m))
                act.activation(xfT[:, :, 1:], psum(use)[:].rearrange("p (k t) -> p k t", k=DK), ACT.Copy)\
                   .then_inc(free_sem(use), 1)

            def ffn_in(L, m, q):
                xf_out(L, m)
                kept, s = last_col[:, (2, 4).index(L), :], f_shift[L]
                act.activation(xfT[:, :, 0], kept, ACT.Copy).then_inc(s.sem, 1)
                act.wait_ge(*s.at(m, 1))
                act.wait_ge(*drained(("xt", L), m))
                act.activation(kept, no_halo[:, 0:DK, 0] if q == BPS - 1 else xfT[:, :, BT], ACT.Copy).then_inc(s.sem, 1)

            def ffn_act(L, m):
                copy_out(("r", L), m, r_t[:], ACT.Tanh, 0.5)
                copy_out(("k", L), m, kr[:].rearrange("p e t -> p (e t)"), ACT.Relu)

            def ssm_raw(u, m):
                use = ("in", u)
                act.wait_ge(*filled(use, m))
                act.wait_ge(*halo3.at(m, 1))
                act.activation(raw3[:, 2 * u:2 * u + 2, KW - 1:], psum(use)[:].rearrange("p (e t) -> p e t", e=2), ACT.Copy)
                for e in range(2):
                    k = 2 * u + e
                    ins = act.activation(y3[:, u, e, :], psum(use)[:, e * BT:(e + 1) * BT], ACT.Identity,
                                         scale=conv3_w[:, k, KW - 1:KW], bias=conv3_b[:, k:k + 1])
                ins.then_inc(free_sem(use), 1)

            def ssm_gate(u, m):
                copy_out(("in", 2 + u), m, sg[:, 2 * u:2 * u + 2, :].rearrange("p e t -> p (e t)"), ACT.Silu)

            def ssm_silu(u, m):
                act.wait_ge(*conv3.at(m, 6 * u + 6))
                act.activation(uT[:, 2 * u:2 * u + 2, :], y3[:, u], ACT.Silu).then_inc(silu3.sem, 1)

            def ssm_bu(m):
                act.wait_ge(*filled("bu", m))
                act.activation(bu[:], psum("bu")[0:STATE, 0:BT], ACT.Copy, scale=INPUT_FACTOR).then_inc(free_sem("bu"), 1)

            def step(n, q):
                attention, later = parts(n)
                m, qm = n - 1, (q - 1) % BPS
                if attention:
                    copy_out("xt1", n, xT1[:].rearrange("p k t -> p (k t)"))
                    keep_halo(halo, raw, q, n, conv.at(n, 0))
                    gate_exps(n, q)
                if later:
                    o_sqrt(m)
                if attention:
                    for u in range(NU):
                        raw_out(u, n)
                        if u >= 1:
                            silu_out(u - 1, n)
                    silu_out(NU - 1, n)
                    copy_out(("kt", 0), n, kD[:, 0].rearrange("p c s -> p (c s)"))
                    copy_out(("kt", 1), n, kD[:, 1].rearrange("p c s -> p (c s)"))
                    logs(n)
                    act.wait_ge(*k_normed.at(n, 2))
                    stack(0, kD, n)
                    act.wait_ge(*drained(("vt", 0), n))
                    act.wait_ge(*drained(("vt", 1), n))
                    stack(1, vD, n)
                    for g in range(4):
                        exp_spread(g, n)
                if later:
                    ffn_in(2, m, qm)
                if attention:
                    for g in range(4):
                        exp_mask(g, n)
                if later:
                    ffn_act(2, m)
                if later:
                    xf_out(3, m)
                    keep_halo(halo3, raw3, qm, m, conv3.at(m, 0))
                    ssm_raw(0, m)
                    ssm_raw(1, m)
                    if not attention:
                        ssm_gate(0, m)
                        ssm_gate(1, m)
                        ssm_silu(0, m)
                        ssm_silu(1, m)
                        ssm_bu(m)
                        ffn_in(4, m, qm)
                        ffn_act(4, m)
                if not attention:
                    return
                for t in range(NC + 1):
                    if t < NC:
                        place_state(t, n)
                    if t >= 1:
                        o_out(t - 1, n)
                    if later and t == 0:
                        ssm_gate(0, m)
                        ssm_gate(1, m)
                        ssm_silu(0, m)
                    if later and t == 1:
                        ssm_silu(1, m)
                        ssm_bu(m)
                    if later and t == 3:
                        ffn_in(4, m, qm)
                        ffn_act(4, m)

            act.wait_ge(*w_ready.at(0, N_READY))
            blocks(act, step)

        @block.vector
        def _(dve):
            dve.wait_ge(w_loaded.sem, 16 * len(loads))
            dve.tensor_scalar(w_o[:], w_o[:], norm_w[:, 0:1], None, ALU.mult).then_inc(w_ready.sem, 1)
            dve.tensor_copy(head_rows[:], M[0:96, :, 0:P]).then_inc(w_ready.sem, 1)
            dve.tensor_copy(head_cols[:], M[0:96, 0, P:P + HQ]).then_inc(w_ready.sem, 1)
            dve.tensor_scalar(f_v[:], f_v[:], 0.5, None, ALU.mult).then_inc(w_ready.sem, 1)
            dve.wait_ge(s_exp_a.sem, 1)
            dve.tensor_scalar(neg_a[:], neg_a[:], -1.0, None, ALU.mult).then_inc(w_ready.sem, 1)

            def norm(i, n, src, dst):
                s, L = ln_dve[i], LNS[i]
                for j in range(NJ):
                    dve.bn_stats(ln_stats[:, L, j, :], src[:, j, :]).then_inc(s.sem, 1)
                dve.drain()
                for j in range(NJ):
                    dve.bn_aggr(ln_mv[:, L, j, :], ln_stats[:, L, j, :]).then_inc(s.sem, 1)
                dve.wait_ge(*s.at(n, 2 * NJ))
                dve.tensor_scalar(ln_ve[:, L, :], ln_mv[:, L, :, 1], EPS_LN, None, ALU.add).then_inc(s.sem, 1)
                dve.wait_ge(*ln_root[i].at(n, 1))
                for j in range(NJ):
                    dve.tensor_scalar(dst[:, j, :], src[:, j, :], ln_mv[:, L, j, 0:1], ln_rs[:, L, j:j + 1],
                                      ALU.subtract, ALU.mult).then_inc(s.sem, 1)

            def gate_args(n, q):
                dve.wait_ge(*filled("gate", n))
                dve.tensor_scalar(az[:], psum("gate")[0:HQ, 0:BT], dt_bias[:, 0:1], None, ALU.add)
                dve.tensor_scalar(al[:, q % 2], psum("gate")[32:32 + HQ, 0:BT], -1.0, 40.0, ALU.mult, ALU.min)\
                   .then_inc(free_sem("gate"), 1)
                dve.wait_ge(*filled("bz", n))
                dve.tensor_copy(beta_z[:].rearrange("q (p c) -> q p c", p=NPAIR),
                                psum("bz")[:, 0:NC * NPAIR].rearrange("q (c p) -> q p c", c=NC)).then_inc(free_sem("bz"), 1)

            def gate_sums(n, q):
                dve.wait_ge(*gate_act.at(n, 4))
                dve.tensor_scalar(beta_e[:], beta_e[:], 1.0, None, ALU.add).then_inc(beta_done.sem, 1)
                dve.tensor_scalar(al[:, q % 2], al[:, q % 2], 1.0, None, ALU.add).then_inc(alpha_done.sem, 1)
                dve.wait_ge(*beta_done.at(n, 1))
                dve.reciprocal(beta[:], beta_e[:]).then_inc(beta_done.sem, 1)
                dve.wait_ge(*alpha_done.at(n, 1))
                dve.scalar_tensor_tensor(al[:, q % 2], al[:, q % 2], DH * EPS, al[:, q % 2], ALU.mult, ALU.mult).then_inc(alpha_done.sem, 1)

            def taps(s, base, n, acc, src, weights, tile):
                for i in range(KW - 1):
                    for e in range(2):
                        if i:
                            dve.wait_ge(*s.at(n, base + 2 * (i - 1) + e + 1))
                        dve.scalar_tensor_tensor(acc[:, e, :], src[:, tile + e, i:i + BT], weights[:, tile + e, i:i + 1],
                                                 acc[:, e, :], ALU.mult, ALU.add).then_inc(s.sem, 1)

            def convolve(u, n):
                dve.wait_ge(*drained(("qkv", u), n))
                taps(conv, 6 * u, n, y[:, u % 2], raw, w_conv, 2 * u)

            def split(s, base, n, src, dst):
                lo = [slice(32 * i, 32 * i + HQ) for i in range(3)]
                dve.tensor_copy(dst[lo[0], :], src).then_inc(s.sem, 1)
                dve.wait_ge(*s.at(n, base + 1))
                dve.tensor_tensor(part[lo[1], :], src, dst[lo[0], :], ALU.subtract).then_inc(s.sem, 1)
                dve.wait_ge(*s.at(n, base + 2))
                dve.tensor_copy(dst[lo[1], :], part[lo[1], :]).then_inc(s.sem, 1)
                dve.wait_ge(*s.at(n, base + 3))
                dve.tensor_tensor(part[lo[2], :], part[lo[1], :], dst[lo[1], :], ALU.subtract).then_inc(s.sem, 1)
                dve.wait_ge(*s.at(n, base + 4))
                dve.tensor_copy(dst[lo[2], :], part[lo[2], :]).then_inc(s.sem, 1)

            def log_decay(n):
                dve.wait_ge(*gate_act.at(n, 5))
                dve.scalar_tensor_tensor(az[:], az[:], 0.0, az_abs[:], ALU.max, ALU.add).then_inc(g_steps.sem, 1)
                dve.wait_ge(*g_steps.at(n, 1))
                dve.tensor_scalar(az[:], az[:], neg_a[:, 0:1], None, ALU.mult).then_inc(g_steps.sem, 1)
                dve.wait_ge(*g_steps.at(n, 2))
                dve.tensor_tensor_scan(gsum[:], chunk_start[:], az[:], 0.0, ALU.mult, ALU.add).then_inc(g_steps.sem, 1)
                dve.wait_ge(*g_steps.at(n, 3))
                split(g_steps, 3, n, gsum[:], g3)

            def k_norms(n):
                for p in range(NPAIR):
                    dve.wait_ge(*k_sq.at(n, p + 1))
                    dve.tensor_reduce(k_ss[:, p * NC:(p + 1) * NC], sq[:, 2 * p:2 * p + 2, :].rearrange(
                        "s a (c d) -> s (a c) d", d=P), AX_X, ALU.add).then_inc(k_red.sem, 1)
                dve.wait_ge(*k_root.at(n, 1))
                dve.tensor_scalar(k_nrm[:], k_nr[:], EPS, None, ALU.add).then_inc(k_red.sem, 1)
                dve.wait_ge(*k_red.at(n, 3))
                dve.reciprocal(k_rn[:], k_nrm[:]).then_inc(k_red.sem, 1)

            def v_out(p, n):
                use = ("vt", p)
                dve.wait_ge(*filled(use, n))
                dve.wait_ge(*beta_done.at(n, 2))
                dve.tensor_tensor(vD[:, p], psum(use)[:].rearrange("s (c d) -> s c d", c=NC),
                                  beta[:, p * NC:(p + 1) * NC].unsqueeze(2).broadcast_to([P, NC, P]), ALU.mult)\
                   .then_inc(free_sem(use), 1)

            def decay_cols(n):
                dve.wait_ge(*filled("gcol", n))
                dve.wait_ge(*k_log.at(n, 1))
                src = psum("gcol")[:, 0:NC * NT].rearrange("q (c p i) -> q p i c", c=NC, p=NPAIR)
                lns = k_ln[:].rearrange("q (p c) -> q p c", p=NPAIR).unsqueeze(2).broadcast_to([P, NPAIR, REP, NC])
                dve.tensor_tensor(gcol[:].rearrange("q (p i) c -> q p i c", p=NPAIR), src, lns, ALU.add)\
                   .then_inc(free_sem("gcol"), 1)

            def decay_diff(g, n):
                use = ("gbc", g)
                dve.wait_ge(*exp_g.at(n, g + 1))
                dve.wait_ge(*drained("gcol", n))
                cols = gcol[:, 2 * g:2 * g + 2, :].rearrange("s e c -> s (e c)").unsqueeze(2).broadcast_to([P, 2 * NC, CT])
                dve.tensor_tensor(M[:, 2 * g:2 * g + 2, :].rearrange("s e (c t) -> s (e c) t", c=NC),
                                  psum(use)[:].rearrange("s (f t) -> s f t", t=CT), cols, ALU.subtract)\
                   .then_inc(free_sem(use), 1)

            def weigh(name, i, t, n):
                use = (name, t)
                dve.wait_ge(*filled(use, n))
                dve.tensor_tensor(Pb[:, i], psum(use)[:].rearrange("s (i t) -> s i t", i=NT),
                                  M[:, :, t * CT:(t + 1) * CT], ALU.mult).then_inc(free_sem(use), 1)

            def correct(name, dst, t, n):
                use = (name, t)
                dve.wait_ge(*filled(use, n))
                dve.scalar_tensor_tensor(dst[:], psum(use)[:].rearrange("s (i t) -> s i t", i=NT), -DAMP,
                                         qT[:, :, t * CT:(t + 1) * CT], ALU.mult, ALU.add).then_inc(free_sem(use), 1)

            def add_state(p, t, n, q):
                use = (f"Hs{p}", t)
                dve.wait_ge(*filled(use, n))
                dve.wait_ge(*h_decayed.at(n, t + 1))
                part_ = Hst[:, p * REP:(p + 1) * REP, :]
                if q == BPS - 1 and t == NC - 1:
                    dve.memset(part_, 0.0).then_inc(free_sem(use), 1)
                else:
                    dve.tensor_tensor(part_, psum(use)[:].rearrange("s (i e) -> s i e", i=REP), part_, ALU.add)\
                       .then_inc(free_sem(use), 1)

            def head_vars(n, q):
                dve.wait_ge(*filled("ms", n))
                dve.tensor_tensor(part[0:HQ, :], psum("ms")[0:HQ, 0:BT], al[:, q % 2], ALU.add).then_inc(free_sem("ms"), 1)

            def head_scales(n):
                dve.wait_ge(*o_root.at(n, 1))
                dve.reciprocal(gsum[:], part[0:HQ, :]).then_inc(o_var.sem, 1)
                dve.wait_ge(*o_var.at(n, 1))
                split(o_var, 1, n, gsum[:], sc3)

            def scale_o(g, n):
                use = ("bc", g)
                dve.wait_ge(*filled(use, n))
                dve.tensor_tensor(oT[:, 2 * g:2 * g + 2, :], psum(use)[:].rearrange("s (e t) -> s e t", e=2),
                                  oT[:, 2 * g:2 * g + 2, :], ALU.mult).then_inc(free_sem(use), 1)

            def attention_residual(n, q):
                dve.wait_ge(*filled("wo", n))
                dve.wait_ge(*x_stored[q % 2].at(n, -8 * (q % 2)))
                dve.tensor_tensor(xres[:, q % 2], psum("wo")[:].rearrange("s (j d) -> s j d", j=NJ), xin[:, q % 2], ALU.add)\
                   .then_inc(free_sem("wo"), 1)

            def ffn_mix(L, m):
                dve.wait_ge(*f_shift[L].at(m, 3))
                for i in range(2):
                    for k in range(DK):
                        dve.scalar_tensor_tensor(mixed[:, i, k, :], diff[:, k, :], mu[:, i, k:k + 1], xfT[:, k, 0:BT],
                                                 ALU.mult, ALU.add).then_inc(f_mix[L].sem, 1)

            def ffn_out(L, m, q):
                use = ("v", L)
                dve.wait_ge(*filled(use, m))
                dve.scalar_tensor_tensor(diff[:].rearrange("p k t -> p (k t)"), r_t[:], 1.0, psum(use)[:], ALU.add,
                                         ALU.mult).then_inc(free_sem(use), 1)
                dve.wait_ge(*drained(use, m))
                dve.tensor_tensor(xres[:, q % 2], xres[:, q % 2], f_out, ALU.add).then_inc(f_res[L].sem, 1)

            def ssm_taps(u, m):
                dve.wait_ge(*drained(("in", u), m))
                taps(conv3, 6 * u, m, y3[:, u], raw3, conv3_w, 2 * u)

            def ssm_scan(m, q):
                dve.wait_ge(*drained("bu", m))
                dve.wait_ge(*scan3.at(m, 0))
                dve.tensor_tensor_scan(h3[:], decay[:, 0:1].broadcast_to([STATE, BT]), bu[:], h_last[:, 0:1],
                                       ALU.mult, ALU.add).then_inc(scan3.sem, 1)
                dve.wait_ge(*scan3.at(m, 1))
                if q == BPS - 1:
                    dve.memset(h_last[:], 0.0).then_inc(scan3.sem, 1)
                else:
                    dve.tensor_copy(h_last[:], h3[:, BT - 1:BT]).then_inc(scan3.sem, 1)

            def ssm_skip(v, m):
                use = ("y", v)
                dve.wait_ge(*filled(use, m))
                for e in range(2):
                    k = 2 * v + e
                    ins = dve.scalar_tensor_tensor(yT[:, k, :], uT[:, k, :], d_skip[:, k:k + 1],
                                                   psum(use)[:, e * BT:(e + 1) * BT], ALU.mult, ALU.add)
                ins.then_inc(free_sem(use), 1)

            def ssm_norm(m):
                dve.wait_ge(*filled("out", m))
                dve.tensor_tensor(z3, psum("out")[:].rearrange("p (j d) -> p j d", j=NJ), xn[:], ALU.add)\
                   .then_inc(free_sem("out"), 1)
                dve.wait_ge(*drained("out", m))
                norm(5, m, z3, z3)

            def step(n, q):
                attention, later = parts(n)
                m, qm = n - 1, (q - 1) % BPS
                if attention:
                    dve.wait_ge(*x_loaded[q % 2].at(n, 16 - 8 * (q % 2)))
                    norm(1, n, xin[:, q % 2], xn1)
                    gate_args(n, q)
                if later:
                    head_vars(m, qm)
                if attention:
                    convolve(0, n)
                if later:
                    head_scales(m)
                if attention:
                    gate_sums(n, q)
                    convolve(1, n)
                    convolve(2, n)
                    convolve(3, n)
                if later:
                    for g in range(4):
                        scale_o(g, m)
                if attention:
                    convolve(4, n)
                    convolve(5, n)
                    k_norms(n)
                if later:
                    attention_residual(m, qm)
                    dve.wait_ge(*drained("wo", m))
                if attention:
                    v_out(0, n)
                    v_out(1, n)
                    log_decay(n)
                    decay_cols(n)
                if later:
                    norm(2, m, xres[:, qm % 2], xn)
                if attention:
                    for g in range(4):
                        decay_diff(g, n)
                if later:
                    ffn_mix(2, m)
                    if not attention:
                        ffn_out(2, m, qm)
                        dve.wait_ge(*f_res[2].at(m, 1))
                        norm(3, m, xres[:, qm % 2], xn)
                        ssm_taps(0, m)
                        ssm_taps(1, m)
                        ssm_scan(m, qm)
                        ssm_skip(0, m)
                        ssm_skip(1, m)
                        ssm_norm(m)
                        dve.wait_ge(*l3_res.at(m, 3))
                        norm(4, m, xres[:, qm % 2], xn)
                        ffn_mix(4, m)
                        ffn_out(4, m, qm)
                if not attention:
                    return
                dve.wait_ge(*exp_m.at(n, 4))
                for t in range(NC + 1):
                    if t < NC:
                        weigh("S1", 0, t, n)
                    if later and t == 0:
                        ffn_out(2, m, qm)
                        dve.wait_ge(*f_res[2].at(m, 1))
                        norm(3, m, xres[:, qm % 2], xn)
                    if t >= 1:
                        if t >= 2:
                            dve.wait_ge(*x2_scaled.at(n, t - 1))
                        correct("A2", x2, t - 1, n)
                    if later and t == 2:
                        ssm_scan(m, qm)
                    if t < NC:
                        if t >= 1:
                            dve.wait_ge(*x1_scaled.at(n, t))
                        correct("A1", x1, t, n)
                    if later and t == 3:
                        ssm_norm(m)
                    if t >= 1:
                        weigh("S3", 2, t - 1, n)
                    if later and t == 2:
                        ssm_skip(0, m)
                        ssm_skip(1, m)
                    if t < NC:
                        add_state(0, t, n, q)
                        add_state(1, t, n, q)
                        weigh("S2", 1, t, n)
                    if later and t == 0:
                        ssm_taps(0, m)
                        ssm_taps(1, m)
                    if later and t == 3:
                        dve.wait_ge(*l3_res.at(m, 3))
                        norm(4, m, xres[:, qm % 2], xn)
                    if later and t == 4:
                        ffn_mix(4, m)
                if later:
                    ffn_out(4, m, qm)

            dve.wait_ge(*w_ready.at(0, N_READY))
            blocks(dve, step)

        @block.gpsimd
        def _(pool):
            for tile in (kT, vT, Hd, Hst, part, g3, sc3, raw, raw3, last_col, h_last, no_halo):
                pool.memset(tile[:], 0.0)
            pool.memset(decay[:], DECAY)
            pool.memset(half_neg[:], -0.5)
            pool.memset(half_pos[:], 0.5).then_inc(w_ready.sem, 1)
            pool.wait_ge(w_loaded.sem, 16 * len(loads))
            pool.wait_ge(*w_ready.at(0, N_READY))

            def rstd(i, n):
                L = LNS[i]
                pool.wait_ge(*ln_dve[i].at(n, 2 * NJ + 1))
                pool.tensor_tensor(ln_rs[:, L, :], ln_ve[:, L, :], half_neg[:, 0:NJ], ALU.pow).then_inc(ln_root[i].sem, 1)

            def k_squares(n):
                for p in range(NPAIR):
                    pool.wait_ge(*drained(("kt", p), n))
                    pool.tensor_tensor(sq[:, 2 * p:2 * p + 2, :].rearrange("s a t -> s (a t)"),
                                       kD[:, p].rearrange("s c d -> s (c d)"), kD[:, p].rearrange("s c d -> s (c d)"),
                                       ALU.mult).then_inc(k_sq.sem, 1)
                pool.wait_ge(*k_red.at(n, 2))
                pool.tensor_tensor(k_nr[:], k_ss[:], half_pos[:], ALU.pow).then_inc(k_root.sem, 1)

            def k_normalize(n):
                pool.wait_ge(*k_red.at(n, 4))
                for p in range(NPAIR):
                    rn = k_rn[:, p * NC:(p + 1) * NC].unsqueeze(2).broadcast_to([P, NC, P])
                    pool.tensor_tensor(kD[:, p], kD[:, p], rn, ALU.mult).then_inc(k_normed.sem, 1)

            def mask(g, n):
                pool.wait_ge(*drained(("gbc", g), n))
                view = M[:, 2 * g:2 * g + 2, :].rearrange("s e (c t) -> s (e c) t", c=NC)
                pool.tensor_tensor(view, view, causal[:].unsqueeze(1).broadcast_to([P, 2 * NC, CT]), ALU.add)\
                    .then_inc(masked.sem, 1)

            def last_weights(n):
                pool.wait_ge(*exp_m.at(n, 4))
                last = M[:].rearrange("s (p i) (c t) -> s p i c t", p=NPAIR, c=NC)[:, :, :, :, CT - 1]
                nrm = k_nrm[:].rearrange("s (p c) -> s p c", p=NPAIR).unsqueeze(2).broadcast_to([P, NPAIR, REP, NC])
                pool.tensor_tensor(wlast[:].rearrange("s (p i) c -> s p i c", p=NPAIR), last, nrm, ALU.mult)\
                    .then_inc(w_last.sem, 1)

            def scale_rows(dst, src, t):
                return pool.tensor_tensor(dst[:], src, expG[:, :, t * CT:(t + 1) * CT], ALU.mult)

            def scale_q(t, n):
                if t >= 1:
                    pool.wait_ge(*filled(("A1", t - 1), n))
                scale_rows(qE, qT[:, :, t * CT:(t + 1) * CT], t).then_inc(q_scaled.sem, 1)

            def weigh_kv(t, n):
                if t >= 1:
                    pool.wait_ge(*filled(("Hs1", t - 1), n))
                src = kv[:, :, t].rearrange("s p m d -> s p (m d)").unsqueeze(2).broadcast_to([P, NPAIR, REP, 2 * DH])
                wts = wlast[:, :, t].rearrange("s (p i) -> s p i", p=NPAIR).unsqueeze(3).broadcast_to([P, NPAIR, REP, 2 * DH])
                pool.tensor_tensor(R[:], src, wts, ALU.mult).then_inc(r_scaled.sem, 1)

            def decay_state(t, n):
                if t >= 1:
                    pool.wait_ge(*h_placed.at(n, t))
                else:
                    pool.wait_ge(*h_placed.at(n, 0))
                dec = expG[:, :, (t + 1) * CT - 1:(t + 1) * CT].broadcast_to([P, NT, 2 * DH])
                pool.tensor_tensor(Hst[:], Hst[:], dec, ALU.mult).then_inc(h_decayed.sem, 1)

            def o_squares(n):
                pool.wait_ge(*drained(("O", NC - 1), n))
                pool.wait_ge(*x2_scaled.at(n, NC))
                for g in range(4):
                    o = oT[:, 2 * g:2 * g + 2, :]
                    pool.tensor_tensor(sq[:, 2 * g:2 * g + 2, :], o, o, ALU.mult).then_inc(o_sq.sem, 1)

            def ffn_diff(L, m):
                s = f_shift[L]
                pool.wait_ge(*s.at(m, 1))
                pool.wait_ge(*drained(("xt", L), m))
                pool.tensor_tensor(diff[:], xfT[:, :, 1:], xfT[:, :, 0:BT], ALU.subtract).then_inc(s.sem, 1)

            def ffn_square(L, m):
                pool.wait_ge(*drained(("k", L), m))
                pool.tensor_tensor(kr[:], kr[:], kr[:], ALU.mult).then_inc(f_sq[L].sem, 1)

            def ssm_gated(v, m):
                pool.wait_ge(*drained(("y", v), m))
                pool.tensor_tensor(yT[:, 2 * v:2 * v + 2, :], yT[:, 2 * v:2 * v + 2, :], sg[:, 2 * v:2 * v + 2, :],
                                   ALU.mult).then_inc(gated3.sem, 1)

            def ssm_affine(m, q):
                pool.wait_ge(*ln_dve[5].at(m, 3 * NJ + 1))
                g_ = gam[:].unsqueeze(1).broadcast_to([P, NJ, D])
                b_ = bet3[:].unsqueeze(1).broadcast_to([P, NJ, D])
                pool.tensor_tensor(z3, z3, g_, ALU.mult).then_inc(l3_res.sem, 1)
                pool.wait_ge(*l3_res.at(m, 1))
                pool.tensor_tensor(z3, z3, b_, ALU.add).then_inc(l3_res.sem, 1)
                pool.wait_ge(*l3_res.at(m, 2))
                pool.tensor_tensor(xres[:, q % 2], xres[:, q % 2], z3, ALU.add).then_inc(l3_res.sem, 1)

            def step(n, q):
                attention, later = parts(n)
                m, qm = n - 1, (q - 1) % BPS
                if later:
                    o_squares(m)
                if attention:
                    rstd(1, n)
                    if later:
                        pool.wait_ge(*filled("ms", m))
                    k_squares(n)
                    k_normalize(n)
                if later:
                    rstd(2, m)
                if attention:
                    for g in range(4):
                        mask(g, n)
                if later:
                    ffn_diff(2, m)
                if attention:
                    last_weights(n)
                    scale_q(0, n)
                    pool.wait_ge(*kv_done.at(n, 2))
                    pool.wait_ge(*w_last.at(n, 1))
                    weigh_kv(0, n)
                    decay_state(0, n)
                if later:
                    ffn_square(2, m)
                    rstd(3, m)
                    if not attention:
                        ssm_gated(0, m)
                        ssm_gated(1, m)
                        rstd(5, m)
                        ssm_affine(m, qm)
                        rstd(4, m)
                        ffn_diff(4, m)
                        ffn_square(4, m)
                if not attention:
                    return
                for t in range(NC + 1):
                    if t >= 1:
                        pool.wait_ge(*drained(("A2", t - 1), n))
                        if t >= 2:
                            pool.wait_ge(*filled(("O", t - 2), n))
                        scale_rows(x2E, x2[:], t - 1).then_inc(x2_scaled.sem, 1)
                    if t < NC:
                        pool.wait_ge(*drained(("A1", t), n))
                        if t >= 1:
                            pool.wait_ge(*filled(("A2", t - 1), n))
                        scale_rows(x1E, x1[:], t).then_inc(x1_scaled.sem, 1)
                    if later and t == 3:
                        rstd(5, m)
                        ssm_affine(m, qm)
                        rstd(4, m)
                    if later and t == 2:
                        ssm_gated(0, m)
                        ssm_gated(1, m)
                    if t + 1 < NC:
                        scale_q(t + 1, n)
                        weigh_kv(t + 1, n)
                        decay_state(t + 1, n)
                    if later and t == 4:
                        ffn_diff(4, m)
                        ffn_square(4, m)

            blocks(pool, step)


def _tiles(w, n):
    import numpy as np
    return np.ascontiguousarray(np.asarray(w).reshape(n, P, -1).transpose(1, 0, 2))


def _laid_out(i):
    import numpy as np
    A = {k: np.asarray(v) for k, v in i.items()}
    g = lambda s: A["L0_attn_a_" + s]
    b3 = lambda s: A["L0_attn_b_" + s]
    f = lambda s: A["L0_ffn_" + s]
    heads = [(2 * p + h) * REP + i for p in range(NPAIR) for i in range(REP) for h in range(2)]
    wq = g("Wq").reshape(D, HQ, DH)[:, heads].reshape(D, HQ * DH)
    conv = g("Wconv")
    cq, ck, cv = conv[:HQ * DH], conv[HQ * DH:HQ * DH + HKV * DH], conv[HQ * DH + HKV * DH:]
    cq = cq.reshape(HQ, DH, KW)[heads].reshape(HQ * DH, KW)
    gate = np.zeros((D, 48), np.float32)
    gate[:, 0:HQ] = g("Wa")
    gate[:, 32:32 + HQ] = g("Walpha")
    rows = np.zeros((96, NT, P), np.float32)
    mean = np.zeros((P, NT, HQ), np.float32)
    for t in range(NT):
        for h in range(2):
            head = heads[2 * t + h]
            rows[[head, 32 + head, 64 + head], t, h * DH:(h + 1) * DH] = 1.0
            mean[h * DH:(h + 1) * DH, t, head] = 1.0 / DH
    cols = np.zeros((96, HQ), np.float32)
    for r in range(3):
        cols[32 * r:32 * r + HQ] = np.eye(HQ)[:, heads[0::2] + heads[1::2]]
    s, t = np.arange(P)[:, None] % CT, np.arange(CT)[None, :]
    start = np.ones((HQ, BT), np.float32)
    start[:, ::CT] = 0.0
    return {
        "x": g("x"),
        "w_qkv": _tiles(np.concatenate([g("Wk"), g("Wv"), wq], 1), DK),
        "w_gate": _tiles(gate, DK), "w_beta": _tiles(g("Wb")[:, [2 * p + h for h in range(2) for p in range(NPAIR)]], DK),
        "w_o": _tiles(g("Wo").reshape(HQ, DH, D)[heads].reshape(HQ * DH, D), NT),
        "w_conv": _tiles(np.concatenate([ck, cv, cq], 0), QKV),
        "f_r": _tiles(f("W_r").T, DK), "f_k": _tiles(f("W_k").T, DK), "f_v": _tiles(f("W_v").T, DK),
        "mu": np.ascontiguousarray(np.stack([f("mu_r").reshape(DK, P).T, f("mu_k").reshape(DK, P).T], 1)),
        "w_in": _tiles(b3("W_in").T, DK), "w_b": _tiles(b3("W_B").T, NE),
        "w_c": np.ascontiguousarray(b3("W_C").T), "w_out": _tiles(b3("W_out").T, NE),
        "conv3_w": _tiles(b3("conv_w").reshape(INNER, KW), NE),
        "conv3_b": np.ascontiguousarray(b3("conv_b").reshape(NE, P).T),
        "d_skip": np.ascontiguousarray(b3("D_param").reshape(NE, P).T),
        "gam": np.ascontiguousarray(np.broadcast_to(b3("ln_gamma"), (P, D))),
        "bet3": np.ascontiguousarray(np.broadcast_to(b3("ln_beta"), (P, D))),
        "norm_w": np.ascontiguousarray(np.concatenate([g("norm_w")] * 2).reshape(P, 1)),
        "dt_bias": g("dt_bias").reshape(HQ, 1), "a_log": g("A_log").reshape(HQ, 1),
        "ident": np.eye(P, dtype=np.float32),
        "causal": np.where(t >= s, 0.0, -1e30).astype(np.float32),
        "chunk_start": start, "head_rows": rows, "head_cols": cols, "head_mean": mean,
    }


def kernel(**inputs):
    import numpy as np
    import concourse.bacc as bacc
    from concourse.bass_utils import run_bass_kernel_spmd

    nc = bacc.Bacc("TRN2", target_bir_lowering=False, num_devices=1)
    arrays, args = {}, {}
    for name, v in _laid_out(inputs).items():
        arrays[f"in_{name}"] = v
        args[name] = nc.dram_tensor(f"in_{name}", v.shape, mybir.dt.from_np(v.dtype), kind="ExternalInput").ap()
    out = nc.dram_tensor("out_x", (BATCH, T, D), F32, kind="ExternalOutput").ap()
    hybrid_block_kernel(nc, args, out)
    r = run_bass_kernel_spmd(nc, [arrays], core_ids=[0])
    return r.results[0]["out_x"]
```

```python
from contextlib import ExitStack

import concourse.bass as bass
from concourse import mybir

F32 = mybir.dt.float32
BF16 = mybir.dt.bfloat16
ALU = mybir.AluOpType
ACT = mybir.ActivationFunctionType
AX_X = mybir.AxisListType.X

P = 128
BATCH, T, D = 16, 1024, 256
HQ, HKV, DH = 16, 4, 64
BT = 256
CT = 64
NJ = BT // P
NC = BT // CT
NBLK = BATCH * T // BT
BPS = T // BT
DK = D // P
NPAIR = HKV // 2
REP = HQ // HKV
NT = NPAIR * REP
QKV = 2 * NPAIR + NT
NU = QKV // 2
KW = 4
INNER, STATE = 512, 64
NE = INNER // P
DAMP = 0.25
DECAY, INPUT_FACTOR = 0.95, 0.05
EPS_LN, EPS = 1e-5, 1e-6


class Stage:

    def __init__(self, sem, per, step=1):
        self.sem, self.per, self.step = sem, per, step

    def at(self, n, k):
        value = (n * self.per + k) * self.step
        return self.sem, max(value, 0) if isinstance(value, int) else value


BANK_USES = [
    ["xt1", "bz", ("qkv", 1), ("qkv", 3), ("kt", 1), ("vt", 0), ("qkv", 5), ("gbc", 0), ("mask", 0)],
    ["gate", ("qkv", 0), ("qkv", 2), ("kt", 0), ("qkv", 4), ("vt", 1), "gcol", ("gbc", 1), ("mask", 1)],
    [("r", 2), ("v", 2), ("in", 0), ("in", 2), "bu", ("y", 1), ("xt", 4), ("k", 4)],
    [("xt", 2), ("k", 2), ("xt", 3), ("in", 1), ("in", 3), ("y", 0), "out", ("r", 4), ("v", 4)],
    [("gbc", 2), ("mask", 2)] + [x for t in range(NC) for x in (("S1", t), ("Hs0", t))] + ["ms", ("bc", 0)],
    [x for t in range(NC) for x in (("Hs1", t), ("A2", t))] + [("bc", 1), "wo"],
    [("gbc", 3), ("mask", 3)] + [x for t in range(NC) for x in (("A1", t), ("S2", t))] + [("bc", 2)],
    [x for t in range(NC) for x in (("S3", t), ("O", t))] + [("bc", 3)],
]
USE = {use: (b, i) for b, uses in enumerate(BANK_USES) for i, use in enumerate(uses)}


def hybrid_block_kernel(nc: bass.Bass, a: dict, out: bass.AP):
    ctx = ExitStack()
    with ctx:
        def sb(name, shape, dt=F32):
            return ctx.enter_context(nc.sbuf_tensor(name, shape, dt))

        def stage(name, per, step=1):
            return Stage(ctx.enter_context(nc.semaphore(name)), per, step)

        bank = [ctx.enter_context(nc.psum_tensor(f"bank{b}", [P, 512], F32)) for b in range(8)]

        w_qkv = sb("w_qkv", [P, DK, QKV * P])
        w_gate = sb("w_gate", [P, DK, 48])
        w_beta = sb("w_beta", [P, DK, HKV])
        w_o = sb("w_o", [P, NT, D])
        w_conv = sb("w_conv", [P, QKV, KW])
        f_r = sb("f_r", [P, DK, D])
        f_k = sb("f_k", [P, DK, D])
        f_v = sb("f_v", [P, DK, D])
        mu = sb("mu", [P, 2, DK])
        w_in = sb("w_in", [P, DK, 2 * INNER])
        w_b = sb("w_b", [P, NE, STATE])
        w_c = sb("w_c", [STATE, INNER])
        w_out = sb("w_out", [P, NE, D])
        conv3_w = sb("conv3_w", [P, NE, KW])
        conv3_b = sb("conv3_b", [P, NE])
        d_skip = sb("d_skip", [P, NE])
        gam = sb("gam", [P, D])
        bet3 = sb("bet3", [P, D])
        norm_w = sb("norm_w", [P, 1])
        dt_bias = sb("dt_bias", [HQ, 1])
        neg_a = sb("neg_a", [HQ, 1])
        ident = sb("ident", [P, P])
        ident_b = sb("ident_b", [P, P], BF16)
        causal = sb("causal", [P, CT], BF16)
        chunk_start = sb("chunk_start", [HQ, BT])
        head_rows = sb("head_rows", [96, NT, P], BF16)
        head_cols = sb("head_cols", [96, HQ], BF16)
        head_mean = sb("head_mean", [P, NT, HQ])
        decay = sb("decay", [STATE, 1])
        no_halo = sb("no_halo", [P, QKV, KW - 1])
        half_neg = sb("half_neg", [P, 8])
        half_pos = sb("half_pos", [P, 8])
        xin = sb("xin", [P, 2, NJ, D])
        xres = sb("xres", [P, 2, NJ, D])
        xn1 = sb("xn1", [P, NJ, D])
        xn = sb("xn", [P, NJ, D])
        ln_stats = sb("ln_stats", [P, 5, NJ, 6])
        ln_mv = sb("ln_mv", [P, 5, NJ, 2])
        ln_ve = sb("ln_ve", [P, 5, NJ])
        ln_rs = sb("ln_rs", [P, 5, NJ])
        xT1 = sb("xT1", [P, DK, BT])
        raw = sb("raw", [P, QKV, KW - 1 + BT])
        y = sb("y", [P, 2, 2, BT])
        kT = sb("kT", [P, NPAIR, NC, P])
        vT = sb("vT", [P, NPAIR, NC, P])
        qT = sb("qT", [P, NT, BT])
        kD = sb("kD", [P, NPAIR, NC, P])
        vD = sb("vD", [P, NPAIR, NC, P])
        kv = sb("kv", [P, NPAIR, NC, 2, DH])
        k_ss = sb("k_ss", [P, NPAIR * NC])
        k_nr = sb("k_nr", [P, NPAIR * NC])
        k_nrm = sb("k_nrm", [P, NPAIR * NC])
        k_rn = sb("k_rn", [P, NPAIR * NC])
        k_ln = sb("k_ln", [P, NPAIR * NC])
        beta = sb("beta", [P, NPAIR * NC])
        beta_e = sb("beta_e", [P, NPAIR * NC])
        beta_z = sb("beta_z", [P, NPAIR * NC])
        az = sb("az", [HQ, BT])
        az_abs = sb("az_abs", [HQ, BT])
        al = sb("al", [HQ, 2, BT])
        gsum = sb("gsum", [HQ, BT])
        part = sb("part", [96, BT])
        g3 = sb("g3", [96, BT], BF16)
        sc3 = sb("sc3", [96, BT], BF16)
        gcol = sb("gcol", [P, NT, NC])
        wlast = sb("wlast", [P, NT, NC])
        expG = sb("expG", [P, NT, BT])
        M = sb("M", [P, NT, BT])
        sq = expG
        Pb = sb("Pb", [P, 3, NT, CT])
        x1 = sb("x1", [P, NT, CT])
        x2 = sb("x2", [P, NT, CT])
        qE = sb("qE", [P, NT, CT])
        x1E = sb("x1E", [P, NT, CT])
        x2E = sb("x2E", [P, NT, CT])
        R = sb("R", [P, NPAIR, REP, 2 * DH])
        Hst = sb("Hst", [P, NT, 2 * DH])
        Hd = sb("Hd", [P, 2, NT, 2, P])
        oT = sb("oT", [P, NT, BT])
        xfT = sb("xfT", [P, DK, 1 + BT])
        last_col = sb("last_col", [P, 2, DK])
        diff = sb("diff", [P, DK, BT])
        mixed = sb("mixed", [P, 2, DK, BT])
        r_t = sb("r_t", [P, NJ * D])
        kr = sb("kr", [P, DK, BT])
        f_out = diff[:].rearrange("p k t -> p (k t)").rearrange("p (j d) -> p j d", j=NJ)
        raw3 = sb("raw3", [P, NE, KW - 1 + BT])
        uT = sb("uT", [P, NE, BT])
        sg = sb("sg", [P, NE, BT])
        bu = sb("bu", [STATE, BT])
        h3 = bu
        h_last = sb("h_last", [STATE, 1])
        yT = sb("yT", [P, NE, BT])
        y3 = mixed
        z3 = f_out

        full = [stage(f"bank{b}_full", len(u)) for b, u in enumerate(BANK_USES)]
        drained_ = [stage(f"bank{b}_drained", len(u)) for b, u in enumerate(BANK_USES)]
        w_loaded = stage("w_loaded", 0)
        w_ready = stage("w_ready", 0)
        s_exp_a = stage("exp_a_ready", 0)
        x_loaded = [stage(f"x_loaded{i}", 8) for i in range(2)]
        x_stored = [stage(f"x_stored{i}", 8) for i in range(2)]
        LNS = {1: 0, 2: 1, 3: 2, 4: 3, 5: 4}
        ln_dve = {i: stage(f"ln{i}_steps", 3 * NJ + 1) for i in LNS}
        ln_root = {i: stage(f"ln{i}_rstd", 1) for i in LNS}
        halo = stage("halo_ready", 1)
        conv = stage("conv_taps", 6 * NU)
        silu = stage("silu_done", NU)
        gate_act = stage("gate_exps", 5)
        beta_done = stage("beta_done", 2)
        alpha_done = stage("alpha_done", 2)
        g_steps = stage("g_steps", 8)
        k_sq = stage("k_squares", 2)
        k_red = stage("k_norm_steps", 4)
        k_root = stage("k_norm_root", 1)
        k_log = stage("k_norm_log", 1)
        k_normed = stage("k_normed", 2)
        kv_done = stage("kv_stacked", 2)
        gcol_done = stage("gcol_done", 1)
        exp_m = stage("exp_m_done", 4)
        w_last = stage("w_last_done", 1)
        q_scaled = stage("q_scaled", NC)
        x1_scaled = stage("x1_scaled", NC)
        x2_scaled = stage("x2_scaled", NC)
        r_scaled = stage("kv_weighted", NC)
        h_decayed = stage("h_decayed", NC)
        h_placed = stage("h_placed", NC)
        o_sq = stage("o_squares", NC)
        o_var = stage("o_scale_steps", 6)
        o_root = stage("o_scale_root", 1)
        f_shift = {i: stage(f"ffn{i}_shift", 3) for i in (2, 4)}
        f_mix = {i: stage(f"ffn{i}_mixed", 4) for i in (2, 4)}
        f_sq = {i: stage(f"ffn{i}_squared", 1) for i in (2, 4)}
        f_res = {i: stage(f"ffn{i}_residual", 1) for i in (2, 4)}
        halo3 = stage("halo3_ready", 1)
        conv3 = stage("conv3_taps", 12)
        silu3 = stage("silu3_done", 2)
        scan3 = stage("scan3_steps", 2)
        gated3 = stage("gated3_done", 2)
        l3_res = stage("l3_residual", 3)

        def fill(use, n):
            b, i = USE[use]
            return drained_[b].at(n, i)

        def filled(use, n):
            b, i = USE[use]
            return full[b].at(n, i + 1)

        def drained(use, n):
            b, i = USE[use]
            return drained_[b].at(n, i + 1)

        def full_sem(use):
            return full[USE[use][0]].sem

        def free_sem(use):
            return drained_[USE[use][0]].sem

        def psum(use):
            return bank[USE[use][0]]

        x_dram = a["x"].rearrange("b (q j p) d -> (b q) p j d", q=BPS, p=P)
        out_dram = out.rearrange("b (q j p) d -> (b q) p j d", q=BPS, p=P)
        halves = [(0, slice(0, DH)), (1, slice(DH, P))]

        loads = [
            (w_qkv[:], "w_qkv"), (w_gate[:], "w_gate"), (w_beta[:], "w_beta"), (w_o[:], "w_o"), (w_conv[:], "w_conv"),
            (f_r[:], "f_r"), (f_k[:], "f_k"), (f_v[:], "f_v"), (mu[:], "mu"), (w_in[:], "w_in"), (w_b[:], "w_b"), (w_c[:], "w_c"),
            (w_out[:], "w_out"), (conv3_w[:], "conv3_w"), (conv3_b[:], "conv3_b"), (d_skip[:], "d_skip"), (gam[:], "gam"),
            (bet3[:], "bet3"), (norm_w[:], "norm_w"), (dt_bias[:], "dt_bias"), (neg_a[:], "a_log"), (ident[:], "ident"),
            (M[:, 1, P:P + CT], "causal"), (chunk_start[:], "chunk_start"), (M[0:96, :, 0:P], "head_rows"), (M[0:96, 0, P:P + HQ], "head_cols"),
            (head_mean[:], "head_mean"),
        ]
        N_READY = 8

        def blocks(engine, step):
            for q in range(BPS):
                step(q, q)
            with engine.Fori(1, BATCH) as b:
                for q in range(BPS):
                    step(b * BPS + q, q)
            step(NBLK, 0)
            step(NBLK + 1, 1)

        def parts(n):
            return (True, True, True) if not isinstance(n, int) else (n < NBLK, 1 <= n <= NBLK, n >= 2)

        block = ctx.enter_context(nc.Block())

        @block.sync
        def _(sp):
            for tile, name in loads:
                sp.dma_start(tile, a[name]).then_inc(w_loaded.sem, 16)

            def load(n, slot):
                sp.wait_ge(*drained("wo", n - 2))
                sp.dma_start(xin[:, slot], x_dram[n]).then_inc(x_loaded[slot].sem, 16)

            def store(m, slot):
                sp.wait_ge(*f_res[4].at(m, 1))
                sp.dma_start(out_dram[m], xres[:, slot]).then_inc(x_stored[slot].sem, 16)

            load(0, 0)
            load(1, 1)
            for n in range(2, BPS):
                load(n, n % 2)
                store(n - 2, n % 2)
            with sp.Fori(1, BATCH) as b:
                for q in range(BPS):
                    load(b * BPS + q, q % 2)
                    store(b * BPS + q - 2, q % 2)
            for m in range(NBLK - 2, NBLK):
                store(m, m % 2)
            for slot in range(2):
                sp.wait_ge(*x_stored[slot].at(NBLK, 0))

        @block.tensor
        def _(pe):
            def transposes(use, n, src, ln):
                pe.wait_ge(*ln_dve[ln].at(n, 3 * NJ + 1))
                pe.wait_ge(*fill(use, n))
                for k in range(DK):
                    for j in range(NJ):
                        mm = pe.transpose(psum(use)[:, k * BT + j * P:k * BT + (j + 1) * P],
                                          src[:, j, k * P:(k + 1) * P], ident[:])
                mm.then_inc(full_sem(use), 1)

            def gates(n):
                pe.wait_ge(*drained("xt1", n))
                pe.wait_ge(*fill("gate", n))
                for k in range(DK):
                    mm = pe.matmul(psum("gate")[0:48, 0:BT], w_gate[:, k, :], xT1[:, k, :], start=k == 0, stop=k == DK - 1)
                mm.then_inc(full_sem("gate"), 1)
                pe.wait_ge(*fill("bz", n))
                for c in range(NC):
                    for h, hs in halves:
                        for k in range(DK):
                            mm = pe.matmul(psum("bz")[hs, c * NPAIR:(c + 1) * NPAIR], xT1[:, k, c * CT:(c + 1) * CT],
                                           w_beta[:, k, h * NPAIR:(h + 1) * NPAIR], start=k == 0, stop=k == DK - 1)
                mm.then_inc(full_sem("bz"), 1)

            def qkv(u, n):
                use = ("qkv", u)
                pe.wait_ge(*fill(use, n))
                for e in range(2):
                    for k in range(DK):
                        c = (2 * u + e) * P
                        mm = pe.matmul(psum(use)[:, e * BT:(e + 1) * BT], w_qkv[:, k, c:c + P], xT1[:, k, :],
                                       start=k == 0, stop=k == DK - 1)
                mm.then_inc(full_sem(use), 1)

            def kv_transposes(name, src, p, done, n):
                use = (name, p)
                pe.wait_ge(*silu.at(n, done))
                pe.wait_ge(*fill(use, n))
                for c in range(NC):
                    mm = pe.transpose(psum(use)[:, c * P:(c + 1) * P], src[:, p, c, :], ident[:])
                mm.then_inc(full_sem(use), 1)

            def decay_columns(n):
                pe.wait_ge(*g_steps.at(n, 8))
                pe.wait_ge(*fill("gcol", n))
                for c in range(NC):
                    for h, hs in halves:
                        mm = pe.matmul(psum("gcol")[hs, c * NT:(c + 1) * NT], g3[:, c * CT:(c + 1) * CT],
                                       head_cols[:, h * NT:(h + 1) * NT], start=True, stop=True)
                mm.then_inc(full_sem("gcol"), 1)

            def spread(name, src, g, n):
                use = (name, g)
                pe.wait_ge(*fill(use, n))
                for e in range(2):
                    mm = pe.matmul(psum(use)[:, e * BT:(e + 1) * BT], head_rows[:, 2 * g + e, :], src[:],
                                   start=e == 0, stop=name == "bc" and e == 1,
                                   skip_group_check=True)
                mm.then_inc(full_sem(use), 1)

            def add_mask(g, n):
                use = ("mask", g)
                pe.wait_ge(*fill(use, n))
                pe.matmul(psum(use)[:], ident_b[:], causal[:].unsqueeze(1).broadcast_to([P, 512 // CT, CT]),
                          start=False, stop=True, skip_group_check=True).then_inc(full_sem(use), 1)

            def score(name, src, t, n):
                use = (name, t)
                pe.wait_ge(*fill(use, n))
                for p in range(NPAIR):
                    mm = pe.matmul(psum(use)[:, p * REP * CT:(p + 1) * REP * CT], kT[:, p, t, :],
                                   src[:, p * REP:(p + 1) * REP, :], start=True, stop=True)
                mm.then_inc(full_sem(use), 1)

            def apply(name, values, Pi, scaled, m, t, n):
                use = (name, t)
                pe.wait_ge(*fill(use, n))
                for p in range(NPAIR):
                    pe.matmul(psum(use)[:, p * REP * CT:(p + 1) * REP * CT], values[:, p, t, :],
                              Pb[:, Pi, p * REP:(p + 1) * REP, :], start=p == 0, stop=False, skip_group_check=True)
                for i in range(NT):
                    mm = pe.matmul(psum(use)[:, i * CT:(i + 1) * CT], Hd[:, t % 2, i, m, :], scaled[:, i, :],
                                   start=False, stop=i == NT - 1, skip_group_check=True)
                mm.then_inc(full_sem(use), 1)

            def state(p, t, n):
                use = (f"Hs{p}", t)
                pe.wait_ge(*fill(use, n))
                pe.matmul(psum(use)[:], kD[:, p, t, :], R[:, p].rearrange("s i e -> s (i e)"),
                          start=True, stop=True).then_inc(full_sem(use), 1)

            def s1(t, n):
                if t == 0:
                    pe.wait_ge(*silu.at(n, NU))
                score("S1", qT[:, :, t * CT:(t + 1) * CT], t, n)

            def a1(t, n):
                pe.wait_ge(*k_normed.at(n, 2))
                pe.wait_ge(*drained(("S1", t), n))
                pe.wait_ge(*q_scaled.at(n, t + 1))
                pe.wait_ge(*h_placed.at(n, t))
                apply("A1", kD, 0, qE, 0, t, n)

            def s2(t, n):
                pe.wait_ge(*drained(("A1", t), n))
                score("S2", x1[:], t, n)

            def a2(t, n):
                pe.wait_ge(*drained(("S2", t), n))
                pe.wait_ge(*x1_scaled.at(n, t + 1))
                apply("A2", kD, 1, x1E, 0, t, n)

            def s3(t, n):
                pe.wait_ge(*drained(("A2", t), n))
                score("S3", x2[:], t, n)

            def o(t, n):
                pe.wait_ge(*drained(("S3", t), n))
                pe.wait_ge(*x2_scaled.at(n, t + 1))
                apply("O", vD, 2, x2E, 1, t, n)

            def new_state(t, n):
                pe.wait_ge(*r_scaled.at(n, t + 1))
                state(0, t, n)
                state(1, t, n)

            def head_means(half, n):
                pe.wait_ge(*o_sq.at(n, (half + 1) * NC // 2))
                pe.wait_ge(*fill("ms", n))
                ts = slice(half * P, (half + 1) * P)
                for i in range(NT):
                    mm = pe.matmul(psum("ms")[0:HQ, ts], head_mean[:, i, :], sq[:, i, ts], start=i == 0, stop=i == NT - 1)
                if half == BT // P - 1:
                    mm.then_inc(full_sem("ms"), 1)

            def attention_out(n):
                pe.wait_ge(*drained(("bc", 3), n))
                pe.wait_ge(*drained(("bc", 2), n))
                pe.wait_ge(*fill("wo", n))
                for j in range(NJ):
                    for i in range(NT):
                        mm = pe.matmul(psum("wo")[:, j * D:(j + 1) * D], oT[:, i, j * P:(j + 1) * P], w_o[:, i, :],
                                       start=i == 0, stop=i == NT - 1)
                mm.then_inc(full_sem("wo"), 1)

            def ffn_receptance(L, m):
                use = ("r", L)
                pe.wait_ge(*f_mix[L].at(m, 2))
                pe.wait_ge(*fill(use, m))
                for j in range(NJ):
                    for k in range(DK):
                        mm = pe.matmul(psum(use)[:, j * D:(j + 1) * D], mixed[:, 0, k, j * P:(j + 1) * P], f_r[:, k, :],
                                       start=k == 0, stop=k == DK - 1)
                mm.then_inc(full_sem(use), 1)

            def ffn_keys(L, m):
                use = ("k", L)
                pe.wait_ge(*f_mix[L].at(m, 4))
                pe.wait_ge(*fill(use, m))
                for e in range(DK):
                    for k in range(DK):
                        mm = pe.matmul(psum(use)[:, e * BT:(e + 1) * BT], f_k[:, k, e * P:(e + 1) * P],
                                       mixed[:, 1, k, :], start=k == 0, stop=k == DK - 1)
                mm.then_inc(full_sem(use), 1)

            def ffn_values(L, m):
                use = ("v", L)
                pe.wait_ge(*f_sq[L].at(m, 1))
                pe.wait_ge(*fill(use, m))
                for j in range(NJ):
                    for e in range(DK):
                        mm = pe.matmul(psum(use)[:, j * D:(j + 1) * D], kr[:, e, j * P:(j + 1) * P], f_v[:, e, :],
                                       start=e == 0, stop=e == DK - 1)
                mm.then_inc(full_sem(use), 1)

            def ssm_in(u, m):
                use = ("in", u)
                pe.wait_ge(*drained(("xt", 3), m))
                pe.wait_ge(*fill(use, m))
                for e in range(2):
                    for k in range(DK):
                        c = (2 * u + e) * P
                        mm = pe.matmul(psum(use)[:, e * BT:(e + 1) * BT], w_in[:, k, c:c + P], xfT[:, k, 1:1 + BT],
                                       start=k == 0, stop=k == DK - 1)
                mm.then_inc(full_sem(use), 1)

            def ssm_b(m):
                pe.wait_ge(*silu3.at(m, 2))
                pe.wait_ge(*fill("bu", m))
                for e in range(NE):
                    mm = pe.matmul(psum("bu")[0:STATE, 0:BT], w_b[:, e, :], uT[:, e, :], start=e == 0, stop=e == NE - 1)
                mm.then_inc(full_sem("bu"), 1)

            def ssm_c(v, m):
                use = ("y", v)
                pe.wait_ge(*scan3.at(m, 1))
                pe.wait_ge(*fill(use, m))
                for e in range(2):
                    c = (2 * v + e) * P
                    mm = pe.matmul(psum(use)[:, e * BT:(e + 1) * BT], w_c[:, c:c + P], h3[:], start=True, stop=True)
                mm.then_inc(full_sem(use), 1)

            def ssm_out(m):
                pe.wait_ge(*gated3.at(m, 2))
                pe.wait_ge(*fill("out", m))
                for j in range(NJ):
                    for e in range(NE):
                        mm = pe.matmul(psum("out")[:, j * D:(j + 1) * D], yT[:, e, j * P:(j + 1) * P], w_out[:, e, :],
                                       start=e == 0, stop=e == NE - 1)
                mm.then_inc(full_sem("out"), 1)

            def step(n, q):
                attention, later, last = parts(n)
                m, l = n - 1, n - 2
                if later:
                    a2(NC - 2, m)
                if last:
                    ssm_b(l)
                if attention:
                    transposes("xt1", n, xn1, 1)
                if later:
                    a1(NC - 1, m)
                    s3(NC - 2, m)
                if last:
                    ssm_c(0, l)
                    ssm_c(1, l)
                if later:
                    new_state(NC - 1, m)
                if attention:
                    gates(n)
                if later:
                    o(NC - 2, m)
                    s2(NC - 1, m)
                if attention:
                    qkv(0, n)
                    qkv(1, n)
                if later:
                    a2(NC - 1, m)
                if last:
                    ssm_out(l)
                if later:
                    head_means(0, m)
                    s3(NC - 1, m)
                if attention:
                    qkv(2, n)
                if later:
                    o(NC - 1, m)
                if attention:
                    qkv(3, n)
                    kv_transposes("kt", kT, 0, 1, n)
                    kv_transposes("kt", kT, 1, 1, n)
                if later:
                    head_means(1, m)
                if attention:
                    qkv(4, n)
                if last:
                    transposes(("xt", 4), l, xn, 4)
                if attention:
                    kv_transposes("vt", vT, 0, 2, n)
                    kv_transposes("vt", vT, 1, 2, n)
                    qkv(5, n)
                if last:
                    ffn_receptance(4, l)
                    ffn_keys(4, l)
                if attention:
                    decay_columns(n)
                if last:
                    ffn_values(4, l)
                if later:
                    pe.wait_ge(*o_var.at(m, 6))
                    for g in range(4):
                        spread("bc", sc3, g, m)
                if attention:
                    for g in range(4):
                        spread("gbc", g3, g, n)
                    for g in range(4):
                        add_mask(g, n)
                    s1(0, n)
                if later:
                    attention_out(m)
                    if not attention:
                        transposes(("xt", 2), m, xn, 2)
                        ffn_receptance(2, m)
                        ffn_keys(2, m)
                        ffn_values(2, m)
                        transposes(("xt", 3), m, xn, 3)
                        for u in range(4):
                            ssm_in(u, m)
                if not attention:
                    return
                a1(0, n)
                new_state(0, n)
                s2(0, n)
                if later:
                    transposes(("xt", 2), m, xn, 2)
                s1(1, n)
                a2(0, n)
                a1(1, n)
                s3(0, n)
                if later:
                    ffn_receptance(2, m)
                new_state(1, n)
                if later:
                    ffn_keys(2, m)
                o(0, n)
                s2(1, n)
                s1(2, n)
                if later:
                    ffn_values(2, m)
                a2(1, n)
                a1(2, n)
                if later:
                    transposes(("xt", 3), m, xn, 3)
                s3(1, n)
                new_state(2, n)
                if later:
                    ssm_in(0, m)
                    ssm_in(1, m)
                o(1, n)
                s2(2, n)
                if later:
                    ssm_in(2, m)
                s1(3, n)
                if later:
                    ssm_in(3, m)

            pe.wait_ge(*w_ready.at(0, N_READY))
            pe.wait_ge(*(w_loaded.sem, 16 * len(loads)))
            blocks(pe, step)

        @block.scalar
        def _(act):
            act.wait_ge(w_loaded.sem, 16 * len(loads))
            act.activation(neg_a[:], neg_a[:], ACT.Exp).then_inc(s_exp_a.sem, 1)

            def copy_out(use, n, dst, func=ACT.Copy, scale=1.0):
                act.wait_ge(*filled(use, n))
                act.activation(dst, psum(use)[:, 0:512], func, scale=scale).then_inc(free_sem(use), 1)

            def gate_exps(n, q):
                act.wait_ge(*drained("gate", n))
                act.activation(az_abs[:], az[:], ACT.Abs).then_inc(gate_act.sem, 1)
                act.activation(al[:, q % 2], al[:, q % 2], ACT.Exp).then_inc(gate_act.sem, 1)
                act.wait_ge(*gate_act.at(n, 1))
                act.activation(az_abs[:], az_abs[:], ACT.Exp, scale=-1.0).then_inc(gate_act.sem, 1)
                act.wait_ge(*drained("bz", n))
                act.activation(beta_e[:], beta_z[:], ACT.Exp, scale=-1.0).then_inc(gate_act.sem, 1)
                act.wait_ge(*gate_act.at(n, 3))
                act.activation(az_abs[:], az_abs[:], ACT.Ln, bias=1.0).then_inc(gate_act.sem, 1)

            def keep_halo(s, buf, q, n, taps_done):
                act.wait_ge(*taps_done)
                tiles = buf.shape[1]
                src = no_halo[:, 0:tiles, :] if q == 0 else buf[:, :, BT:BT + KW - 1]
                act.activation(buf[:, :, 0:KW - 1], src, ACT.Copy).then_inc(s.sem, 1)

            def raw_out(u, n):
                use = ("qkv", u)
                act.wait_ge(*filled(use, n))
                act.wait_ge(*halo.at(n, 1))
                act.activation(raw[:, 2 * u:2 * u + 2, KW - 1:], psum(use)[:].rearrange("p (e t) -> p e t", e=2), ACT.Copy)
                act.wait_ge(*silu.at(n, max(u - 1, 0)))
                for e in range(2):
                    ins = act.activation(y[:, u % 2, e, :], psum(use)[:, e * BT:(e + 1) * BT], ACT.Copy,
                                         scale=w_conv[:, 2 * u + e, KW - 1:KW])
                ins.then_inc(free_sem(use), 1)

            def silu_out(u, n):
                if u == 0:
                    act.wait_ge(*filled(("S3", NC - 1), n - 1))
                act.wait_ge(*conv.at(n, 6 * u + 6))
                if u < 2:
                    dst = (kT, vT)[u]
                    for _, hs in halves:
                        for p in range(NPAIR):
                            ins = act.activation(dst[hs, p, :, hs], y[hs, u % 2, p, :].rearrange("q (c t) -> q c t", c=NC),
                                                 ACT.Silu)
                else:
                    ins = act.activation(qT[:, 2 * (u - 2):2 * (u - 1), :], y[:, u % 2], ACT.Silu)
                ins.then_inc(silu.sem, 1)

            def log_norms(n):
                act.wait_ge(*k_red.at(n, 4))
                act.activation(k_ln[:], k_nrm[:], ACT.Ln).then_inc(k_log.sem, 1)

            def stack(i, src, n):
                for _, hs in halves:
                    ins = act.activation(kv[hs, :, :, i, :], src[hs, :, :, hs], ACT.Copy)
                ins.then_inc(kv_done.sem, 1)

            def exp_spread(g, n):
                use = ("gbc", g)
                act.wait_ge(*filled(use, n))
                act.activation(expG[:, 2 * g:2 * g + 2, :], psum(use)[:].rearrange("p (e t) -> p e t", e=2), ACT.Exp)\
                   .then_inc(free_sem(use), 1)

            def exp_mask(g, n):
                act.wait_ge(*drained(("mask", g), n))
                act.activation(M[:, 2 * g:2 * g + 2, :], M[:, 2 * g:2 * g + 2, :], ACT.Exp).then_inc(exp_m.sem, 1)

            def place_state(t, n):
                act.wait_ge(*drained(("Hs0", t), n))
                act.wait_ge(*drained(("Hs1", t), n))
                if t >= 1:
                    act.wait_ge(*filled(("O", t - 1), n))
                for _, hs in halves:
                    ins = act.activation(Hd[hs, (t + 1) % 2, :, :, hs].rearrange("q i m d -> q (i m) d"),
                                         Hst[hs].rearrange("q i (m d) -> q (i m) d", m=2), ACT.Copy)
                ins.then_inc(h_placed.sem, 1)

            def o_out(t, n):
                use = ("O", t)
                act.wait_ge(*filled(use, n))
                src, ts = psum(use)[:].rearrange("p (i t) -> p i t", i=NT), slice(t * CT, (t + 1) * CT)
                act.activation(sq[:, :, ts], src, ACT.Square).then_inc(o_sq.sem, 1)
                act.activation(oT[:, :, ts], src, ACT.Copy).then_inc(free_sem(use), 1)

            def o_sqrt(n):
                act.wait_ge(*drained("ms", n))
                act.activation(part[0:HQ, :], part[0:HQ, :], ACT.Sqrt).then_inc(o_root.sem, 1)

            def xf_out(L, m):
                use = ("xt", L)
                act.wait_ge(*filled(use, m))
                act.activation(xfT[:, :, 1:], psum(use)[:].rearrange("p (k t) -> p k t", k=DK), ACT.Copy)\
                   .then_inc(free_sem(use), 1)

            def ffn_in(L, m, q):
                xf_out(L, m)
                kept, s = last_col[:, (2, 4).index(L), :], f_shift[L]
                act.activation(xfT[:, :, 0], kept, ACT.Copy).then_inc(s.sem, 1)
                act.wait_ge(*s.at(m, 1))
                act.wait_ge(*drained(("xt", L), m))
                act.activation(kept, no_halo[:, 0:DK, 0] if q == BPS - 1 else xfT[:, :, BT], ACT.Copy).then_inc(s.sem, 1)

            def ffn_act(L, m):
                copy_out(("r", L), m, r_t[:], ACT.Tanh, 0.5)
                copy_out(("k", L), m, kr[:].rearrange("p e t -> p (e t)"), ACT.Relu)
                act.wait_ge(*drained(("k", L), m))
                act.activation(kr[:], kr[:], ACT.Square).then_inc(f_sq[L].sem, 1)

            def ssm_raw(u, m):
                use = ("in", u)
                act.wait_ge(*filled(use, m))
                act.wait_ge(*halo3.at(m, 1))
                act.activation(raw3[:, 2 * u:2 * u + 2, KW - 1:], psum(use)[:].rearrange("p (e t) -> p e t", e=2), ACT.Copy)
                for e in range(2):
                    k = 2 * u + e
                    ins = act.activation(y3[:, u, e, :], psum(use)[:, e * BT:(e + 1) * BT], ACT.Identity,
                                         scale=conv3_w[:, k, KW - 1:KW], bias=conv3_b[:, k:k + 1])
                ins.then_inc(free_sem(use), 1)

            def ssm_gate(u, m):
                copy_out(("in", 2 + u), m, sg[:, 2 * u:2 * u + 2, :].rearrange("p e t -> p (e t)"), ACT.Silu)

            def ssm_silu(u, m):
                act.wait_ge(*conv3.at(m, 6 * u + 6))
                act.activation(uT[:, 2 * u:2 * u + 2, :], y3[:, u], ACT.Silu).then_inc(silu3.sem, 1)

            def ssm_bu(m):
                act.wait_ge(*filled("bu", m))
                act.activation(bu[:], psum("bu")[0:STATE, 0:BT], ACT.Copy, scale=INPUT_FACTOR).then_inc(free_sem("bu"), 1)

            def step(n, q):
                attention, later, last = parts(n)
                m, qm = n - 1, (q - 1) % BPS
                l, ql = n - 2, (q - 2) % BPS
                if last:
                    ssm_bu(l)
                if attention:
                    copy_out("xt1", n, xT1[:].rearrange("p k t -> p (k t)"))
                    keep_halo(halo, raw, q, n, conv.at(n, 0))
                    gate_exps(n, q)
                if later:
                    o_out(NC - 2, m)
                if attention:
                    raw_out(0, n)
                if later:
                    place_state(NC - 1, m)
                if attention:
                    raw_out(1, n)
                    silu_out(0, n)
                    raw_out(2, n)
                    silu_out(1, n)
                if later:
                    o_out(NC - 1, m)
                if attention:
                    raw_out(3, n)
                    copy_out(("kt", 0), n, kD[:, 0].rearrange("p c s -> p (c s)"))
                    copy_out(("kt", 1), n, kD[:, 1].rearrange("p c s -> p (c s)"))
                    silu_out(2, n)
                    raw_out(4, n)
                if last:
                    ffn_in(4, l, ql)
                if attention:
                    silu_out(3, n)
                if later:
                    o_sqrt(m)
                if attention:
                    log_norms(n)
                    raw_out(5, n)
                if last:
                    ffn_act(4, l)
                if attention:
                    silu_out(4, n)
                    act.wait_ge(*k_normed.at(n, 2))
                    stack(0, kD, n)
                    act.wait_ge(*drained(("vt", 0), n))
                    act.wait_ge(*drained(("vt", 1), n))
                    stack(1, vD, n)
                    silu_out(5, n)
                    for g in range(4):
                        exp_spread(g, n)
                    for g in range(4):
                        exp_mask(g, n)
                    place_state(0, n)
                if later:
                    ffn_in(2, m, qm)
                    ffn_act(2, m)
                if attention:
                    o_out(0, n)
                    place_state(1, n)
                if later:
                    xf_out(3, m)
                    keep_halo(halo3, raw3, qm, m, conv3.at(m, 0))
                    ssm_raw(0, m)
                    ssm_raw(1, m)
                if attention:
                    o_out(1, n)
                    place_state(2, n)
                if later:
                    ssm_gate(0, m)
                    ssm_gate(1, m)
                    ssm_silu(0, m)
                    ssm_silu(1, m)

            act.wait_ge(*w_ready.at(0, N_READY))
            blocks(act, step)

        @block.vector
        def _(dve):
            dve.wait_ge(w_loaded.sem, 16 * len(loads))
            dve.tensor_scalar(w_o[:], w_o[:], norm_w[:, 0:1], None, ALU.mult).then_inc(w_ready.sem, 1)
            dve.tensor_copy(ident_b[:], ident[:]).then_inc(w_ready.sem, 1)
            dve.tensor_copy(causal[:], M[:, 1, P:P + CT]).then_inc(w_ready.sem, 1)
            dve.tensor_copy(head_rows[:], M[0:96, :, 0:P]).then_inc(w_ready.sem, 1)
            dve.tensor_copy(head_cols[:], M[0:96, 0, P:P + HQ]).then_inc(w_ready.sem, 1)
            dve.tensor_scalar(f_v[:], f_v[:], 0.5, None, ALU.mult).then_inc(w_ready.sem, 1)
            dve.wait_ge(s_exp_a.sem, 1)
            dve.tensor_scalar(neg_a[:], neg_a[:], -1.0, None, ALU.mult).then_inc(w_ready.sem, 1)

            def norm_stats(i, n, src):
                s, L = ln_dve[i], LNS[i]
                for j in range(NJ):
                    dve.bn_stats(ln_stats[:, L, j, :], src[:, j, :]).then_inc(s.sem, 1)
                dve.drain()
                for j in range(NJ):
                    dve.bn_aggr(ln_mv[:, L, j, :], ln_stats[:, L, j, :]).then_inc(s.sem, 1)
                dve.wait_ge(*s.at(n, 2 * NJ))
                dve.tensor_scalar(ln_ve[:, L, :], ln_mv[:, L, :, 1], EPS_LN, None, ALU.add).then_inc(s.sem, 1)

            def norm_apply(i, n, src, dst):
                s, L = ln_dve[i], LNS[i]
                dve.wait_ge(*ln_root[i].at(n, 1))
                for j in range(NJ):
                    dve.tensor_scalar(dst[:, j, :], src[:, j, :], ln_mv[:, L, j, 0:1], ln_rs[:, L, j:j + 1],
                                      ALU.subtract, ALU.mult).then_inc(s.sem, 1)

            def gate_args(n, q):
                dve.wait_ge(*filled("gate", n))
                dve.tensor_scalar(az[:], psum("gate")[0:HQ, 0:BT], dt_bias[:, 0:1], None, ALU.add)
                dve.tensor_scalar(al[:, q % 2], psum("gate")[32:32 + HQ, 0:BT], -1.0, 40.0, ALU.mult, ALU.min)\
                   .then_inc(free_sem("gate"), 1)
                dve.wait_ge(*filled("bz", n))
                dve.tensor_copy(beta_z[:].rearrange("q (p c) -> q p c", p=NPAIR),
                                psum("bz")[:, 0:NC * NPAIR].rearrange("q (c p) -> q p c", c=NC)).then_inc(free_sem("bz"), 1)

            def gate_sums(n, q):
                dve.wait_ge(*gate_act.at(n, 4))
                dve.tensor_scalar(beta_e[:], beta_e[:], 1.0, None, ALU.add).then_inc(beta_done.sem, 1)
                dve.tensor_scalar(al[:, q % 2], al[:, q % 2], 1.0, None, ALU.add).then_inc(alpha_done.sem, 1)
                dve.wait_ge(*beta_done.at(n, 1))
                dve.reciprocal(beta[:], beta_e[:]).then_inc(beta_done.sem, 1)
                dve.wait_ge(*alpha_done.at(n, 1))
                dve.scalar_tensor_tensor(al[:, q % 2], al[:, q % 2], DH * EPS, al[:, q % 2], ALU.mult, ALU.mult).then_inc(alpha_done.sem, 1)

            def taps(s, base, n, acc, src, weights, tile):
                for i in range(KW - 1):
                    for e in range(2):
                        if i:
                            dve.wait_ge(*s.at(n, base + 2 * (i - 1) + e + 1))
                        dve.scalar_tensor_tensor(acc[:, e, :], src[:, tile + e, i:i + BT], weights[:, tile + e, i:i + 1],
                                                 acc[:, e, :], ALU.mult, ALU.add).then_inc(s.sem, 1)

            def convolve(u, n):
                dve.wait_ge(*drained(("qkv", u), n))
                taps(conv, 6 * u, n, y[:, u % 2], raw, w_conv, 2 * u)

            def split(s, base, n, src, dst):
                lo = [slice(32 * i, 32 * i + HQ) for i in range(3)]
                dve.tensor_copy(dst[lo[0], :], src).then_inc(s.sem, 1)
                dve.wait_ge(*s.at(n, base + 1))
                dve.tensor_tensor(part[lo[1], :], src, dst[lo[0], :], ALU.subtract).then_inc(s.sem, 1)
                dve.wait_ge(*s.at(n, base + 2))
                dve.tensor_copy(dst[lo[1], :], part[lo[1], :]).then_inc(s.sem, 1)
                dve.wait_ge(*s.at(n, base + 3))
                dve.tensor_tensor(part[lo[2], :], part[lo[1], :], dst[lo[1], :], ALU.subtract).then_inc(s.sem, 1)
                dve.wait_ge(*s.at(n, base + 4))
                dve.tensor_copy(dst[lo[2], :], part[lo[2], :]).then_inc(s.sem, 1)

            def log_decay(n):
                dve.wait_ge(*gate_act.at(n, 5))
                dve.scalar_tensor_tensor(az[:], az[:], 0.0, az_abs[:], ALU.max, ALU.add).then_inc(g_steps.sem, 1)
                dve.wait_ge(*g_steps.at(n, 1))
                dve.tensor_scalar(az[:], az[:], neg_a[:, 0:1], None, ALU.mult).then_inc(g_steps.sem, 1)
                dve.wait_ge(*g_steps.at(n, 2))
                dve.tensor_tensor_scan(gsum[:], chunk_start[:], az[:], 0.0, ALU.mult, ALU.add).then_inc(g_steps.sem, 1)
                dve.wait_ge(*g_steps.at(n, 3))
                split(g_steps, 3, n, gsum[:], g3)

            def k_sums(n):
                for p in range(NPAIR):
                    dve.wait_ge(*k_sq.at(n, p + 1))
                    dve.tensor_reduce(k_ss[:, p * NC:(p + 1) * NC], M[:, 2 * p:2 * p + 2, :].rearrange(
                        "s a (c d) -> s (a c) d", d=P), AX_X, ALU.add).then_inc(k_red.sem, 1)

            def k_norms(n):
                dve.wait_ge(*k_root.at(n, 1))
                dve.tensor_scalar(k_nrm[:], k_nr[:], EPS, None, ALU.add).then_inc(k_red.sem, 1)
                dve.wait_ge(*k_red.at(n, 3))
                dve.reciprocal(k_rn[:], k_nrm[:]).then_inc(k_red.sem, 1)

            def v_out(p, n):
                use = ("vt", p)
                dve.wait_ge(*filled(use, n))
                dve.wait_ge(*beta_done.at(n, 2))
                dve.tensor_tensor(vD[:, p], psum(use)[:].rearrange("s (c d) -> s c d", c=NC),
                                  beta[:, p * NC:(p + 1) * NC].unsqueeze(2).broadcast_to([P, NC, P]), ALU.mult)\
                   .then_inc(free_sem(use), 1)

            def decay_cols(n):
                dve.wait_ge(*filled("gcol", n))
                dve.wait_ge(*k_log.at(n, 1))
                src = psum("gcol")[:, 0:NC * NT].rearrange("q (c p i) -> q p i c", c=NC, p=NPAIR)
                lns = k_ln[:].rearrange("q (p c) -> q p c", p=NPAIR).unsqueeze(2).broadcast_to([P, NPAIR, REP, NC])
                dve.tensor_tensor(gcol[:].rearrange("q (p i) c -> q p i c", p=NPAIR), src, lns, ALU.add)\
                   .then_inc(free_sem("gcol"), 1)

            def decay_diff(g, n):
                use = ("mask", g)
                dve.wait_ge(*filled(use, n))
                dve.wait_ge(*drained("gcol", n))
                cols = gcol[:, 2 * g:2 * g + 2, :].rearrange("s e c -> s (e c)").unsqueeze(2).broadcast_to([P, 2 * NC, CT])
                dve.tensor_tensor(M[:, 2 * g:2 * g + 2, :].rearrange("s e (c t) -> s (e c) t", c=NC),
                                  psum(use)[:].rearrange("s (f t) -> s f t", t=CT), cols, ALU.subtract)\
                   .then_inc(free_sem(use), 1)

            def weigh(name, i, t, n):
                use = (name, t)
                dve.wait_ge(*filled(use, n))
                dve.tensor_tensor(Pb[:, i], psum(use)[:].rearrange("s (i t) -> s i t", i=NT),
                                  M[:, :, t * CT:(t + 1) * CT], ALU.mult).then_inc(free_sem(use), 1)

            def correct(name, dst, t, n):
                use = (name, t)
                dve.wait_ge(*filled(use, n))
                dve.scalar_tensor_tensor(dst[:], psum(use)[:].rearrange("s (i t) -> s i t", i=NT), -DAMP,
                                         qT[:, :, t * CT:(t + 1) * CT], ALU.mult, ALU.add).then_inc(free_sem(use), 1)

            def add_state(p, t, n, q):
                use = (f"Hs{p}", t)
                dve.wait_ge(*filled(use, n))
                dve.wait_ge(*h_decayed.at(n, t + 1))
                part_ = Hst[:, p * REP:(p + 1) * REP, :]
                if q == BPS - 1 and t == NC - 1:
                    dve.memset(part_, 0.0).then_inc(free_sem(use), 1)
                else:
                    dve.tensor_tensor(part_, psum(use)[:].rearrange("s (i e) -> s i e", i=REP), part_, ALU.add)\
                       .then_inc(free_sem(use), 1)

            def head_vars(n, q):
                dve.wait_ge(*filled("ms", n))
                dve.tensor_tensor(part[0:HQ, :], psum("ms")[0:HQ, 0:BT], al[:, q % 2], ALU.add).then_inc(free_sem("ms"), 1)

            def head_scales(n):
                dve.wait_ge(*o_root.at(n, 1))
                dve.reciprocal(gsum[:], part[0:HQ, :]).then_inc(o_var.sem, 1)
                dve.wait_ge(*o_var.at(n, 1))
                split(o_var, 1, n, gsum[:], sc3)

            def scale_o(g, n):
                use = ("bc", g)
                dve.wait_ge(*filled(use, n))
                dve.tensor_tensor(oT[:, 2 * g:2 * g + 2, :], psum(use)[:].rearrange("s (e t) -> s e t", e=2),
                                  oT[:, 2 * g:2 * g + 2, :], ALU.mult).then_inc(free_sem(use), 1)

            def attention_residual(n, q):
                dve.wait_ge(*filled("wo", n))
                dve.wait_ge(*x_stored[q % 2].at(n, -8 * (q % 2)))
                dve.tensor_tensor(xres[:, q % 2], psum("wo")[:].rearrange("s (j d) -> s j d", j=NJ), xin[:, q % 2], ALU.add)\
                   .then_inc(free_sem("wo"), 1)

            def ffn_mix(L, m):
                dve.wait_ge(*f_shift[L].at(m, 3))
                for i in range(2):
                    for k in range(DK):
                        dve.scalar_tensor_tensor(mixed[:, i, k, :], diff[:, k, :], mu[:, i, k:k + 1], xfT[:, k, 0:BT],
                                                 ALU.mult, ALU.add).then_inc(f_mix[L].sem, 1)

            def ffn_out(L, m, q):
                use = ("v", L)
                dve.wait_ge(*filled(use, m))
                dve.scalar_tensor_tensor(diff[:].rearrange("p k t -> p (k t)"), r_t[:], 1.0, psum(use)[:], ALU.add,
                                         ALU.mult).then_inc(free_sem(use), 1)
                dve.wait_ge(*drained(use, m))
                dve.tensor_tensor(xres[:, q % 2], xres[:, q % 2], f_out, ALU.add).then_inc(f_res[L].sem, 1)

            def ssm_taps(u, m):
                dve.wait_ge(*drained(("in", u), m))
                taps(conv3, 6 * u, m, y3[:, u], raw3, conv3_w, 2 * u)

            def ssm_scan(m, q):
                dve.wait_ge(*drained("bu", m))
                dve.wait_ge(*scan3.at(m, 0))
                dve.tensor_tensor_scan(h3[:], decay[:, 0:1].broadcast_to([STATE, BT]), bu[:], h_last[:, 0:1],
                                       ALU.mult, ALU.add).then_inc(scan3.sem, 1)
                dve.wait_ge(*scan3.at(m, 1))
                if q == BPS - 1:
                    dve.memset(h_last[:], 0.0).then_inc(scan3.sem, 1)
                else:
                    dve.tensor_copy(h_last[:], h3[:, BT - 1:BT]).then_inc(scan3.sem, 1)

            def ssm_skip(v, m):
                use = ("y", v)
                dve.wait_ge(*filled(use, m))
                for e in range(2):
                    k = 2 * v + e
                    ins = dve.scalar_tensor_tensor(yT[:, k, :], uT[:, k, :], d_skip[:, k:k + 1],
                                                   psum(use)[:, e * BT:(e + 1) * BT], ALU.mult, ALU.add)
                ins.then_inc(free_sem(use), 1)

            def ssm_norm_stats(m):
                dve.wait_ge(*filled("out", m))
                dve.tensor_tensor(z3, psum("out")[:].rearrange("p (j d) -> p j d", j=NJ), xn[:], ALU.add)\
                   .then_inc(free_sem("out"), 1)
                dve.wait_ge(*drained("out", m))
                norm_stats(5, m, z3)

            def step(n, q):
                attention, later, last = parts(n)
                m, qm = n - 1, (q - 1) % BPS
                l, ql = n - 2, (q - 2) % BPS
                if attention:
                    dve.wait_ge(*x_loaded[q % 2].at(n, 16 - 8 * (q % 2)))
                    norm_stats(1, n, xin[:, q % 2])
                    norm_apply(1, n, xin[:, q % 2], xn1)
                if later:
                    dve.wait_ge(*x2_scaled.at(m, NC - 2))
                    correct("A2", x2, NC - 2, m)
                    dve.wait_ge(*x1_scaled.at(m, NC - 1))
                    correct("A1", x1, NC - 1, m)
                if last:
                    ssm_scan(l, ql)
                if later:
                    weigh("S3", 2, NC - 2, m)
                    add_state(0, NC - 1, m, qm)
                    add_state(1, NC - 1, m, qm)
                if attention:
                    gate_args(n, q)
                if later:
                    weigh("S2", 1, NC - 1, m)
                if last:
                    ssm_skip(0, l)
                    ssm_skip(1, l)
                if attention:
                    gate_sums(n, q)
                    convolve(0, n)
                if later:
                    dve.wait_ge(*x2_scaled.at(m, NC - 1))
                    correct("A2", x2, NC - 1, m)
                if last:
                    ssm_norm_stats(l)
                if later:
                    weigh("S3", 2, NC - 1, m)
                if last:
                    norm_apply(5, l, z3, z3)
                if attention:
                    convolve(1, n)
                    convolve(2, n)
                    log_decay(n)
                    k_sums(n)
                if last:
                    dve.wait_ge(*l3_res.at(l, 3))
                    norm_stats(4, l, xres[:, ql % 2])
                if attention:
                    convolve(3, n)
                if last:
                    norm_apply(4, l, xres[:, ql % 2], xn)
                if attention:
                    k_norms(n)
                if later:
                    head_vars(m, qm)
                if attention:
                    v_out(0, n)
                    v_out(1, n)
                    convolve(4, n)
                if last:
                    ffn_mix(4, l)
                if later:
                    head_scales(m)
                if attention:
                    convolve(5, n)
                    decay_cols(n)
                if later:
                    for g in range(4):
                        scale_o(g, m)
                if last:
                    ffn_out(4, l, ql)
                if attention:
                    for g in range(4):
                        decay_diff(g, n)
                    dve.wait_ge(*exp_m.at(n, 4))
                    weigh("S1", 0, 0, n)
                if later:
                    attention_residual(m, qm)
                    dve.wait_ge(*drained("wo", m))
                    norm_stats(2, m, xres[:, qm % 2])
                    norm_apply(2, m, xres[:, qm % 2], xn)
                    if not attention:
                        ffn_mix(2, m)
                        ffn_out(2, m, qm)
                        dve.wait_ge(*f_res[2].at(m, 1))
                        norm_stats(3, m, xres[:, qm % 2])
                        norm_apply(3, m, xres[:, qm % 2], xn)
                        ssm_taps(0, m)
                        ssm_taps(1, m)
                if not attention:
                    return
                correct("A1", x1, 0, n)
                add_state(0, 0, n, q)
                add_state(1, 0, n, q)
                weigh("S2", 1, 0, n)
                weigh("S1", 0, 1, n)
                if later:
                    ffn_mix(2, m)
                correct("A2", x2, 0, n)
                dve.wait_ge(*x1_scaled.at(n, 1))
                correct("A1", x1, 1, n)
                weigh("S3", 2, 0, n)
                add_state(0, 1, n, q)
                add_state(1, 1, n, q)
                weigh("S2", 1, 1, n)
                weigh("S1", 0, 2, n)
                if later:
                    ffn_out(2, m, qm)
                    dve.wait_ge(*f_res[2].at(m, 1))
                    norm_stats(3, m, xres[:, qm % 2])
                dve.wait_ge(*x2_scaled.at(n, 1))
                correct("A2", x2, 1, n)
                if later:
                    norm_apply(3, m, xres[:, qm % 2], xn)
                dve.wait_ge(*x1_scaled.at(n, 2))
                correct("A1", x1, 2, n)
                weigh("S3", 2, 1, n)
                add_state(0, 2, n, q)
                add_state(1, 2, n, q)
                weigh("S2", 1, 2, n)
                weigh("S1", 0, 3, n)
                if later:
                    ssm_taps(0, m)
                    ssm_taps(1, m)

            dve.wait_ge(*w_ready.at(0, N_READY))
            blocks(dve, step)

        @block.gpsimd
        def _(pool):
            for tile in (kT, vT, Hd, Hst, part, g3, sc3, raw, raw3, last_col, h_last, no_halo):
                pool.memset(tile[:], 0.0)
            pool.memset(decay[:], DECAY)
            pool.memset(half_neg[:], -0.5)
            pool.memset(half_pos[:], 0.5).then_inc(w_ready.sem, 1)
            pool.wait_ge(w_loaded.sem, 16 * len(loads))
            pool.wait_ge(*w_ready.at(0, N_READY))

            def rstd(i, n):
                L = LNS[i]
                pool.wait_ge(*ln_dve[i].at(n, 2 * NJ + 1))
                pool.tensor_tensor(ln_rs[:, L, :], ln_ve[:, L, :], half_neg[:, 0:NJ], ALU.pow).then_inc(ln_root[i].sem, 1)

            def k_squares(n):
                pool.wait_ge(*drained(("S3", NC - 1), n - 1))
                for p in range(NPAIR):
                    pool.wait_ge(*drained(("kt", p), n))
                    pool.tensor_tensor(M[:, 2 * p:2 * p + 2, :].rearrange("s a t -> s (a t)"),
                                       kD[:, p].rearrange("s c d -> s (c d)"), kD[:, p].rearrange("s c d -> s (c d)"),
                                       ALU.mult).then_inc(k_sq.sem, 1)

            def k_roots(n):
                pool.wait_ge(*k_red.at(n, 2))
                pool.tensor_tensor(k_nr[:], k_ss[:], half_pos[:], ALU.pow).then_inc(k_root.sem, 1)

            def k_normalize(n):
                pool.wait_ge(*k_red.at(n, 4))
                for p in range(NPAIR):
                    rn = k_rn[:, p * NC:(p + 1) * NC].unsqueeze(2).broadcast_to([P, NC, P])
                    pool.tensor_tensor(kD[:, p], kD[:, p], rn, ALU.mult).then_inc(k_normed.sem, 1)

            def last_weights(n):
                pool.wait_ge(*exp_m.at(n, 4))
                last = M[:].rearrange("s (p i) (c t) -> s p i c t", p=NPAIR, c=NC)[:, :, :, :, CT - 1]
                nrm = k_nrm[:].rearrange("s (p c) -> s p c", p=NPAIR).unsqueeze(2).broadcast_to([P, NPAIR, REP, NC])
                pool.tensor_tensor(wlast[:].rearrange("s (p i) c -> s p i c", p=NPAIR), last, nrm, ALU.mult)\
                    .then_inc(w_last.sem, 1)

            def scale_rows(dst, src, t):
                return pool.tensor_tensor(dst[:], src, expG[:, :, t * CT:(t + 1) * CT], ALU.mult)

            def scale_q(t, n):
                if t >= 1:
                    pool.wait_ge(*filled(("A1", t - 1), n))
                scale_rows(qE, qT[:, :, t * CT:(t + 1) * CT], t).then_inc(q_scaled.sem, 1)

            def weigh_kv(t, n):
                if t >= 1:
                    pool.wait_ge(*filled(("Hs1", t - 1), n))
                src = kv[:, :, t].rearrange("s p m d -> s p (m d)").unsqueeze(2).broadcast_to([P, NPAIR, REP, 2 * DH])
                wts = wlast[:, :, t].rearrange("s (p i) -> s p i", p=NPAIR).unsqueeze(3).broadcast_to([P, NPAIR, REP, 2 * DH])
                pool.tensor_tensor(R[:], src, wts, ALU.mult).then_inc(r_scaled.sem, 1)

            def decay_state(t, n):
                if t >= 1:
                    pool.wait_ge(*h_placed.at(n, t))
                else:
                    pool.wait_ge(*h_placed.at(n, 0))
                dec = expG[:, :, (t + 1) * CT - 1:(t + 1) * CT].broadcast_to([P, NT, 2 * DH])
                pool.tensor_tensor(Hst[:], Hst[:], dec, ALU.mult).then_inc(h_decayed.sem, 1)

            def ffn_diff(L, m):
                s = f_shift[L]
                pool.wait_ge(*s.at(m, 1))
                pool.wait_ge(*drained(("xt", L), m))
                pool.tensor_tensor(diff[:], xfT[:, :, 1:], xfT[:, :, 0:BT], ALU.subtract).then_inc(s.sem, 1)

            def ssm_gated(v, m):
                pool.wait_ge(*drained(("y", v), m))
                pool.tensor_tensor(yT[:, 2 * v:2 * v + 2, :], yT[:, 2 * v:2 * v + 2, :], sg[:, 2 * v:2 * v + 2, :],
                                   ALU.mult).then_inc(gated3.sem, 1)

            def ssm_affine(m, q):
                pool.wait_ge(*ln_dve[5].at(m, 3 * NJ + 1))
                g_ = gam[:].unsqueeze(1).broadcast_to([P, NJ, D])
                b_ = bet3[:].unsqueeze(1).broadcast_to([P, NJ, D])
                pool.tensor_tensor(z3, z3, g_, ALU.mult).then_inc(l3_res.sem, 1)
                pool.wait_ge(*l3_res.at(m, 1))
                pool.tensor_tensor(z3, z3, b_, ALU.add).then_inc(l3_res.sem, 1)
                pool.wait_ge(*l3_res.at(m, 2))
                pool.tensor_tensor(xres[:, q % 2], xres[:, q % 2], z3, ALU.add).then_inc(l3_res.sem, 1)

            def x1_rows(t, n):
                pool.wait_ge(*drained(("A1", t), n))
                if t >= 1:
                    pool.wait_ge(*filled(("A2", t - 1), n))
                scale_rows(x1E, x1[:], t).then_inc(x1_scaled.sem, 1)

            def x2_rows(t, n):
                pool.wait_ge(*drained(("A2", t), n))
                if t >= 1:
                    pool.wait_ge(*filled(("O", t - 1), n))
                scale_rows(x2E, x2[:], t).then_inc(x2_scaled.sem, 1)

            def step(n, q):
                attention, later, last = parts(n)
                m, qm = n - 1, (q - 1) % BPS
                l, ql = n - 2, (q - 2) % BPS
                if attention:
                    rstd(1, n)
                if later:
                    x2_rows(NC - 2, m)
                    x1_rows(NC - 1, m)
                if last:
                    ssm_gated(0, l)
                    ssm_gated(1, l)
                if later:
                    x2_rows(NC - 1, m)
                if last:
                    rstd(5, l)
                    ssm_affine(l, ql)
                if attention:
                    k_squares(n)
                if last:
                    rstd(4, l)
                if attention:
                    k_roots(n)
                    k_normalize(n)
                if last:
                    ffn_diff(4, l)
                if attention:
                    last_weights(n)
                    scale_q(0, n)
                    pool.wait_ge(*kv_done.at(n, 2))
                    pool.wait_ge(*w_last.at(n, 1))
                    weigh_kv(0, n)
                    decay_state(0, n)
                if later:
                    rstd(2, m)
                if attention:
                    x1_rows(0, n)
                    scale_q(1, n)
                if later:
                    ffn_diff(2, m)
                    if not attention:
                        rstd(3, m)
                if not attention:
                    return
                weigh_kv(1, n)
                decay_state(1, n)
                x2_rows(0, n)
                x1_rows(1, n)
                scale_q(2, n)
                weigh_kv(2, n)
                decay_state(2, n)
                if later:
                    rstd(3, m)
                x2_rows(1, n)
                x1_rows(2, n)
                scale_q(3, n)
                weigh_kv(3, n)
                decay_state(3, n)

            blocks(pool, step)


def _tiles(w, n):
    import numpy as np
    return np.ascontiguousarray(np.asarray(w).reshape(n, P, -1).transpose(1, 0, 2))


def _laid_out(i):
    import numpy as np
    A = {k: np.asarray(v) for k, v in i.items()}
    g = lambda s: A["L0_attn_a_" + s]
    b3 = lambda s: A["L0_attn_b_" + s]
    f = lambda s: A["L0_ffn_" + s]
    heads = [(2 * p + h) * REP + i for p in range(NPAIR) for i in range(REP) for h in range(2)]
    wq = g("Wq").reshape(D, HQ, DH)[:, heads].reshape(D, HQ * DH)
    conv = g("Wconv")
    cq, ck, cv = conv[:HQ * DH], conv[HQ * DH:HQ * DH + HKV * DH], conv[HQ * DH + HKV * DH:]
    cq = cq.reshape(HQ, DH, KW)[heads].reshape(HQ * DH, KW)
    gate = np.zeros((D, 48), np.float32)
    gate[:, 0:HQ] = g("Wa")
    gate[:, 32:32 + HQ] = g("Walpha")
    rows = np.zeros((96, NT, P), np.float32)
    mean = np.zeros((P, NT, HQ), np.float32)
    for t in range(NT):
        for h in range(2):
            head = heads[2 * t + h]
            rows[[head, 32 + head, 64 + head], t, h * DH:(h + 1) * DH] = 1.0
            mean[h * DH:(h + 1) * DH, t, head] = 1.0 / DH
    cols = np.zeros((96, HQ), np.float32)
    for r in range(3):
        cols[32 * r:32 * r + HQ] = np.eye(HQ)[:, heads[0::2] + heads[1::2]]
    s, t = np.arange(P)[:, None] % CT, np.arange(CT)[None, :]
    start = np.ones((HQ, BT), np.float32)
    start[:, ::CT] = 0.0
    return {
        "x": g("x"),
        "w_qkv": _tiles(np.concatenate([g("Wk"), g("Wv"), wq], 1), DK),
        "w_gate": _tiles(gate, DK), "w_beta": _tiles(g("Wb")[:, [2 * p + h for h in range(2) for p in range(NPAIR)]], DK),
        "w_o": _tiles(g("Wo").reshape(HQ, DH, D)[heads].reshape(HQ * DH, D), NT),
        "w_conv": _tiles(np.concatenate([ck, cv, cq], 0), QKV),
        "f_r": _tiles(f("W_r").T, DK), "f_k": _tiles(f("W_k").T, DK), "f_v": _tiles(f("W_v").T, DK),
        "mu": np.ascontiguousarray(np.stack([f("mu_r").reshape(DK, P).T, f("mu_k").reshape(DK, P).T], 1)),
        "w_in": _tiles(b3("W_in").T, DK), "w_b": _tiles(b3("W_B").T, NE),
        "w_c": np.ascontiguousarray(b3("W_C").T), "w_out": _tiles(b3("W_out").T, NE),
        "conv3_w": _tiles(b3("conv_w").reshape(INNER, KW), NE),
        "conv3_b": np.ascontiguousarray(b3("conv_b").reshape(NE, P).T),
        "d_skip": np.ascontiguousarray(b3("D_param").reshape(NE, P).T),
        "gam": np.ascontiguousarray(np.broadcast_to(b3("ln_gamma"), (P, D))),
        "bet3": np.ascontiguousarray(np.broadcast_to(b3("ln_beta"), (P, D))),
        "norm_w": np.ascontiguousarray(np.concatenate([g("norm_w")] * 2).reshape(P, 1)),
        "dt_bias": g("dt_bias").reshape(HQ, 1), "a_log": g("A_log").reshape(HQ, 1),
        "ident": np.eye(P, dtype=np.float32),
        "causal": np.where(t >= s, 0.0, -1e30).astype(np.float32),
        "chunk_start": start, "head_rows": rows, "head_cols": cols, "head_mean": mean,
    }


def kernel(**inputs):
    import numpy as np
    import concourse.bacc as bacc
    from concourse.bass_utils import run_bass_kernel_spmd

    nc = bacc.Bacc("TRN2", target_bir_lowering=False, num_devices=1)
    arrays, args = {}, {}
    for name, v in _laid_out(inputs).items():
        arrays[f"in_{name}"] = v
        args[name] = nc.dram_tensor(f"in_{name}", v.shape, mybir.dt.from_np(v.dtype), kind="ExternalInput").ap()
    out = nc.dram_tensor("out_x", (BATCH, T, D), F32, kind="ExternalOutput").ap()
    hybrid_block_kernel(nc, args, out)
    r = run_bass_kernel_spmd(nc, [arrays], core_ids=[0])
    return r.results[0]["out_x"]
```

```python
from contextlib import ExitStack

import concourse.bass as bass
from concourse import mybir

F32 = mybir.dt.float32
BF16 = mybir.dt.bfloat16
F32R = mybir.dt.float32r
ALU = mybir.AluOpType
ACT = mybir.ActivationFunctionType
AX_X = mybir.AxisListType.X

P = 128
BATCH, T, D = 16, 1024, 256
HQ, HKV, DH = 16, 4, 64
BT = 256
CT = 64
NJ = BT // P
NC = BT // CT
NBLK = BATCH * T // BT
BPS = T // BT
DK = D // P
NPAIR = HKV // 2
REP = HQ // HKV
NT = NPAIR * REP
QKV = 2 * NPAIR + NT
NU = QKV // 2
KW = 4
ALPHA, GROW = 0, 32
INNER, STATE = 512, 64
NE = INNER // P
DAMP = 0.25
DECAY, INPUT_FACTOR = 0.95, 0.05
EPS_LN, EPS = 1e-5, 1e-6


class Stage:

    def __init__(self, sem, per, step=1):
        self.sem, self.per, self.step = sem, per, step

    def at(self, n, k):
        value = (n * self.per + k) * self.step
        return self.sem, max(value, 0) if isinstance(value, int) else value


BANK_USES = [
    ["xt1", "bz", ("qkv", 1), ("qkv", 3), ("kt", 1), ("vt", 0), ("qkv", 5), ("gbc", 0), ("mask", 0)],
    ["gate", ("qkv", 0), ("qkv", 2), ("kt", 0), ("qkv", 4), ("vt", 1), "gcol", ("gbc", 1), ("mask", 1)],
    [("r", 2), ("v", 2), ("in", 0), ("in", 2), "bu", ("y", 1), ("xt", 4), ("k", 4)],
    [("xt", 2), ("k", 2), ("xt", 3), ("in", 1), ("in", 3), ("y", 0), "out", ("r", 4), ("v", 4)],
    [("gbc", 2), ("mask", 2), ("S1", 0), ("Hs0", 0), ("S1", 1), ("Hs0", 1), ("S1", 2), ("Hs0", 2), ("S1", 3),
     ("Hs0", 3), "ms", ("bc", 0)],
    [("Hs1", 0), ("A2", 0), ("Hs1", 1), ("A2", 1), ("Hs1", 2), ("A2", 2), ("Hs1", 3), ("A2", 3), ("bc", 1), "wo"],
    [("gbc", 3), ("mask", 3), ("A1", 0), ("S2", 0), ("A1", 1), ("S2", 1), ("A1", 2), ("S2", 2), ("A1", 3),
     ("S2", 3), ("bc", 2)],
    [("S3", 0), ("O", 0), ("S3", 1), ("O", 1), ("S3", 2), ("O", 2), ("S3", 3), ("O", 3), ("bc", 3)],
]
USE = {use: (b, i) for b, uses in enumerate(BANK_USES) for i, use in enumerate(uses)}


def hybrid_block_kernel(nc: bass.Bass, a: dict, out: bass.AP):
    ctx = ExitStack()
    with ctx:
        def sb(name, shape, dt=F32):
            return ctx.enter_context(nc.sbuf_tensor(name, shape, dt))

        def stage(name, per, step=1):
            return Stage(ctx.enter_context(nc.semaphore(name)), per, step)

        bank = [ctx.enter_context(nc.psum_tensor(f"bank{b}", [P, 512], F32)) for b in range(8)]

        w_qkv_hi = sb("w_qkv_hi", [P, DK, QKV * P], F32R)
        w_qkv_lo = sb("w_qkv_lo", [P, DK, QKV * P], F32R)
        w_gate = sb("w_gate", [P, DK, DH])
        w_beta = sb("w_beta", [P, DK, HKV])
        w_o = sb("w_o", [P, NT, D])
        w_conv = sb("w_conv", [P, QKV, KW])
        f_r = sb("f_r", [P, DK, D])
        f_k = sb("f_k", [P, DK, D])
        f_v = sb("f_v", [P, DK, D])
        mu = sb("mu", [P, 2, DK])
        w_in = sb("w_in", [P, DK, 2 * INNER])
        w_b = sb("w_b", [P, NE, STATE])
        w_c = sb("w_c", [P, NE, P])
        w_out = sb("w_out", [P, NE, D])
        conv3_w = sb("conv3_w", [P, NE, KW])
        conv3_b = sb("conv3_b", [P, NE])
        d_skip = sb("d_skip", [P, NE])
        gam = sb("gam", [P, D])
        bet3 = sb("bet3", [P, D])
        dt_bias = sb("dt_bias", [P, 1])
        neg_a = sb("neg_a", [P, 1])
        ident = sb("ident", [P, P])
        ident_b = sb("ident_b", [P, P], BF16)
        causal = sb("causal", [P, CT], BF16)
        chunk_start = sb("chunk_start", [P, P])
        head_rows = sb("head_rows", [96, NT, P], BF16)
        head_cols = sb("head_cols", [96, HQ], BF16)
        head_mean = sb("head_mean", [P, NT, DH])
        decay = sb("decay", [P, 1])
        no_halo = sb("no_halo", [P, NE, KW - 1])
        half_neg = sb("half_neg", [P, NJ])
        half_pos = sb("half_pos", [P, NPAIR * NC])
        xin = sb("xin", [P, 2, NJ, D])
        xres = sb("xres", [P, 2, NJ, D])
        xn1 = sb("xn1", [P, NJ, D])
        xn = sb("xn", [P, NJ, D])
        ln_stats = sb("ln_stats", [P, 5, NJ, 6])
        ln_mv = sb("ln_mv", [P, 5, NJ, 2])
        ln_ve = sb("ln_ve", [P, 5, NJ])
        ln_rs = sb("ln_rs", [P, 5, NJ])
        xT1 = sb("xT1", [P, DK, BT])
        xT1_hi = sb("xT1_hi", [P, DK, BT], F32R)
        xT1_lo = sb("xT1_lo", [P, DK, BT], F32R)
        raw = sb("raw", [P, 2, 2, KW - 1 + BT])
        raw_end = sb("raw_end", [P, 2, QKV, KW - 1])
        y = sb("y", [P, 4, 2, BT])
        kT = sb("kT", [P, NPAIR, NC, P])
        vT = sb("vT", [P, NPAIR, NC, P])
        qT = sb("qT", [P, NT, BT])
        kD = sb("kD", [P, NPAIR, NC, P])
        vD = sb("vD", [P, NPAIR, NC, P])
        kv = sb("kv", [P, NPAIR, NC, 2, DH])
        k_ss = sb("k_ss", [P, NPAIR * NC])
        k_nr = sb("k_nr", [P, NPAIR * NC])
        k_nrm = sb("k_nrm", [P, NPAIR * NC])
        k_rn = sb("k_rn", [P, NPAIR * NC])
        k_ln = sb("k_ln", [P, NPAIR * NC])
        beta = sb("beta", [P, NPAIR * NC])
        beta_e = sb("beta_e", [P, NPAIR * NC])
        beta_z = sb("beta_z", [P, NPAIR * NC])
        az = sb("az", [P, P])
        az_abs = sb("az_abs", [P, P])
        al = sb("al", [P, 2, P])
        gsum = sb("gsum", [P, P])
        o_scale = sb("o_scale", [P, P])
        part = sb("part", [96, BT])
        g3 = sb("g3", [96, BT], BF16)
        sc3 = sb("sc3", [96, BT], BF16)
        gcol = sb("gcol", [P, NT, NC])
        wlast = sb("wlast", [P, NT, NC])
        expG = sb("expG", [P, NT, BT])
        M = sb("M", [P, NT, BT])
        sq = expG
        Pb = sb("Pb", [P, 3, NT, CT])
        x1 = sb("x1", [P, NT, CT])
        x2 = sb("x2", [P, NT, CT])
        qE = sb("qE", [P, NT, CT])
        x1E = sb("x1E", [P, NT, CT])
        x2E = sb("x2E", [P, NT, CT])
        R = sb("R", [P, NPAIR, REP, 2 * DH])
        Hst = sb("Hst", [P, 2, NT, 2 * DH])
        oT = sb("oT", [P, NT, BT])
        xfT = sb("xfT", [P, DK, 1 + BT])
        last_col = sb("last_col", [P, 2, DK])
        diff = sb("diff", [P, DK, BT])
        mixed = sb("mixed", [P, 2, DK, BT])
        r_t = sb("r_t", [P, NJ * D])
        kr = sb("kr", [P, DK, BT])
        f_out = diff[:].rearrange("p k t -> p (k t)").rearrange("p (j d) -> p j d", j=NJ)
        raw3 = sb("raw3", [P, NE, KW - 1 + BT])
        uT = sb("uT", [P, NE, BT])
        sg = sb("sg", [P, NE, BT])
        bu = sb("bu", [P, BT])
        h3 = bu
        h_last = sb("h_last", [P, 1])
        yT = sb("yT", [P, NE, BT])
        y3 = mixed
        z3 = f_out

        full = [stage(f"bank{b}_full", len(u)) for b, u in enumerate(BANK_USES)]
        drained_ = [stage(f"bank{b}_drained", len(u)) for b, u in enumerate(BANK_USES)]
        w_loaded = stage("w_loaded", 0)
        w_ready = stage("w_ready", 0)
        w_split = stage("w_split", 0)
        x_split = stage("x_split", 2)
        s_exp_a = stage("exp_a_ready", 0)
        x_loaded = [stage(f"x_loaded{i}", 8) for i in range(2)]
        x_stored = [stage(f"x_stored{i}", 8) for i in range(2)]
        LNS = {1: 0, 2: 1, 3: 2, 4: 3, 5: 4}
        ln_dve = {i: stage(f"ln{i}_steps", 3 * NJ + 1) for i in LNS}
        ln_root = {i: stage(f"ln{i}_rstd", 1) for i in LNS}
        conv = stage("conv_taps", 6 * NU)
        silu = stage("silu_done", NU)
        gate_act = stage("gate_exps", 5)
        beta_done = stage("beta_done", 2)
        alpha_done = stage("alpha_done", 2)
        g_steps = stage("g_steps", 10)
        k_sq = stage("k_squares", 2)
        k_red = stage("k_norm_steps", 4)
        k_root = stage("k_norm_root", 1)
        k_log = stage("k_norm_log", 1)
        k_normed = stage("k_normed", 2)
        kv_done = stage("kv_stacked", 2)
        gcol_done = stage("gcol_done", 1)
        exp_m = stage("exp_m_done", 4)
        w_last = stage("w_last_done", 1)
        q_scaled = stage("q_scaled", NC)
        x1_scaled = stage("x1_scaled", NC)
        x2_scaled = stage("x2_scaled", NC)
        r_scaled = stage("kv_weighted", NC)
        h_decayed = stage("h_decayed", NC)
        o_sq = stage("o_squares", NC)
        o_var = stage("o_scale_steps", 8)
        o_root = stage("o_scale_root", 1)
        f_shift = {i: stage(f"ffn{i}_shift", 3) for i in (2, 4)}
        f_mix = {i: stage(f"ffn{i}_mixed", 4) for i in (2, 4)}
        f_sq = {i: stage(f"ffn{i}_squared", 1) for i in (2, 4)}
        f_res = {i: stage(f"ffn{i}_residual", 1) for i in (2, 4)}
        halo3 = stage("halo3_ready", 1)
        conv3 = stage("conv3_taps", 12)
        silu3 = stage("silu3_done", 2)
        scan3 = stage("scan3_steps", 2)
        gated3 = stage("gated3_done", 2)
        l3_res = stage("l3_residual", 3)

        def fill(use, n):
            b, i = USE[use]
            return drained_[b].at(n, i)

        def filled(use, n):
            b, i = USE[use]
            return full[b].at(n, i + 1)

        def drained(use, n):
            b, i = USE[use]
            return drained_[b].at(n, i + 1)

        def full_sem(use):
            return full[USE[use][0]].sem

        def free_sem(use):
            return drained_[USE[use][0]].sem

        def psum(use):
            return bank[USE[use][0]]

        x_dram = a["x"].rearrange("b (q j p) d -> (b q) p j d", q=BPS, p=P)
        out_dram = out.rearrange("b (q j p) d -> (b q) p j d", q=BPS, p=P)
        halves = [(0, slice(0, DH)), (1, slice(DH, P))]

        qkv_stage = [t[:].rearrange("p i t -> p (i t)")[:, 0:QKV * P] for t in (expG, oT)]
        loads = [
            (qkv_stage[0], "w_qkv0"), (qkv_stage[1], "w_qkv1"), (w_gate[:], "w_gate"), (w_beta[:], "w_beta"), (w_o[:], "w_o"), (w_conv[:], "w_conv"),
            (f_r[:], "f_r"), (f_k[:], "f_k"), (f_v[:], "f_v"), (mu[:], "mu"), (w_in[:], "w_in"), (w_b[:], "w_b"), (w_c[:], "w_c"),
            (w_out[:], "w_out"), (conv3_w[:], "conv3_w"), (conv3_b[:], "conv3_b"), (d_skip[:], "d_skip"), (gam[:], "gam"),
            (bet3[:], "bet3"), (M[:, 2, P:P + 1], "norm_w"), (dt_bias[:], "dt_bias"), (neg_a[:], "a_log"), (ident[:], "ident"),
            (M[:, 1, P:P + CT], "causal"), (chunk_start[:], "chunk_start"), (M[0:96, :, 0:P], "head_rows"), (M[0:96, 0, P:P + HQ], "head_cols"),
            (head_mean[:], "head_mean"),
        ]
        N_READY = 10

        def blocks(engine, step):
            for q in range(BPS):
                step(q, q)
            with engine.Fori(1, BATCH) as b:
                for q in range(BPS):
                    step(b * BPS + q, q)
            step(NBLK, 0)
            step(NBLK + 1, 1)

        def parts(n):
            return (True, True, True) if not isinstance(n, int) else (n < NBLK, 1 <= n <= NBLK, n >= 2)

        block = ctx.enter_context(nc.Block())

        @block.sync
        def _(sp):
            for tile, name in loads:
                sp.dma_start(tile, a[name]).then_inc(w_loaded.sem, 16)

            def load(n, slot):
                sp.wait_ge(*drained("wo", n - 2))
                sp.dma_start(xin[:, slot], x_dram[n]).then_inc(x_loaded[slot].sem, 16)

            def store(m, slot):
                sp.wait_ge(*f_res[4].at(m, 1))
                sp.dma_start(out_dram[m], xres[:, slot]).then_inc(x_stored[slot].sem, 16)

            load(0, 0)
            load(1, 1)
            for n in range(2, BPS):
                load(n, n % 2)
                store(n - 2, n % 2)
            with sp.Fori(1, BATCH) as b:
                for q in range(BPS):
                    load(b * BPS + q, q % 2)
                    store(b * BPS + q - 2, q % 2)
            for m in range(NBLK - 2, NBLK):
                store(m, m % 2)
            for slot in range(2):
                sp.wait_ge(*x_stored[slot].at(NBLK, 0))

        @block.tensor
        def _(pe):
            def transposes(use, n, src, ln):
                pe.wait_ge(*ln_dve[ln].at(n, 3 * NJ + 1))
                pe.wait_ge(*fill(use, n))
                for k in range(DK):
                    for j in range(NJ):
                        mm = pe.transpose(psum(use)[:, k * BT + j * P:k * BT + (j + 1) * P],
                                          src[:, j, k * P:(k + 1) * P], ident[:])
                mm.then_inc(full_sem(use), 1)

            def gates(n):
                pe.wait_ge(*drained("xt1", n))
                pe.wait_ge(*fill("gate", n))
                for k in range(DK):
                    for j, hs in halves:
                        mm = pe.matmul(psum("gate")[hs, 0:P], w_gate[:, k, :], xT1[:, k, j * P:(j + 1) * P],
                                       start=k == 0, stop=k == DK - 1)
                mm.then_inc(full_sem("gate"), 1)
                pe.wait_ge(*fill("bz", n))
                for c in range(NC):
                    for h, hs in halves:
                        for k in range(DK):
                            mm = pe.matmul(psum("bz")[hs, c * NPAIR:(c + 1) * NPAIR], xT1[:, k, c * CT:(c + 1) * CT],
                                           w_beta[:, k, h * NPAIR:(h + 1) * NPAIR], start=k == 0, stop=k == DK - 1)
                mm.then_inc(full_sem("bz"), 1)

            def qkv(u, n):
                use = ("qkv", u)
                pe.wait_ge(*x_split.at(n, 2))
                pe.wait_ge(*fill(use, n))
                parts_ = [(w, x, k) for k in range(DK) for w, x in
                          ((w_qkv_lo, xT1_hi), (w_qkv_hi, xT1_lo), (w_qkv_hi, xT1_hi))]
                for e in range(2):
                    c = (2 * u + e) * P
                    for i, (w, x, k) in enumerate(parts_):
                        mm = pe.matmul(psum(use)[:, e * BT:(e + 1) * BT], w[:, k, c:c + P], x[:, k, :],
                                       start=i == 0, stop=i == len(parts_) - 1)
                mm.then_inc(full_sem(use), 1)

            def kv_transposes(name, src, p, done, n):
                use = (name, p)
                pe.wait_ge(*silu.at(n, done))
                pe.wait_ge(*fill(use, n))
                for c in range(NC):
                    mm = pe.transpose(psum(use)[:, c * P:(c + 1) * P], src[:, p, c, :], ident[:])
                mm.then_inc(full_sem(use), 1)

            def decay_columns(n):
                pe.wait_ge(*g_steps.at(n, 10))
                pe.wait_ge(*fill("gcol", n))
                for c in range(NC):
                    for h, hs in halves:
                        mm = pe.matmul(psum("gcol")[hs, c * NT:(c + 1) * NT], g3[:, c * CT:(c + 1) * CT],
                                       head_cols[:, h * NT:(h + 1) * NT], start=True, stop=True)
                mm.then_inc(full_sem("gcol"), 1)

            def spread(name, src, g, n):
                use = (name, g)
                pe.wait_ge(*fill(use, n))
                for e in range(2):
                    mm = pe.matmul(psum(use)[:, e * BT:(e + 1) * BT], head_rows[:, 2 * g + e, :], src[:],
                                   start=e == 0, stop=name == "bc" and e == 1,
                                   skip_group_check=True)
                mm.then_inc(full_sem(use), 1)

            def add_mask(g, n):
                use = ("mask", g)
                pe.wait_ge(*fill(use, n))
                pe.matmul(psum(use)[:], ident_b[:], causal[:].unsqueeze(1).broadcast_to([P, 512 // CT, CT]),
                          start=False, stop=True, skip_group_check=True).then_inc(full_sem(use), 1)

            def score(name, src, t, n):
                use = (name, t)
                pe.wait_ge(*fill(use, n))
                for p in range(NPAIR):
                    mm = pe.matmul(psum(use)[:, p * REP * CT:(p + 1) * REP * CT], kT[:, p, t, :],
                                   src[:, p * REP:(p + 1) * REP, :], start=True, stop=True)
                mm.then_inc(full_sem(use), 1)

            def apply(name, values, Pi, scaled, m, t, n):
                use = (name, t)
                pe.wait_ge(*fill(use, n))
                for p in range(NPAIR):
                    pe.matmul(psum(use)[:, p * REP * CT:(p + 1) * REP * CT], values[:, p, t, :],
                              Pb[:, Pi, p * REP:(p + 1) * REP, :], start=p == 0, stop=False, skip_group_check=True)
                for i in range(NT):
                    for _, hs in halves:
                        mm = pe.matmul(psum(use)[hs, i * CT:(i + 1) * CT], Hst[hs, t % 2, i, m * DH:(m + 1) * DH],
                                       scaled[hs, i, :], start=False, stop=i == NT - 1, skip_group_check=True)
                mm.then_inc(full_sem(use), 1)

            def state(p, t, n):
                use = (f"Hs{p}", t)
                pe.wait_ge(*fill(use, n))
                pe.matmul(psum(use)[:], kD[:, p, t, :], R[:, p].rearrange("s i e -> s (i e)"),
                          start=True, stop=True).then_inc(full_sem(use), 1)

            def s1(t, n):
                if t == 0:
                    pe.wait_ge(*silu.at(n, NU))
                score("S1", qT[:, :, t * CT:(t + 1) * CT], t, n)

            def a1(t, n):
                pe.wait_ge(*k_normed.at(n, 2))
                pe.wait_ge(*drained(("S1", t), n))
                pe.wait_ge(*q_scaled.at(n, t + 1))
                pe.wait_ge(*(drained(("Hs0", t - 1), n) if t else drained(("Hs0", NC - 1), n - 1)))
                pe.wait_ge(*(drained(("Hs1", t - 1), n) if t else drained(("Hs1", NC - 1), n - 1)))
                apply("A1", kD, 0, qE, 0, t, n)

            def s2(t, n):
                pe.wait_ge(*drained(("A1", t), n))
                score("S2", x1[:], t, n)

            def a2(t, n):
                pe.wait_ge(*drained(("S2", t), n))
                pe.wait_ge(*x1_scaled.at(n, t + 1))
                apply("A2", kD, 1, x1E, 0, t, n)

            def s3(t, n):
                pe.wait_ge(*drained(("A2", t), n))
                score("S3", x2[:], t, n)

            def o(t, n):
                pe.wait_ge(*drained(("S3", t), n))
                pe.wait_ge(*x2_scaled.at(n, t + 1))
                apply("O", vD, 2, x2E, 1, t, n)

            def new_state(t, n):
                pe.wait_ge(*r_scaled.at(n, t + 1))
                state(0, t, n)
                state(1, t, n)

            def head_means(j, n):
                pe.wait_ge(*o_sq.at(n, (j + 1) * NC // NJ))
                pe.wait_ge(*fill("ms", n))
                for i in range(NT):
                    mm = pe.matmul(psum("ms")[halves[j][1], 0:P], head_mean[:, i, :], sq[:, i, j * P:(j + 1) * P],
                                   start=i == 0, stop=i == NT - 1)
                if j == NJ - 1:
                    mm.then_inc(full_sem("ms"), 1)

            def attention_out(n):
                pe.wait_ge(*drained(("bc", 3), n))
                pe.wait_ge(*drained(("bc", 2), n))
                pe.wait_ge(*fill("wo", n))
                for j in range(NJ):
                    for i in range(NT):
                        mm = pe.matmul(psum("wo")[:, j * D:(j + 1) * D], oT[:, i, j * P:(j + 1) * P], w_o[:, i, :],
                                       start=i == 0, stop=i == NT - 1)
                mm.then_inc(full_sem("wo"), 1)

            def ffn_receptance(L, m):
                use = ("r", L)
                pe.wait_ge(*f_mix[L].at(m, 2))
                pe.wait_ge(*fill(use, m))
                for j in range(NJ):
                    for k in range(DK):
                        mm = pe.matmul(psum(use)[:, j * D:(j + 1) * D], mixed[:, 0, k, j * P:(j + 1) * P], f_r[:, k, :],
                                       start=k == 0, stop=k == DK - 1)
                mm.then_inc(full_sem(use), 1)

            def ffn_keys(L, m):
                use = ("k", L)
                pe.wait_ge(*f_mix[L].at(m, 4))
                pe.wait_ge(*fill(use, m))
                for e in range(DK):
                    for k in range(DK):
                        mm = pe.matmul(psum(use)[:, e * BT:(e + 1) * BT], f_k[:, k, e * P:(e + 1) * P],
                                       mixed[:, 1, k, :], start=k == 0, stop=k == DK - 1)
                mm.then_inc(full_sem(use), 1)

            def ffn_values(L, m):
                use = ("v", L)
                pe.wait_ge(*f_sq[L].at(m, 1))
                pe.wait_ge(*fill(use, m))
                for j in range(NJ):
                    for e in range(DK):
                        mm = pe.matmul(psum(use)[:, j * D:(j + 1) * D], kr[:, e, j * P:(j + 1) * P], f_v[:, e, :],
                                       start=e == 0, stop=e == DK - 1)
                mm.then_inc(full_sem(use), 1)

            def ssm_in(u, m):
                use = ("in", u)
                pe.wait_ge(*drained(("xt", 3), m))
                pe.wait_ge(*fill(use, m))
                for e in range(2):
                    for k in range(DK):
                        c = (2 * u + e) * P
                        mm = pe.matmul(psum(use)[:, e * BT:(e + 1) * BT], w_in[:, k, c:c + P], xfT[:, k, 1:1 + BT],
                                       start=k == 0, stop=k == DK - 1)
                mm.then_inc(full_sem(use), 1)

            def ssm_b(m):
                pe.wait_ge(*silu3.at(m, 2))
                pe.wait_ge(*fill("bu", m))
                for e in range(NE // 2):
                    for v, hs in halves:
                        mm = pe.matmul(psum("bu")[hs, 0:BT], w_b[:, v * NE // 2 + e, :], uT[:, v * NE // 2 + e, :],
                                       start=e == 0, stop=e == NE // 2 - 1)
                mm.then_inc(full_sem("bu"), 1)

            def ssm_c(m):
                pe.wait_ge(*scan3.at(m, 1))
                for v in range(2):
                    use = ("y", v)
                    pe.wait_ge(*fill(use, m))
                    for e in range(2):
                        mm = pe.matmul(psum(use)[:, e * BT:(e + 1) * BT], w_c[:, 2 * v + e, :], h3[:], start=True, stop=True)
                    mm.then_inc(full_sem(use), 1)

            def ssm_out(m):
                pe.wait_ge(*gated3.at(m, 2))
                pe.wait_ge(*fill("out", m))
                for j in range(NJ):
                    for e in range(NE):
                        mm = pe.matmul(psum("out")[:, j * D:(j + 1) * D], yT[:, e, j * P:(j + 1) * P], w_out[:, e, :],
                                       start=e == 0, stop=e == NE - 1)
                mm.then_inc(full_sem("out"), 1)

            def step(n, q):
                attention, later, last = parts(n)
                m, l = n - 1, n - 2
                if later:
                    a2(NC - 2, m)
                    a1(NC - 1, m)
                if attention:
                    transposes("xt1", n, xn1, 1)
                if later:
                    s3(NC - 2, m)
                    s2(NC - 1, m)
                if attention:
                    gates(n)
                if last:
                    ssm_b(l)
                if attention:
                    qkv(0, n)
                if later:
                    o(NC - 2, m)
                if last:
                    ssm_c(l)
                if later:
                    new_state(NC - 1, m)
                if attention:
                    qkv(1, n)
                if later:
                    a2(NC - 1, m)
                if last:
                    ssm_out(l)
                if later:
                    s3(NC - 1, m)
                if attention:
                    qkv(2, n)
                    qkv(3, n)
                    kv_transposes("kt", kT, 0, 1, n)
                if later:
                    o(NC - 1, m)
                if attention:
                    kv_transposes("kt", kT, 1, 1, n)
                    qkv(4, n)
                    kv_transposes("vt", vT, 0, 2, n)
                if later:
                    head_means(0, m)
                if attention:
                    kv_transposes("vt", vT, 1, 2, n)
                if last:
                    transposes(("xt", 4), l, xn, 4)
                if attention:
                    qkv(5, n)
                if later:
                    head_means(1, m)
                if attention:
                    decay_columns(n)
                    spread("gbc", g3, 0, n)
                if last:
                    ffn_receptance(4, l)
                    ffn_keys(4, l)
                if later:
                    pe.wait_ge(*o_var.at(m, 8))
                    spread("bc", sc3, 0, m)
                    spread("bc", sc3, 2, m)
                if attention:
                    spread("gbc", g3, 1, n)
                    spread("gbc", g3, 2, n)
                    spread("gbc", g3, 3, n)
                if later:
                    spread("bc", sc3, 3, m)
                if attention:
                    add_mask(0, n)
                if later:
                    spread("bc", sc3, 1, m)
                if attention:
                    add_mask(1, n)
                    add_mask(2, n)
                if last:
                    ffn_values(4, l)
                if attention:
                    add_mask(3, n)
                    s1(0, n)
                if later:
                    attention_out(m)
                if attention:
                    a1(0, n)
                    new_state(0, n)
                    s2(0, n)
                    s1(1, n)
                if later:
                    transposes(("xt", 2), m, xn, 2)
                if attention:
                    a2(0, n)
                    a1(1, n)
                if later:
                    ffn_receptance(2, m)
                if attention:
                    s3(0, n)
                if later:
                    ffn_keys(2, m)
                if attention:
                    o(0, n)
                    s2(1, n)
                    new_state(1, n)
                if later:
                    ffn_values(2, m)
                if attention:
                    s1(2, n)
                    a2(1, n)
                    a1(2, n)
                    new_state(2, n)
                if later:
                    transposes(("xt", 3), m, xn, 3)
                if attention:
                    s3(1, n)
                if later:
                    ssm_in(0, m)
                if attention:
                    o(1, n)
                    s2(2, n)
                if later:
                    ssm_in(1, m)
                    ssm_in(2, m)
                if attention:
                    s1(3, n)
                if later:
                    ssm_in(3, m)

            pe.wait_ge(*w_ready.at(0, N_READY))
            pe.wait_ge(*(w_loaded.sem, 16 * len(loads)))
            blocks(pe, step)

        @block.scalar
        def _(act):
            act.wait_ge(w_loaded.sem, 16 * len(loads))
            act.activation(neg_a[:], neg_a[:], ACT.Exp).then_inc(s_exp_a.sem, 1)

            def copy_out(use, n, dst, func=ACT.Copy, scale=1.0):
                act.wait_ge(*filled(use, n))
                act.activation(dst, psum(use)[:, 0:512], func, scale=scale).then_inc(free_sem(use), 1)

            def x_out(n):
                act.wait_ge(*filled("xt1", n))
                src = psum("xt1")[:].rearrange("p (k t) -> p k t", k=DK)
                act.activation(xT1_hi[:], src, ACT.Copy).then_inc(x_split.sem, 1)
                act.activation(xT1[:], src, ACT.Copy).then_inc(free_sem("xt1"), 1)

            def gate_exps(n, q):
                act.wait_ge(*drained("gate", n))
                act.activation(az_abs[:], az[:], ACT.Abs).then_inc(gate_act.sem, 1)
                act.activation(al[:, q % 2], al[:, q % 2], ACT.Exp).then_inc(gate_act.sem, 1)
                act.wait_ge(*gate_act.at(n, 1))
                act.activation(az_abs[:], az_abs[:], ACT.Exp, scale=-1.0).then_inc(gate_act.sem, 1)
                act.wait_ge(*drained("bz", n))
                act.activation(beta_e[:], beta_z[:], ACT.Exp, scale=-1.0).then_inc(gate_act.sem, 1)
                act.wait_ge(*gate_act.at(n, 3))
                act.activation(az_abs[:], az_abs[:], ACT.Ln, bias=1.0).then_inc(gate_act.sem, 1)

            def keep_halo(s, buf, q, n, taps_done):
                act.wait_ge(*taps_done)
                tiles = buf.shape[1]
                src = no_halo[:, 0:tiles, :] if q == 0 else buf[:, :, BT:BT + KW - 1]
                act.activation(buf[:, :, 0:KW - 1], src, ACT.Copy).then_inc(s.sem, 1)

            def raw_out(u, n, q):
                use, k = ("qkv", u), 2 * u
                act.wait_ge(*filled(use, n))
                act.wait_ge(*conv.at(n, 6 * (u - 1)))
                src = psum(use)[:].rearrange("p (e t) -> p e t", e=2)
                before = no_halo[:, 0:2, :] if q == 0 else raw_end[:, (q + 1) % 2, k:k + 2, :]
                act.activation(raw[:, u % 2, :, 0:KW - 1], before, ACT.Copy)
                act.activation(raw[:, u % 2, :, KW - 1:], src, ACT.Copy)
                act.activation(raw_end[:, q % 2, k:k + 2, :], src[:, :, BT - KW + 1:], ACT.Copy)
                act.wait_ge(*silu.at(n, max(u - 3, 0)))
                for e in range(2):
                    ins = act.activation(y[:, u % 4, e, :], psum(use)[:, e * BT:(e + 1) * BT], ACT.Copy,
                                         scale=w_conv[:, k + e, KW - 1:KW])
                ins.then_inc(free_sem(use), 1)

            def silu_out(u, n):
                if u == 0:
                    act.wait_ge(*filled(("S3", NC - 1), n - 1))
                act.wait_ge(*conv.at(n, 6 * u + 6))
                if u < 2:
                    dst = (kT, vT)[u]
                    for _, hs in halves:
                        for p in range(NPAIR):
                            ins = act.activation(dst[hs, p, :, hs], y[hs, u % 4, p, :].rearrange("q (c t) -> q c t", c=NC),
                                                 ACT.Silu)
                else:
                    ins = act.activation(qT[:, 2 * (u - 2):2 * (u - 1), :], y[:, u % 4], ACT.Silu)
                ins.then_inc(silu.sem, 1)

            def log_norms(n):
                act.wait_ge(*k_red.at(n, 4))
                act.activation(k_ln[:], k_nrm[:], ACT.Ln).then_inc(k_log.sem, 1)

            def stack(i, src, n):
                for _, hs in halves:
                    ins = act.activation(kv[hs, :, :, i, :], src[hs, :, :, hs], ACT.Copy)
                ins.then_inc(kv_done.sem, 1)

            def exp_spread(g, n):
                use = ("gbc", g)
                act.wait_ge(*filled(use, n))
                act.activation(expG[:, 2 * g:2 * g + 2, :], psum(use)[:].rearrange("p (e t) -> p e t", e=2), ACT.Exp)\
                   .then_inc(free_sem(use), 1)

            def exp_mask(g, n):
                act.wait_ge(*drained(("mask", g), n))
                act.activation(M[:, 2 * g:2 * g + 2, :], M[:, 2 * g:2 * g + 2, :], ACT.Exp).then_inc(exp_m.sem, 1)

            def o_out(t, n):
                use = ("O", t)
                act.wait_ge(*filled(use, n))
                src, ts = psum(use)[:].rearrange("p (i t) -> p i t", i=NT), slice(t * CT, (t + 1) * CT)
                act.activation(sq[:, :, ts], src, ACT.Square).then_inc(o_sq.sem, 1)
                act.activation(oT[:, :, ts], src, ACT.Copy).then_inc(free_sem(use), 1)

            def o_sqrt(n):
                act.wait_ge(*drained("ms", n))
                act.activation(o_scale[:], o_scale[:], ACT.Sqrt).then_inc(o_root.sem, 1)

            def xf_out(L, m):
                use = ("xt", L)
                act.wait_ge(*filled(use, m))
                act.activation(xfT[:, :, 1:], psum(use)[:].rearrange("p (k t) -> p k t", k=DK), ACT.Copy)\
                   .then_inc(free_sem(use), 1)

            def ffn_in(L, m, q):
                xf_out(L, m)
                kept, s = last_col[:, (2, 4).index(L), :], f_shift[L]
                act.activation(xfT[:, :, 0], kept, ACT.Copy).then_inc(s.sem, 1)
                act.wait_ge(*s.at(m, 1))
                act.wait_ge(*drained(("xt", L), m))
                act.activation(kept, no_halo[:, 0:DK, 0] if q == BPS - 1 else xfT[:, :, BT], ACT.Copy).then_inc(s.sem, 1)

            def ffn_act(L, m):
                copy_out(("r", L), m, r_t[:], ACT.Tanh, 0.5)
                copy_out(("k", L), m, kr[:].rearrange("p e t -> p (e t)"), ACT.Relu)
                act.wait_ge(*drained(("k", L), m))
                act.activation(kr[:], kr[:], ACT.Square).then_inc(f_sq[L].sem, 1)

            def ssm_raw(u, m):
                use = ("in", u)
                act.wait_ge(*filled(use, m))
                act.wait_ge(*halo3.at(m, 1))
                act.activation(raw3[:, 2 * u:2 * u + 2, KW - 1:], psum(use)[:].rearrange("p (e t) -> p e t", e=2), ACT.Copy)
                for e in range(2):
                    k = 2 * u + e
                    ins = act.activation(y3[:, u, e, :], psum(use)[:, e * BT:(e + 1) * BT], ACT.Identity,
                                         scale=conv3_w[:, k, KW - 1:KW], bias=conv3_b[:, k:k + 1])
                ins.then_inc(free_sem(use), 1)

            def ssm_gate(u, m):
                copy_out(("in", 2 + u), m, sg[:, 2 * u:2 * u + 2, :].rearrange("p e t -> p (e t)"), ACT.Silu)

            def ssm_silu(u, m):
                act.wait_ge(*conv3.at(m, 6 * u + 6))
                act.activation(uT[:, 2 * u:2 * u + 2, :], y3[:, u], ACT.Silu).then_inc(silu3.sem, 1)

            def ssm_bu(m):
                act.wait_ge(*filled("bu", m))
                act.activation(bu[:], psum("bu")[:, 0:BT], ACT.Copy, scale=INPUT_FACTOR).then_inc(free_sem("bu"), 1)

            def step(n, q):
                attention, later, last = parts(n)
                m, l = n - 1, n - 2
                qm, ql = (q - 1) % BPS, (q - 2) % BPS
                if attention:
                    x_out(n)
                if last:
                    ssm_bu(l)
                if attention:
                    raw_out(0, n, q)
                    gate_exps(n, q)
                    raw_out(1, n, q)
                if later:
                    o_out(NC - 2, m)
                if attention:
                    silu_out(0, n)
                    raw_out(2, n, q)
                    raw_out(3, n, q)
                if later:
                    keep_halo(halo3, raw3, qm, m, conv3.at(m, 0))
                if attention:
                    copy_out(("kt", 0), n, kD[:, 0].rearrange("p c s -> p (c s)"))
                    silu_out(1, n)
                    copy_out(("kt", 1), n, kD[:, 1].rearrange("p c s -> p (c s)"))
                    silu_out(2, n)
                if later:
                    o_out(NC - 1, m)
                if attention:
                    raw_out(4, n, q)
                    silu_out(3, n)
                if last:
                    ffn_in(4, l, ql)
                if attention:
                    raw_out(5, n, q)
                if later:
                    o_sqrt(m)
                if attention:
                    log_norms(n)
                    exp_spread(0, n)
                if last:
                    ffn_act(4, l)
                if attention:
                    exp_spread(1, n)
                    exp_spread(2, n)
                    exp_spread(3, n)
                    silu_out(4, n)
                    silu_out(5, n)
                    act.wait_ge(*k_normed.at(n, 2))
                    stack(0, kD, n)
                    exp_mask(0, n)
                    exp_mask(1, n)
                    exp_mask(2, n)
                    exp_mask(3, n)
                    act.wait_ge(*drained(("vt", 0), n))
                    act.wait_ge(*drained(("vt", 1), n))
                    stack(1, vD, n)
                if later:
                    ffn_in(2, m, qm)
                    ffn_act(2, m)
                if attention:
                    o_out(0, n)
                if later:
                    xf_out(3, m)
                    ssm_raw(0, m)
                    ssm_raw(1, m)
                    ssm_silu(0, m)
                    ssm_gate(0, m)
                    ssm_gate(1, m)
                    ssm_silu(1, m)
                if attention:
                    o_out(1, n)

            act.wait_ge(*w_ready.at(0, N_READY))
            blocks(act, step)

        @block.vector
        def _(dve):
            dve.wait_ge(w_loaded.sem, 16 * len(loads))
            for k in range(DK):
                dve.tensor_copy(w_qkv_hi[:, k, :], qkv_stage[k]).then_inc(w_split.sem, 1)
            for k in range(DK):
                dve.wait_ge(w_split.sem, k + 1)
                dve.tensor_tensor(w_qkv_lo[:, k, :], qkv_stage[k], w_qkv_hi[:, k, :], ALU.subtract).then_inc(w_ready.sem, 1)
            dve.tensor_scalar(w_o[:], w_o[:], M[:, 2, P:P + 1], None, ALU.mult).then_inc(w_ready.sem, 1)
            dve.tensor_copy(ident_b[:], ident[:]).then_inc(w_ready.sem, 1)
            dve.tensor_copy(causal[:], M[:, 1, P:P + CT]).then_inc(w_ready.sem, 1)
            dve.tensor_copy(head_rows[:], M[0:96, :, 0:P]).then_inc(w_ready.sem, 1)
            dve.tensor_copy(head_cols[:], M[0:96, 0, P:P + HQ]).then_inc(w_ready.sem, 1)
            dve.tensor_scalar(f_v[:], f_v[:], 0.5, None, ALU.mult).then_inc(w_ready.sem, 1)
            dve.wait_ge(s_exp_a.sem, 1)
            dve.tensor_scalar(neg_a[:], neg_a[:], -1.0, None, ALU.mult).then_inc(w_ready.sem, 1)

            def norm_stats(i, n, src):
                s, L = ln_dve[i], LNS[i]
                for j in range(NJ):
                    dve.bn_stats(ln_stats[:, L, j, :], src[:, j, :]).then_inc(s.sem, 1)
                dve.drain()
                for j in range(NJ):
                    dve.bn_aggr(ln_mv[:, L, j, :], ln_stats[:, L, j, :]).then_inc(s.sem, 1)
                dve.wait_ge(*s.at(n, 2 * NJ))
                dve.tensor_scalar(ln_ve[:, L, :], ln_mv[:, L, :, 1], EPS_LN, None, ALU.add).then_inc(s.sem, 1)

            def norm_apply(i, n, src, dst):
                s, L = ln_dve[i], LNS[i]
                dve.wait_ge(*ln_root[i].at(n, 1))
                for j in range(NJ):
                    dve.tensor_scalar(dst[:, j, :], src[:, j, :], ln_mv[:, L, j, 0:1], ln_rs[:, L, j:j + 1],
                                      ALU.subtract, ALU.mult).then_inc(s.sem, 1)

            def gate_args(n, q):
                dve.wait_ge(*filled("gate", n))
                dve.tensor_scalar(az[:], psum("gate")[:, 0:P], dt_bias[:, 0:1], None, ALU.add)
                dve.tensor_scalar(al[:, q % 2], psum("gate")[:, 0:P], -1.0, 40.0, ALU.mult, ALU.min)\
                   .then_inc(free_sem("gate"), 1)
                dve.wait_ge(*filled("bz", n))
                dve.tensor_copy(beta_z[:].rearrange("q (p c) -> q p c", p=NPAIR),
                                psum("bz")[:, 0:NC * NPAIR].rearrange("q (c p) -> q p c", c=NC)).then_inc(free_sem("bz"), 1)

            def gate_sums(n, q):
                dve.wait_ge(*gate_act.at(n, 4))
                dve.tensor_scalar(beta_e[:], beta_e[:], 1.0, None, ALU.add).then_inc(beta_done.sem, 1)
                dve.tensor_scalar(al[:, q % 2], al[:, q % 2], 1.0, None, ALU.add).then_inc(alpha_done.sem, 1)
                dve.wait_ge(*beta_done.at(n, 1))
                dve.reciprocal(beta[:], beta_e[:]).then_inc(beta_done.sem, 1)
                dve.wait_ge(*alpha_done.at(n, 1))
                dve.scalar_tensor_tensor(al[:, q % 2], al[:, q % 2], DH * EPS, al[:, q % 2], ALU.mult, ALU.mult).then_inc(alpha_done.sem, 1)

            def taps(s, base, n, acc, src, weights, tile, first):
                for i in range(KW - 1):
                    for e in range(2):
                        if i:
                            dve.wait_ge(*s.at(n, base + 2 * (i - 1) + e + 1))
                        dve.scalar_tensor_tensor(acc[:, e, :], src[:, first + e, i:i + BT], weights[:, tile + e, i:i + 1],
                                                 acc[:, e, :], ALU.mult, ALU.add).then_inc(s.sem, 1)

            def convolve(u, n):
                dve.wait_ge(*drained(("qkv", u), n))
                taps(conv, 6 * u, n, y[:, u % 4], raw[:, u % 2], w_conv, 2 * u, 0)

            def split(s, base, n, src, row, dst):
                r0, r1, r2 = [slice(32 * i, 32 * i + HQ) for i in range(3)]
                tokens = [(src[j * DH + row:j * DH + row + HQ, :], slice(j * P, (j + 1) * P)) for j in range(NJ)]
                for x, ts in tokens:
                    dve.tensor_copy(dst[r0, ts], x).then_inc(s.sem, 1)
                dve.wait_ge(*s.at(n, base + NJ))
                for x, ts in tokens:
                    dve.tensor_tensor(part[r1, ts], x, dst[r0, ts], ALU.subtract).then_inc(s.sem, 1)
                dve.wait_ge(*s.at(n, base + 2 * NJ))
                dve.tensor_copy(dst[r1, :], part[r1, :]).then_inc(s.sem, 1)
                dve.wait_ge(*s.at(n, base + 2 * NJ + 1))
                dve.tensor_tensor(part[r2, :], part[r1, :], dst[r1, :], ALU.subtract).then_inc(s.sem, 1)
                dve.wait_ge(*s.at(n, base + 2 * NJ + 2))
                dve.tensor_copy(dst[r2, :], part[r2, :]).then_inc(s.sem, 1)

            def log_decay(n):
                dve.wait_ge(*gate_act.at(n, 5))
                dve.scalar_tensor_tensor(az[:], az[:], 0.0, az_abs[:], ALU.max, ALU.add).then_inc(g_steps.sem, 1)
                dve.wait_ge(*g_steps.at(n, 1))
                dve.tensor_scalar(az[:], az[:], neg_a[:, 0:1], None, ALU.mult).then_inc(g_steps.sem, 1)
                dve.wait_ge(*g_steps.at(n, 2))
                dve.tensor_tensor_scan(gsum[:], chunk_start[:], az[:], 0.0, ALU.mult, ALU.add).then_inc(g_steps.sem, 1)
                dve.wait_ge(*g_steps.at(n, 3))
                split(g_steps, 3, n, gsum, GROW, g3)

            def k_sums(n):
                for p in range(NPAIR):
                    dve.wait_ge(*k_sq.at(n, p + 1))
                    dve.tensor_reduce(k_ss[:, p * NC:(p + 1) * NC], M[:, 2 * p:2 * p + 2, :].rearrange(
                        "s a (c d) -> s (a c) d", d=P), AX_X, ALU.add).then_inc(k_red.sem, 1)

            def k_norms(n):
                dve.wait_ge(*k_root.at(n, 1))
                dve.tensor_scalar(k_nrm[:], k_nr[:], EPS, None, ALU.add).then_inc(k_red.sem, 1)
                dve.wait_ge(*k_red.at(n, 3))
                dve.reciprocal(k_rn[:], k_nrm[:]).then_inc(k_red.sem, 1)

            def v_out(p, n):
                use = ("vt", p)
                dve.wait_ge(*filled(use, n))
                dve.wait_ge(*beta_done.at(n, 2))
                dve.tensor_tensor(vD[:, p], psum(use)[:].rearrange("s (c d) -> s c d", c=NC),
                                  beta[:, p * NC:(p + 1) * NC].unsqueeze(2).broadcast_to([P, NC, P]), ALU.mult)\
                   .then_inc(free_sem(use), 1)

            def decay_cols(n):
                dve.wait_ge(*filled("gcol", n))
                dve.wait_ge(*k_log.at(n, 1))
                src = psum("gcol")[:, 0:NC * NT].rearrange("q (c p i) -> q p i c", c=NC, p=NPAIR)
                lns = k_ln[:].rearrange("q (p c) -> q p c", p=NPAIR).unsqueeze(2).broadcast_to([P, NPAIR, REP, NC])
                dve.tensor_tensor(gcol[:].rearrange("q (p i) c -> q p i c", p=NPAIR), src, lns, ALU.add)\
                   .then_inc(free_sem("gcol"), 1)

            def decay_diff(g, n):
                use = ("mask", g)
                dve.wait_ge(*filled(use, n))
                dve.wait_ge(*drained("gcol", n))
                cols = gcol[:, 2 * g:2 * g + 2, :].rearrange("s e c -> s (e c)").unsqueeze(2).broadcast_to([P, 2 * NC, CT])
                dve.tensor_tensor(M[:, 2 * g:2 * g + 2, :].rearrange("s e (c t) -> s (e c) t", c=NC),
                                  psum(use)[:].rearrange("s (f t) -> s f t", t=CT), cols, ALU.subtract)\
                   .then_inc(free_sem(use), 1)

            def weigh(name, i, t, n):
                use = (name, t)
                dve.wait_ge(*filled(use, n))
                dve.tensor_tensor(Pb[:, i], psum(use)[:].rearrange("s (i t) -> s i t", i=NT),
                                  M[:, :, t * CT:(t + 1) * CT], ALU.mult).then_inc(free_sem(use), 1)

            def correct(name, dst, t, n):
                use = (name, t)
                dve.wait_ge(*filled(use, n))
                dve.scalar_tensor_tensor(dst[:], psum(use)[:].rearrange("s (i t) -> s i t", i=NT), -DAMP,
                                         qT[:, :, t * CT:(t + 1) * CT], ALU.mult, ALU.add).then_inc(free_sem(use), 1)

            def add_state(p, t, n, q):
                use = (f"Hs{p}", t)
                dve.wait_ge(*filled(use, n))
                dve.wait_ge(*h_decayed.at(n, t + 1))
                part_ = Hst[:, (t + 1) % 2, p * REP:(p + 1) * REP, :]
                if q == BPS - 1 and t == NC - 1:
                    dve.memset(part_, 0.0).then_inc(free_sem(use), 1)
                else:
                    dve.tensor_tensor(part_, psum(use)[:].rearrange("s (i e) -> s i e", i=REP), part_, ALU.add)\
                       .then_inc(free_sem(use), 1)

            def head_vars(n, q):
                dve.wait_ge(*filled("ms", n))
                dve.tensor_tensor(o_scale[:], psum("ms")[:, 0:P], al[:, q % 2], ALU.add).then_inc(free_sem("ms"), 1)

            def head_scales(n):
                dve.wait_ge(*o_root.at(n, 1))
                dve.reciprocal(o_scale[:], o_scale[:]).then_inc(o_var.sem, 1)
                dve.wait_ge(*o_var.at(n, 1))
                split(o_var, 1, n, o_scale, ALPHA, sc3)

            def scale_o(g, n):
                use = ("bc", g)
                dve.wait_ge(*filled(use, n))
                dve.tensor_tensor(oT[:, 2 * g:2 * g + 2, :], psum(use)[:].rearrange("s (e t) -> s e t", e=2),
                                  oT[:, 2 * g:2 * g + 2, :], ALU.mult).then_inc(free_sem(use), 1)

            def attention_residual(n, q):
                dve.wait_ge(*filled("wo", n))
                dve.wait_ge(*x_stored[q % 2].at(n, -8 * (q % 2)))
                dve.tensor_tensor(xres[:, q % 2], psum("wo")[:].rearrange("s (j d) -> s j d", j=NJ), xin[:, q % 2], ALU.add)\
                   .then_inc(free_sem("wo"), 1)

            def ffn_mix(L, m):
                dve.wait_ge(*f_shift[L].at(m, 3))
                for i in range(2):
                    for k in range(DK):
                        dve.scalar_tensor_tensor(mixed[:, i, k, :], diff[:, k, :], mu[:, i, k:k + 1], xfT[:, k, 0:BT],
                                                 ALU.mult, ALU.add).then_inc(f_mix[L].sem, 1)

            def ffn_out(L, m, q):
                use = ("v", L)
                dve.wait_ge(*filled(use, m))
                dve.scalar_tensor_tensor(diff[:].rearrange("p k t -> p (k t)"), r_t[:], 1.0, psum(use)[:], ALU.add,
                                         ALU.mult).then_inc(free_sem(use), 1)
                dve.wait_ge(*drained(use, m))
                dve.tensor_tensor(xres[:, q % 2], xres[:, q % 2], f_out, ALU.add).then_inc(f_res[L].sem, 1)

            def ssm_taps(u, m):
                dve.wait_ge(*drained(("in", u), m))
                taps(conv3, 6 * u, m, y3[:, u], raw3, conv3_w, 2 * u, 2 * u)

            def ssm_scan(m, q):
                dve.wait_ge(*drained("bu", m))
                dve.wait_ge(*scan3.at(m, 0))
                dve.tensor_tensor_scan(h3[:], decay[:, 0:1].broadcast_to([P, BT]), bu[:], h_last[:, 0:1],
                                       ALU.mult, ALU.add).then_inc(scan3.sem, 1)
                dve.wait_ge(*scan3.at(m, 1))
                if q == BPS - 1:
                    dve.memset(h_last[:], 0.0).then_inc(scan3.sem, 1)
                else:
                    dve.tensor_copy(h_last[:], h3[:, BT - 1:BT]).then_inc(scan3.sem, 1)

            def ssm_skip(v, m):
                use = ("y", v)
                dve.wait_ge(*filled(use, m))
                for e in range(2):
                    k = 2 * v + e
                    ins = dve.scalar_tensor_tensor(yT[:, k, :], uT[:, k, :], d_skip[:, k:k + 1],
                                                   psum(use)[:, e * BT:(e + 1) * BT], ALU.mult, ALU.add)
                ins.then_inc(free_sem(use), 1)

            def ssm_norm_stats(m):
                dve.wait_ge(*filled("out", m))
                dve.tensor_tensor(z3, psum("out")[:].rearrange("p (j d) -> p j d", j=NJ), xn[:], ALU.add)\
                   .then_inc(free_sem("out"), 1)
                dve.wait_ge(*drained("out", m))
                norm_stats(5, m, z3)

            def step(n, q):
                attention, later, last = parts(n)
                m, l = n - 1, n - 2
                qm, ql = (q - 1) % BPS, (q - 2) % BPS
                if attention:
                    dve.wait_ge(*x_loaded[q % 2].at(n, 16 - 8 * (q % 2)))
                    norm_stats(1, n, xin[:, q % 2])
                if later:
                    dve.wait_ge(*x2_scaled.at(m, NC - 2))
                    correct("A2", x2, NC - 2, m)
                if attention:
                    norm_apply(1, n, xin[:, q % 2], xn1)
                if later:
                    dve.wait_ge(*x1_scaled.at(m, NC - 1))
                    correct("A1", x1, NC - 1, m)
                    weigh("S3", 2, NC - 2, m)
                if attention:
                    gate_args(n, q)
                if last:
                    ssm_scan(l, ql)
                if later:
                    weigh("S2", 1, NC - 1, m)
                if attention:
                    convolve(0, n)
                if last:
                    ssm_skip(0, l)
                    ssm_skip(1, l)
                if later:
                    add_state(1, NC - 1, m, qm)
                if attention:
                    log_decay(n)
                if later:
                    dve.wait_ge(*x2_scaled.at(m, NC - 1))
                    correct("A2", x2, NC - 1, m)
                if attention:
                    convolve(1, n)
                if last:
                    ssm_norm_stats(l)
                if attention:
                    gate_sums(n, q)
                if later:
                    weigh("S3", 2, NC - 1, m)
                if last:
                    norm_apply(5, l, z3, z3)
                if attention:
                    convolve(2, n)
                    convolve(3, n)
                if last:
                    dve.wait_ge(*l3_res.at(l, 3))
                    norm_stats(4, l, xres[:, ql % 2])
                if later:
                    add_state(0, NC - 1, m, qm)
                if attention:
                    k_sums(n)
                if last:
                    norm_apply(4, l, xres[:, ql % 2], xn)
                if attention:
                    v_out(0, n)
                    convolve(4, n)
                    v_out(1, n)
                if later:
                    head_vars(m, qm)
                if last:
                    ffn_mix(4, l)
                if attention:
                    k_norms(n)
                if later:
                    head_scales(m)
                if attention:
                    decay_cols(n)
                if later:
                    scale_o(0, m)
                    scale_o(2, m)
                if attention:
                    convolve(5, n)
                    decay_diff(2, n)
                if later:
                    scale_o(1, m)
                    scale_o(3, m)
                if attention:
                    decay_diff(0, n)
                    decay_diff(1, n)
                if last:
                    ffn_out(4, l, ql)
                if attention:
                    decay_diff(3, n)
                    dve.wait_ge(*exp_m.at(n, 4))
                    weigh("S1", 0, 0, n)
                if later:
                    attention_residual(m, qm)
                    dve.wait_ge(*drained("wo", m))
                    norm_stats(2, m, xres[:, qm % 2])
                if attention:
                    correct("A1", x1, 0, n)
                    add_state(0, 0, n, q)
                if later:
                    norm_apply(2, m, xres[:, qm % 2], xn)
                if attention:
                    add_state(1, 0, n, q)
                    weigh("S2", 1, 0, n)
                    weigh("S1", 0, 1, n)
                    correct("A2", x2, 0, n)
                if later:
                    ffn_mix(2, m)
                if attention:
                    weigh("S3", 2, 0, n)
                    dve.wait_ge(*x1_scaled.at(n, 1))
                    correct("A1", x1, 1, n)
                    add_state(0, 1, n, q)
                    add_state(1, 1, n, q)
                    weigh("S2", 1, 1, n)
                if later:
                    ffn_out(2, m, qm)
                if attention:
                    weigh("S1", 0, 2, n)
                if later:
                    dve.wait_ge(*f_res[2].at(m, 1))
                    norm_stats(3, m, xres[:, qm % 2])
                if attention:
                    dve.wait_ge(*x2_scaled.at(n, 1))
                    correct("A2", x2, 1, n)
                if later:
                    norm_apply(3, m, xres[:, qm % 2], xn)
                if attention:
                    dve.wait_ge(*x1_scaled.at(n, 2))
                    correct("A1", x1, 2, n)
                    weigh("S3", 2, 1, n)
                if later:
                    ssm_taps(0, m)
                if attention:
                    weigh("S2", 1, 2, n)
                    add_state(1, 2, n, q)
                    add_state(0, 2, n, q)
                if later:
                    ssm_taps(1, m)
                if attention:
                    weigh("S1", 0, 3, n)

            dve.wait_ge(*w_ready.at(0, N_READY))
            blocks(dve, step)

        @block.gpsimd
        def _(pool):
            for tile in (kT, vT, Hst, part, g3, sc3, raw3, last_col, h_last, no_halo):
                pool.memset(tile[:], 0.0)
            pool.memset(decay[:], DECAY)
            pool.memset(half_neg[:], -0.5)
            pool.memset(half_pos[:], 0.5).then_inc(w_ready.sem, 1)
            pool.wait_ge(w_loaded.sem, 16 * len(loads))
            pool.wait_ge(*w_ready.at(0, N_READY))

            def rstd(i, n):
                L = LNS[i]
                pool.wait_ge(*ln_dve[i].at(n, 2 * NJ + 1))
                pool.tensor_tensor(ln_rs[:, L, :], ln_ve[:, L, :], half_neg[:, 0:NJ], ALU.pow).then_inc(ln_root[i].sem, 1)

            def x_rest(n):
                pool.wait_ge(*x_split.at(n, 1))
                pool.wait_ge(*drained("xt1", n))
                pool.tensor_tensor(xT1_lo[:], xT1[:], xT1_hi[:], ALU.subtract).then_inc(x_split.sem, 1)

            def k_squares(n):
                pool.wait_ge(*drained(("S3", NC - 1), n - 1))
                for p in range(NPAIR):
                    pool.wait_ge(*drained(("kt", p), n))
                    pool.tensor_tensor(M[:, 2 * p:2 * p + 2, :].rearrange("s a t -> s (a t)"),
                                       kD[:, p].rearrange("s c d -> s (c d)"), kD[:, p].rearrange("s c d -> s (c d)"),
                                       ALU.mult).then_inc(k_sq.sem, 1)

            def k_roots(n):
                pool.wait_ge(*k_red.at(n, 2))
                pool.tensor_tensor(k_nr[:], k_ss[:], half_pos[:], ALU.pow).then_inc(k_root.sem, 1)

            def k_normalize(n):
                pool.wait_ge(*k_red.at(n, 4))
                for p in range(NPAIR):
                    rn = k_rn[:, p * NC:(p + 1) * NC].unsqueeze(2).broadcast_to([P, NC, P])
                    pool.tensor_tensor(kD[:, p], kD[:, p], rn, ALU.mult).then_inc(k_normed.sem, 1)

            def last_weights(n):
                pool.wait_ge(*exp_m.at(n, 4))
                last = M[:].rearrange("s (p i) (c t) -> s p i c t", p=NPAIR, c=NC)[:, :, :, :, CT - 1]
                nrm = k_nrm[:].rearrange("s (p c) -> s p c", p=NPAIR).unsqueeze(2).broadcast_to([P, NPAIR, REP, NC])
                pool.tensor_tensor(wlast[:].rearrange("s (p i) c -> s p i c", p=NPAIR), last, nrm, ALU.mult)\
                    .then_inc(w_last.sem, 1)

            def scale_rows(dst, src, t):
                return pool.tensor_tensor(dst[:], src, expG[:, :, t * CT:(t + 1) * CT], ALU.mult)

            def scale_q(t, n):
                if t >= 1:
                    pool.wait_ge(*filled(("A1", t - 1), n))
                scale_rows(qE, qT[:, :, t * CT:(t + 1) * CT], t).then_inc(q_scaled.sem, 1)

            def weigh_kv(t, n):
                if t >= 1:
                    pool.wait_ge(*filled(("Hs1", t - 1), n))
                src = kv[:, :, t].rearrange("s p m d -> s p (m d)").unsqueeze(2).broadcast_to([P, NPAIR, REP, 2 * DH])
                wts = wlast[:, :, t].rearrange("s (p i) -> s p i", p=NPAIR).unsqueeze(3).broadcast_to([P, NPAIR, REP, 2 * DH])
                pool.tensor_tensor(R[:], src, wts, ALU.mult).then_inc(r_scaled.sem, 1)

            def decay_state(t, n):
                t0, n0 = (t - 1, n) if t else (NC - 1, n - 1)
                pool.wait_ge(*drained(("Hs0", t0), n0))
                pool.wait_ge(*drained(("Hs1", t0), n0))
                pool.wait_ge(*filled(("O", t0), n0))
                dec = expG[:, :, (t + 1) * CT - 1:(t + 1) * CT].broadcast_to([P, NT, 2 * DH])
                pool.tensor_tensor(Hst[:, (t + 1) % 2], Hst[:, t % 2], dec, ALU.mult).then_inc(h_decayed.sem, 1)

            def ffn_diff(L, m):
                s = f_shift[L]
                pool.wait_ge(*s.at(m, 1))
                pool.wait_ge(*drained(("xt", L), m))
                pool.tensor_tensor(diff[:], xfT[:, :, 1:], xfT[:, :, 0:BT], ALU.subtract).then_inc(s.sem, 1)

            def ssm_gated(v, m):
                pool.wait_ge(*drained(("y", v), m))
                pool.tensor_tensor(yT[:, 2 * v:2 * v + 2, :], yT[:, 2 * v:2 * v + 2, :], sg[:, 2 * v:2 * v + 2, :],
                                   ALU.mult).then_inc(gated3.sem, 1)

            def ssm_affine(m, q):
                pool.wait_ge(*ln_dve[5].at(m, 3 * NJ + 1))
                g_ = gam[:].unsqueeze(1).broadcast_to([P, NJ, D])
                b_ = bet3[:].unsqueeze(1).broadcast_to([P, NJ, D])
                pool.tensor_tensor(z3, z3, g_, ALU.mult).then_inc(l3_res.sem, 1)
                pool.wait_ge(*l3_res.at(m, 1))
                pool.tensor_tensor(z3, z3, b_, ALU.add).then_inc(l3_res.sem, 1)
                pool.wait_ge(*l3_res.at(m, 2))
                pool.tensor_tensor(xres[:, q % 2], xres[:, q % 2], z3, ALU.add).then_inc(l3_res.sem, 1)

            def x1_rows(t, n):
                pool.wait_ge(*drained(("A1", t), n))
                if t >= 1:
                    pool.wait_ge(*filled(("A2", t - 1), n))
                scale_rows(x1E, x1[:], t).then_inc(x1_scaled.sem, 1)

            def x2_rows(t, n):
                pool.wait_ge(*drained(("A2", t), n))
                if t >= 1:
                    pool.wait_ge(*filled(("O", t - 1), n))
                scale_rows(x2E, x2[:], t).then_inc(x2_scaled.sem, 1)

            def step(n, q):
                attention, later, last = parts(n)
                m, l = n - 1, n - 2
                ql = (q - 2) % BPS
                if attention:
                    rstd(1, n)
                if later:
                    x2_rows(NC - 2, m)
                if attention:
                    x_rest(n)
                if later:
                    decay_state(3, m)
                    x1_rows(NC - 1, m)
                if last:
                    ssm_gated(0, l)
                    ssm_gated(1, l)
                if later:
                    x2_rows(NC - 1, m)
                if last:
                    rstd(5, l)
                    ssm_affine(l, ql)
                if attention:
                    k_squares(n)
                if last:
                    rstd(4, l)
                if attention:
                    k_roots(n)
                if last:
                    ffn_diff(4, l)
                if attention:
                    k_normalize(n)
                    last_weights(n)
                    scale_q(0, n)
                    pool.wait_ge(*kv_done.at(n, 2))
                    pool.wait_ge(*w_last.at(n, 1))
                    weigh_kv(0, n)
                    decay_state(0, n)
                if later:
                    rstd(2, m)
                if attention:
                    scale_q(1, n)
                    x1_rows(0, n)
                if later:
                    ffn_diff(2, m)
                if attention:
                    weigh_kv(1, n)
                    scale_q(2, n)
                    x2_rows(0, n)
                    x1_rows(1, n)
                    decay_state(1, n)
                    weigh_kv(2, n)
                if later:
                    rstd(3, m)
                if attention:
                    x2_rows(1, n)
                    scale_q(3, n)
                    x1_rows(2, n)
                    weigh_kv(3, n)
                    decay_state(2, n)

            blocks(pool, step)


def _tiles(w, n):
    import numpy as np
    return np.ascontiguousarray(np.asarray(w).reshape(n, P, -1).transpose(1, 0, 2))


def _laid_out(i):
    import numpy as np
    A = {k: np.asarray(v) for k, v in i.items()}
    g = lambda s: A["L0_attn_a_" + s]
    b3 = lambda s: A["L0_attn_b_" + s]
    f = lambda s: A["L0_ffn_" + s]
    heads = [(2 * p + h) * REP + i for p in range(NPAIR) for i in range(REP) for h in range(2)]
    wq = g("Wq").reshape(D, HQ, DH)[:, heads].reshape(D, HQ * DH)
    w_qkv = np.concatenate([g("Wk"), g("Wv"), wq], 1)
    conv = g("Wconv")
    cq, ck, cv = conv[:HQ * DH], conv[HQ * DH:HQ * DH + HKV * DH], conv[HQ * DH + HKV * DH:]
    cq = cq.reshape(HQ, DH, KW)[heads].reshape(HQ * DH, KW)
    gate = np.zeros((D, DH), np.float32)
    gate[:, GROW:GROW + HQ] = g("Wa")
    gate[:, ALPHA:ALPHA + HQ] = g("Walpha")
    a_rows = np.zeros((2, P, 1), np.float32)
    for j in range(NJ):
        a_rows[0, j * DH + GROW:j * DH + GROW + HQ, 0] = g("dt_bias")
        a_rows[1, j * DH + GROW:j * DH + GROW + HQ, 0] = g("A_log")
    rows = np.zeros((96, NT, P), np.float32)
    mean = np.zeros((P, NT, DH), np.float32)
    for t in range(NT):
        for h in range(2):
            head = heads[2 * t + h]
            rows[[head, 32 + head, 64 + head], t, h * DH:(h + 1) * DH] = 1.0
            mean[h * DH:(h + 1) * DH, t, ALPHA + head] = 1.0 / DH
    cols = np.zeros((96, HQ), np.float32)
    for r in range(3):
        cols[32 * r:32 * r + HQ] = np.eye(HQ)[:, heads[0::2] + heads[1::2]]
    s, t = np.arange(P)[:, None] % CT, np.arange(CT)[None, :]
    start = np.ones((P, P), np.float32)
    start[:, ::CT] = 0.0
    return {
        "x": g("x"),
        "w_qkv0": w_qkv[0:P], "w_qkv1": w_qkv[P:],
        "w_gate": _tiles(gate, DK), "w_beta": _tiles(g("Wb")[:, [2 * p + h for h in range(2) for p in range(NPAIR)]], DK),
        "w_o": _tiles(g("Wo").reshape(HQ, DH, D)[heads].reshape(HQ * DH, D), NT),
        "w_conv": _tiles(np.concatenate([ck, cv, cq], 0), QKV),
        "f_r": _tiles(f("W_r").T, DK), "f_k": _tiles(f("W_k").T, DK), "f_v": _tiles(f("W_v").T, DK),
        "mu": np.ascontiguousarray(np.stack([f("mu_r").reshape(DK, P).T, f("mu_k").reshape(DK, P).T], 1)),
        "w_in": _tiles(b3("W_in").T, DK), "w_b": _tiles(b3("W_B").T, NE),
        "w_c": np.ascontiguousarray(np.concatenate([b3("W_C").T] * 2, 0).reshape(P, NE, P)), "w_out": _tiles(b3("W_out").T, NE),
        "conv3_w": _tiles(b3("conv_w").reshape(INNER, KW), NE),
        "conv3_b": np.ascontiguousarray(b3("conv_b").reshape(NE, P).T),
        "d_skip": np.ascontiguousarray(b3("D_param").reshape(NE, P).T),
        "gam": np.ascontiguousarray(np.broadcast_to(b3("ln_gamma"), (P, D))),
        "bet3": np.ascontiguousarray(np.broadcast_to(b3("ln_beta"), (P, D))),
        "norm_w": np.ascontiguousarray(np.concatenate([g("norm_w")] * 2).reshape(P, 1)),
        "dt_bias": a_rows[0], "a_log": a_rows[1],
        "ident": np.eye(P, dtype=np.float32),
        "causal": np.where(t >= s, 0.0, -1e30).astype(np.float32),
        "chunk_start": start, "head_rows": rows, "head_cols": cols, "head_mean": mean,
    }


def kernel(**inputs):
    import numpy as np
    import concourse.bacc as bacc
    from concourse.bass_utils import run_bass_kernel_spmd

    nc = bacc.Bacc("TRN2", target_bir_lowering=False, num_devices=1)
    arrays, args = {}, {}
    for name, v in _laid_out(inputs).items():
        arrays[f"in_{name}"] = v
        args[name] = nc.dram_tensor(f"in_{name}", v.shape, mybir.dt.from_np(v.dtype), kind="ExternalInput").ap()
    out = nc.dram_tensor("out_x", (BATCH, T, D), F32, kind="ExternalOutput").ap()
    hybrid_block_kernel(nc, args, out)
    r = run_bass_kernel_spmd(nc, [arrays], core_ids=[0])
    return r.results[0]["out_x"]
```
